# Optimizing a Trainium2 kernel written in Bass

```python
import numpy as np
import jax
import jax.numpy as jnp

def _softmax(x, axis=-1):
    return jax.nn.softmax(x, axis=axis)

def _gelu(x):
    return jax.nn.gelu(x, approximate=True)

def _silu(x):
    return jax.nn.silu(x)

def _sigmoid(x):
    return jax.nn.sigmoid(x)

def _layernorm(x, axis=-1, eps=1e-05):
    m = jnp.mean(x, axis=axis, keepdims=True)
    v = jnp.var(x, axis=axis, keepdims=True)
    return (x - m) / jnp.sqrt(v + eps)

def _scatter_add(tgt, idx, src, axis=0):
    return tgt.at[idx].add(src)

def _segment_sum(src, seg, n):
    return jax.ops.segment_sum(src, seg, n)
kernel_name = 'mk_lm_tower_d2_tok_ids768_r4_d5c365'

def setup_inputs(seed: int=0):
    np.random.seed(seed)
    _w = jnp.asarray

    def _rec_inputs():
        import jax
        import jax.numpy as jnp
        _rk = jax.random.key(seed)
        x = jax.random.randint(jax.random.fold_in(_rk, 1), (32, 256), 0, 12564, jnp.int32)
        return x
    x = _rec_inputs()

    def _L0_tok_setup():
        import jax, jax.numpy as jnp
        import numpy as np
        D_MODEL = 192
        N_HEADS = 8
        D_TRACE = 64
        TRACE_LR = 0.1
        TRACE_DECAY = 0.99
        LN_EPS = 1e-05
        B, S, VOCAB = (8, 1024, 50257)

        def _ln(x, w, b):
            m = x.mean(-1, keepdims=True)
            v = ((x - m) ** 2).mean(-1, keepdims=True)
            return (x - m) / jnp.sqrt(v + LN_EPS) * w + b
        key = jax.random.key(seed)
        ks = jax.random.split(key, 6)
        return {'input_ids': jax.random.randint(ks[0], (B, S), 0, VOCAB), 'wte': jax.random.normal(ks[1], (VOCAB, D_MODEL), jnp.float32) * 0.02, 'W_proj': jax.random.normal(ks[2], (N_HEADS * D_TRACE, D_MODEL), jnp.float32) / np.float32(np.sqrt(D_MODEL)), 'ln_w': jnp.ones((D_MODEL,), jnp.float32), 'ln_b': jnp.zeros((D_MODEL,), jnp.float32), 'W_val': jax.random.normal(ks[3], (N_HEADS * D_TRACE, D_MODEL), jnp.float32) / np.float32(np.sqrt(D_MODEL)), 'W_out': jax.random.normal(ks[4], (D_MODEL, N_HEADS * D_TRACE), jnp.float32) / np.float32(np.sqrt(N_HEADS * D_TRACE)), 'trace0': jax.random.normal(ks[5], (N_HEADS, D_TRACE, D_TRACE), jnp.float32) * 0.01}
    _L0_tok_all = _L0_tok_setup()
    _L0_tok_in = {k: v for k, v in _L0_tok_all.items() if k in ('wte', 'W_proj', 'ln_w', 'ln_b', 'W_val', 'W_out', 'trace0')}
    del _L0_tok_all

    def _L0_attn_setup():
        import jax, jax.numpy as jnp
        import numpy as np
        HIDDEN = 192
        KV_DIM = HIDDEN // 3
        BATCH, SEQ = (2, 2048)
        THETA = 10000.0

        def rope_table(seq_len, dim):
            pos = jnp.arange(seq_len, dtype=jnp.float32)
            freqs = THETA ** (-jnp.arange(0, dim, 2, dtype=jnp.float32) / dim)
            ang = pos[:, None] * freqs[None, :]
            return jnp.concatenate([jnp.sin(ang), jnp.cos(ang)], axis=-1)[None]
        key = jax.random.key(seed)
        kx, kq, kk, kv, ko = jax.random.split(key, 5)
        s = 1.0 / np.sqrt(HIDDEN)
        return {'x': jax.random.normal(kx, (BATCH, SEQ, HIDDEN), dtype=jnp.float32), 'Wq': jax.random.uniform(kq, (HIDDEN, HIDDEN), jnp.float32, -s, s), 'Wk': jax.random.uniform(kk, (KV_DIM, HIDDEN), jnp.float32, -s, s), 'Wv': jax.random.uniform(kv, (KV_DIM, HIDDEN), jnp.float32, -s, s), 'Wo': jax.random.uniform(ko, (HIDDEN, KV_DIM), jnp.float32, -s, s)}
    _L0_attn_all = _L0_attn_setup()
    _L0_attn_in = {k: v for k, v in _L0_attn_all.items() if k in ('Wq', 'Wk', 'Wv', 'Wo')}
    del _L0_attn_all

    def _L0_ffn_setup():
        import math
        import jax, jax.numpy as jnp
        import numpy as np
        EMBED_CHOICES = [96, 144, 192]
        RATIO_CHOICES = [2, 3, 4]
        E_MAX = 192
        H_MAX = 768

        def new_gelu(x):
            c = math.sqrt(2.0 / math.pi)
            return 0.5 * x * (1.0 + jnp.tanh(c * (x + 0.044715 * x * x * x)))

        def _mixed_coeffs(alpha_e, alpha_r):
            h_idx = jnp.arange(H_MAX)
            d_idx = jnp.arange(E_MAX)
            C0 = jnp.zeros((H_MAX, E_MAX), jnp.float32)
            c0b = jnp.zeros((H_MAX,), jnp.float32)
            C1 = jnp.zeros((E_MAX, H_MAX), jnp.float32)
            c1b = jnp.zeros((E_MAX,), jnp.float32)
            for i, e in enumerate(EMBED_CHOICES):
                m_in = (d_idx < e).astype(jnp.float32)
                for j, r in enumerate(RATIO_CHOICES):
                    a = alpha_e[i] * alpha_r[j]
                    m_out = (h_idx < r * e).astype(jnp.float32)
                    C0 = C0 + a * (m_out[:, None] * m_in[None, :])
                    c0b = c0b + a * m_out
                    C1 = C1 + a * (m_in[:, None] * m_out[None, :])
                    c1b = c1b + a * m_in
            return (C0, c0b, C1, c1b)
        key = jax.random.key(seed)
        ks = jax.random.split(key, 6)
        x = jax.random.normal(ks[0], (8, 512, E_MAX), jnp.float32)
        w_fc = jax.random.normal(ks[1], (H_MAX, E_MAX), jnp.float32) * 0.02
        b_fc = jnp.zeros((H_MAX,), jnp.float32)
        w_proj = jax.random.normal(ks[2], (E_MAX, H_MAX), jnp.float32) * 0.02
        b_proj = jnp.zeros((E_MAX,), jnp.float32)
        alpha_e = jax.nn.softmax(jax.random.normal(ks[3], (3,), jnp.float32))
        alpha_r = jax.nn.softmax(jax.random.normal(ks[4], (3,), jnp.float32))
        return {'x': x, 'w_fc': w_fc, 'b_fc': b_fc, 'w_proj': w_proj, 'b_proj': b_proj, 'alpha_e': alpha_e, 'alpha_r': alpha_r}
    _L0_ffn_all = _L0_ffn_setup()
    _L0_ffn_in = {k: v for k, v in _L0_ffn_all.items() if k in ('w_fc', 'b_fc', 'w_proj', 'b_proj', 'alpha_e', 'alpha_r')}
    del _L0_ffn_all

    def _L1_attn_setup():
        import jax, jax.numpy as jnp
        import numpy as np
        from jax import lax
        ENC_IN = 64
        NODE_DIM = 16
        D_MODEL = 192
        D_STATE = 16
        D_CONV = 4
        EXPAND = 2
        D_INNER = EXPAND * D_MODEL
        DT_RANK = (D_MODEL + 15) // 16
        K_SP = min(7, D_MODEL // 4 + 1)
        B, L = (8, 128)
        EPS = 1e-05

        def _layernorm(x, w, b):
            mu = jnp.mean(x, axis=-1, keepdims=True)
            var = jnp.var(x, axis=-1, keepdims=True)
            return (x - mu) * lax.rsqrt(var + EPS) * w + b

        def _mamba(x, m_in_w, m_conv_w, m_conv_b, m_xproj_w, m_dt_w, m_dt_b, m_A_log, m_D, m_out_w):
            xz = x @ m_in_w
            xm, z = jnp.split(xz, 2, axis=-1)
            xc = jnp.swapaxes(xm, 1, 2)
            xc = lax.conv_general_dilated(xc, m_conv_w[:, None, :], window_strides=(1,), padding=[(D_CONV - 1, 0)], feature_group_count=D_INNER, dimension_numbers=('NCH', 'OIH', 'NCH'))
            xc = xc + m_conv_b[None, :, None]
            xm = jax.nn.silu(jnp.swapaxes(xc, 1, 2))
            x_dbl = xm @ m_xproj_w
            dt, Bm, Cm = jnp.split(x_dbl, [DT_RANK, DT_RANK + D_STATE], axis=-1)
            dt = jax.nn.softplus(dt @ m_dt_w + m_dt_b)
            A = -jnp.exp(m_A_log)
            dA = jnp.exp(dt[..., None] * A)
            dBx = dt[..., None] * Bm[:, :, None, :] * xm[..., None]
            dA_t = jnp.moveaxis(dA, 1, 0)
            dBx_t = jnp.moveaxis(dBx, 1, 0)
            h0 = jnp.zeros((xm.shape[0], D_INNER, D_STATE), xm.dtype)

            def step(h, c):
                dAt, dBxt = c
                h = dAt * h + dBxt
                return (h, h)
            _, hs = lax.scan(step, h0, (dA_t, dBx_t))
            y = jnp.einsum('lbdn,bln->bld', hs, Cm)
            y = y + m_D * xm
            y = y * jax.nn.silu(z)
            return y @ m_out_w

        def _reference_tuple_inner(x, nodevec1, nodevec2, norm1_w, norm1_b, norm2_w, norm2_b, gcn_w, gcn_b, conv_w, conv_b, gate_gcn_w, gate_gcn_b, gate_mamba_w, gate_mamba_b, out_w, out_b, m_in_w, m_conv_w, m_conv_b, m_xproj_w, m_dt_w, m_dt_b, m_A_log, m_D, m_out_w):
            residual = x
            adj = jax.nn.sigmoid(nodevec1 @ nodevec2)
            adj = adj * (1.0 - jnp.eye(ENC_IN, dtype=adj.dtype))
            xn = _layernorm(x, norm1_w, norm1_b)
            x_gcn = xn @ gcn_w + gcn_b
            pad = (K_SP - 1) // 2
            xc = lax.conv_general_dilated(jnp.swapaxes(xn, 1, 2), conv_w, window_strides=(1,), padding=[(pad, K_SP - 1 - pad)], dimension_numbers=('NCH', 'OIH', 'NCH'))
            xc = xc + conv_b[None, :, None]
            x_gcn = x_gcn + jnp.swapaxes(xc, 1, 2)
            x_mamba = _mamba(xn, m_in_w, m_conv_w, m_conv_b, m_xproj_w, m_dt_w, m_dt_b, m_A_log, m_D, m_out_w)
            gate = jax.nn.sigmoid(x_gcn @ gate_gcn_w + gate_gcn_b + (x_mamba @ gate_mamba_w + gate_mamba_b))
            fused = gate * x_gcn + (1.0 - gate) * x_mamba
            out = fused @ out_w + out_b
            out = _layernorm(out + residual, norm2_w, norm2_b)
            return (out, adj)
        key = jax.random.key(seed)
        ks = jax.random.split(key, 24)
        s = 0.02
        inp = {'x': jax.random.normal(ks[0], (B, L, D_MODEL), jnp.float32), 'nodevec1': jax.random.normal(ks[1], (ENC_IN, NODE_DIM), jnp.float32) * 0.1, 'nodevec2': jax.random.normal(ks[2], (NODE_DIM, ENC_IN), jnp.float32) * 0.1, 'norm1_w': jnp.ones((D_MODEL,), jnp.float32), 'norm1_b': jnp.zeros((D_MODEL,), jnp.float32), 'norm2_w': jnp.ones((D_MODEL,), jnp.float32), 'norm2_b': jnp.zeros((D_MODEL,), jnp.float32), 'gcn_w': jax.random.normal(ks[3], (D_MODEL, D_MODEL), jnp.float32) * s, 'gcn_b': jnp.zeros((D_MODEL,), jnp.float32), 'conv_w': jax.random.normal(ks[4], (D_MODEL, D_MODEL, K_SP), jnp.float32) * s, 'conv_b': jnp.zeros((D_MODEL,), jnp.float32), 'gate_gcn_w': jax.random.normal(ks[5], (D_MODEL, D_MODEL), jnp.float32) * s, 'gate_gcn_b': jnp.zeros((D_MODEL,), jnp.float32), 'gate_mamba_w': jax.random.normal(ks[6], (D_MODEL, D_MODEL), jnp.float32) * s, 'gate_mamba_b': jnp.zeros((D_MODEL,), jnp.float32), 'out_w': jax.random.normal(ks[7], (D_MODEL, D_MODEL), jnp.float32) * s, 'out_b': jnp.zeros((D_MODEL,), jnp.float32), 'm_in_w': jax.random.normal(ks[8], (D_MODEL, 2 * D_INNER), jnp.float32) * s, 'm_conv_w': jax.random.normal(ks[9], (D_INNER, D_CONV), jnp.float32) * s, 'm_conv_b': jnp.zeros((D_INNER,), jnp.float32), 'm_xproj_w': jax.random.normal(ks[10], (D_INNER, DT_RANK + 2 * D_STATE), jnp.float32) * s, 'm_dt_w': jax.random.normal(ks[11], (DT_RANK, D_INNER), jnp.float32) * s, 'm_dt_b': jnp.full((D_INNER,), 0.5, jnp.float32), 'm_A_log': jnp.log(jnp.tile(jnp.arange(1, D_STATE + 1, dtype=jnp.float32), (D_INNER, 1))), 'm_D': jnp.ones((D_INNER,), jnp.float32), 'm_out_w': jax.random.normal(ks[12], (D_INNER, D_MODEL), jnp.float32) * s}
        return inp
    _L1_attn_all = _L1_attn_setup()
    _L1_attn_in = {k: v for k, v in _L1_attn_all.items() if k in ('nodevec1', 'nodevec2', 'norm1_w', 'norm1_b', 'norm2_w', 'norm2_b', 'gcn_w', 'gcn_b', 'conv_w', 'conv_b', 'gate_gcn_w', 'gate_gcn_b', 'gate_mamba_w', 'gate_mamba_b', 'out_w', 'out_b', 'm_in_w', 'm_conv_w', 'm_conv_b', 'm_xproj_w', 'm_dt_w', 'm_dt_b', 'm_A_log', 'm_D', 'm_out_w')}
    del _L1_attn_all

    def _L1_ffn_setup():
        import jax, jax.numpy as jnp
        import numpy as np
        D_MODEL, D_FF, N_EXPERTS, TOP_K = (192, 768, 8, 2)
        B, S = (2, 256)
        LN_EPS = 1e-05

        def _layernorm(x, gamma, beta):
            mu = jnp.mean(x, axis=-1, keepdims=True)
            var = jnp.mean(jnp.square(x - mu), axis=-1, keepdims=True)
            return (x - mu) * jax.lax.rsqrt(var + LN_EPS) * gamma + beta
        key = jax.random.key(seed)
        k1, k2, k3, k4 = jax.random.split(key, 4)
        return {'hidden_states': jax.random.normal(k1, (B, S, D_MODEL), dtype=jnp.float32), 'ln_gamma': jnp.ones((D_MODEL,), dtype=jnp.float32), 'ln_beta': jnp.zeros((D_MODEL,), dtype=jnp.float32), 'router_w': jax.random.normal(k2, (D_MODEL, N_EXPERTS), dtype=jnp.float32) * 0.02, 'w1': jax.random.normal(k3, (N_EXPERTS, D_MODEL, D_FF), dtype=jnp.float32) * 0.02, 'w2': jax.random.normal(k4, (N_EXPERTS, D_FF, D_MODEL), dtype=jnp.float32) * 0.02}
    _L1_ffn_all = _L1_ffn_setup()
    _L1_ffn_in = {k: v for k, v in _L1_ffn_all.items() if k in ('ln_gamma', 'ln_beta', 'router_w', 'w1', 'w2')}
    del _L1_ffn_all
    return {'x': x, 'L0_tok_wte': _L0_tok_in['wte'], 'L0_tok_W_proj': _L0_tok_in['W_proj'], 'L0_tok_ln_w': _L0_tok_in['ln_w'], 'L0_tok_ln_b': _L0_tok_in['ln_b'], 'L0_tok_W_val': _L0_tok_in['W_val'], 'L0_tok_W_out': _L0_tok_in['W_out'], 'L0_tok_trace0': _L0_tok_in['trace0'], 'L0_attn_Wq': _L0_attn_in['Wq'], 'L0_attn_Wk': _L0_attn_in['Wk'], 'L0_attn_Wv': _L0_attn_in['Wv'], 'L0_attn_Wo': _L0_attn_in['Wo'], 'L0_ffn_w_fc': _L0_ffn_in['w_fc'], 'L0_ffn_b_fc': _L0_ffn_in['b_fc'], 'L0_ffn_w_proj': _L0_ffn_in['w_proj'], 'L0_ffn_b_proj': _L0_ffn_in['b_proj'], 'L0_ffn_alpha_e': _L0_ffn_in['alpha_e'], 'L0_ffn_alpha_r': _L0_ffn_in['alpha_r'], 'L1_attn_nodevec1': _L1_attn_in['nodevec1'], 'L1_attn_nodevec2': _L1_attn_in['nodevec2'], 'L1_attn_norm1_w': _L1_attn_in['norm1_w'], 'L1_attn_norm1_b': _L1_attn_in['norm1_b'], 'L1_attn_norm2_w': _L1_attn_in['norm2_w'], 'L1_attn_norm2_b': _L1_attn_in['norm2_b'], 'L1_attn_gcn_w': _L1_attn_in['gcn_w'], 'L1_attn_gcn_b': _L1_attn_in['gcn_b'], 'L1_attn_conv_w': _L1_attn_in['conv_w'], 'L1_attn_conv_b': _L1_attn_in['conv_b'], 'L1_attn_gate_gcn_w': _L1_attn_in['gate_gcn_w'], 'L1_attn_gate_gcn_b': _L1_attn_in['gate_gcn_b'], 'L1_attn_gate_mamba_w': _L1_attn_in['gate_mamba_w'], 'L1_attn_gate_mamba_b': _L1_attn_in['gate_mamba_b'], 'L1_attn_out_w': _L1_attn_in['out_w'], 'L1_attn_out_b': _L1_attn_in['out_b'], 'L1_attn_m_in_w': _L1_attn_in['m_in_w'], 'L1_attn_m_conv_w': _L1_attn_in['m_conv_w'], 'L1_attn_m_conv_b': _L1_attn_in['m_conv_b'], 'L1_attn_m_xproj_w': _L1_attn_in['m_xproj_w'], 'L1_attn_m_dt_w': _L1_attn_in['m_dt_w'], 'L1_attn_m_dt_b': _L1_attn_in['m_dt_b'], 'L1_attn_m_A_log': _L1_attn_in['m_A_log'], 'L1_attn_m_D': _L1_attn_in['m_D'], 'L1_attn_m_out_w': _L1_attn_in['m_out_w'], 'L1_ffn_ln_gamma': _L1_ffn_in['ln_gamma'], 'L1_ffn_ln_beta': _L1_ffn_in['ln_beta'], 'L1_ffn_router_w': _L1_ffn_in['router_w'], 'L1_ffn_w1': _L1_ffn_in['w1'], 'L1_ffn_w2': _L1_ffn_in['w2']}

def reference(x, L0_tok_wte, L0_tok_W_proj, L0_tok_ln_w, L0_tok_ln_b, L0_tok_W_val, L0_tok_W_out, L0_tok_trace0, L0_attn_Wq, L0_attn_Wk, L0_attn_Wv, L0_attn_Wo, L0_ffn_w_fc, L0_ffn_b_fc, L0_ffn_w_proj, L0_ffn_b_proj, L0_ffn_alpha_e, L0_ffn_alpha_r, L1_attn_nodevec1, L1_attn_nodevec2, L1_attn_norm1_w, L1_attn_norm1_b, L1_attn_norm2_w, L1_attn_norm2_b, L1_attn_gcn_w, L1_attn_gcn_b, L1_attn_conv_w, L1_attn_conv_b, L1_attn_gate_gcn_w, L1_attn_gate_gcn_b, L1_attn_gate_mamba_w, L1_attn_gate_mamba_b, L1_attn_out_w, L1_attn_out_b, L1_attn_m_in_w, L1_attn_m_conv_w, L1_attn_m_conv_b, L1_attn_m_xproj_w, L1_attn_m_dt_w, L1_attn_m_dt_b, L1_attn_m_A_log, L1_attn_m_D, L1_attn_m_out_w, L1_ffn_ln_gamma, L1_ffn_ln_beta, L1_ffn_router_w, L1_ffn_w1, L1_ffn_w2):
    import jax
    import jax.numpy as jnp

    def _L0_tok_ref(input_ids, wte, W_proj, ln_w, ln_b, W_val, W_out, trace0):
        import jax, jax.numpy as jnp
        import numpy as np
        D_MODEL = 192
        N_HEADS = 8
        D_TRACE = 64
        TRACE_LR = 0.1
        TRACE_DECAY = 0.99
        LN_EPS = 1e-05
        B, S, VOCAB = (8, 1024, 50257)

        def _ln(x, w, b):
            m = x.mean(-1, keepdims=True)
            v = ((x - m) ** 2).mean(-1, keepdims=True)
            return (x - m) / jnp.sqrt(v + LN_EPS) * w + b
        B_, S_ = input_ids.shape
        tok = wte[input_ids]
        Q = _ln(tok, ln_w, ln_b) @ W_proj.T
        V = tok @ W_val.T
        Q = Q.reshape(B_, S_, N_HEADS, D_TRACE).transpose(0, 2, 1, 3)
        V = V.reshape(B_, S_, N_HEADS, D_TRACE).transpose(0, 2, 1, 3)
        Q_store = Q[:, :, :-2, :]
        V_store = V[:, :, 2:, :]
        denom = jnp.float32(B_ * (S_ - 2))
        upd = jnp.einsum('bhip,bhiq->hpq', Q_store, V_store) / denom
        trace = TRACE_DECAY * trace0 + TRACE_LR * upd
        Q_addr = jnp.concatenate([jnp.zeros_like(Q[:, :, :1, :]), Q[:, :, :-1, :]], axis=2)
        V_ret = jnp.einsum('bhsp,hpq->bhsq', Q_addr, trace)
        V_flat = V_ret.transpose(0, 2, 1, 3).reshape(B_, S_, N_HEADS * D_TRACE)
        return V_flat @ W_out.T

    def _L0_attn_ref(x, Wq, Wk, Wv, Wo):
        import jax, jax.numpy as jnp
        import numpy as np
        HIDDEN = 192
        KV_DIM = HIDDEN // 3
        BATCH, SEQ = (2, 2048)
        THETA = 10000.0

        def rope_table(seq_len, dim):
            pos = jnp.arange(seq_len, dtype=jnp.float32)
            freqs = THETA ** (-jnp.arange(0, dim, 2, dtype=jnp.float32) / dim)
            ang = pos[:, None] * freqs[None, :]
            return jnp.concatenate([jnp.sin(ang), jnp.cos(ang)], axis=-1)[None]
        B, S, H = x.shape
        q = jnp.einsum('bsh,oh->bso', x, Wq)
        k = jnp.einsum('bsh,oh->bso', x, Wk)
        v = jnp.einsum('bsh,oh->bso', x, Wv)
        r = rope_table(S, H)
        attn_weights = jnp.matmul(r, jnp.swapaxes(r, -2, -1))
        attn_probs = jax.nn.softmax(attn_weights, axis=-1)
        attn_output = jnp.matmul(attn_probs, v)
        out = jnp.einsum('bsk,ok->bso', attn_output, Wo)
        return out

    def _L0_ffn_ref(x, w_fc, b_fc, w_proj, b_proj, alpha_e, alpha_r):
        import math
        import jax, jax.numpy as jnp
        import numpy as np
        EMBED_CHOICES = [96, 144, 192]
        RATIO_CHOICES = [2, 3, 4]
        E_MAX = 192
        H_MAX = 768

        def new_gelu(x):
            c = math.sqrt(2.0 / math.pi)
            return 0.5 * x * (1.0 + jnp.tanh(c * (x + 0.044715 * x * x * x)))

        def _mixed_coeffs(alpha_e, alpha_r):
            h_idx = jnp.arange(H_MAX)
            d_idx = jnp.arange(E_MAX)
            C0 = jnp.zeros((H_MAX, E_MAX), jnp.float32)
            c0b = jnp.zeros((H_MAX,), jnp.float32)
            C1 = jnp.zeros((E_MAX, H_MAX), jnp.float32)
            c1b = jnp.zeros((E_MAX,), jnp.float32)
            for i, e in enumerate(EMBED_CHOICES):
                m_in = (d_idx < e).astype(jnp.float32)
                for j, r in enumerate(RATIO_CHOICES):
                    a = alpha_e[i] * alpha_r[j]
                    m_out = (h_idx < r * e).astype(jnp.float32)
                    C0 = C0 + a * (m_out[:, None] * m_in[None, :])
                    c0b = c0b + a * m_out
                    C1 = C1 + a * (m_in[:, None] * m_out[None, :])
                    c1b = c1b + a * m_in
            return (C0, c0b, C1, c1b)
        C0, c0b, C1, c1b = _mixed_coeffs(alpha_e, alpha_r)
        W0 = w_fc * C0
        b0 = b_fc * c0b
        h = jnp.einsum('bte,he->bth', x, W0) + b0
        h = new_gelu(h)
        W1 = w_proj * C1
        b1 = b_proj * c1b
        out = jnp.einsum('bth,eh->bte', h, W1) + b1
        return out

    def _L1_attn_ref(x, nodevec1, nodevec2, norm1_w, norm1_b, norm2_w, norm2_b, gcn_w, gcn_b, conv_w, conv_b, gate_gcn_w, gate_gcn_b, gate_mamba_w, gate_mamba_b, out_w, out_b, m_in_w, m_conv_w, m_conv_b, m_xproj_w, m_dt_w, m_dt_b, m_A_log, m_D, m_out_w):
        import jax, jax.numpy as jnp
        import numpy as np
        from jax import lax
        ENC_IN = 64
        NODE_DIM = 16
        D_MODEL = 192
        D_STATE = 16
        D_CONV = 4
        EXPAND = 2
        D_INNER = EXPAND * D_MODEL
        DT_RANK = (D_MODEL + 15) // 16
        K_SP = min(7, D_MODEL // 4 + 1)
        B, L = (8, 128)
        EPS = 1e-05

        def _layernorm(x, w, b):
            mu = jnp.mean(x, axis=-1, keepdims=True)
            var = jnp.var(x, axis=-1, keepdims=True)
            return (x - mu) * lax.rsqrt(var + EPS) * w + b

        def _mamba(x, m_in_w, m_conv_w, m_conv_b, m_xproj_w, m_dt_w, m_dt_b, m_A_log, m_D, m_out_w):
            xz = x @ m_in_w
            xm, z = jnp.split(xz, 2, axis=-1)
            xc = jnp.swapaxes(xm, 1, 2)
            xc = lax.conv_general_dilated(xc, m_conv_w[:, None, :], window_strides=(1,), padding=[(D_CONV - 1, 0)], feature_group_count=D_INNER, dimension_numbers=('NCH', 'OIH', 'NCH'))
            xc = xc + m_conv_b[None, :, None]
            xm = jax.nn.silu(jnp.swapaxes(xc, 1, 2))
            x_dbl = xm @ m_xproj_w
            dt, Bm, Cm = jnp.split(x_dbl, [DT_RANK, DT_RANK + D_STATE], axis=-1)
            dt = jax.nn.softplus(dt @ m_dt_w + m_dt_b)
            A = -jnp.exp(m_A_log)
            dA = jnp.exp(dt[..., None] * A)
            dBx = dt[..., None] * Bm[:, :, None, :] * xm[..., None]
            dA_t = jnp.moveaxis(dA, 1, 0)
            dBx_t = jnp.moveaxis(dBx, 1, 0)
            h0 = jnp.zeros((xm.shape[0], D_INNER, D_STATE), xm.dtype)

            def step(h, c):
                dAt, dBxt = c
                h = dAt * h + dBxt
                return (h, h)
            _, hs = lax.scan(step, h0, (dA_t, dBx_t))
            y = jnp.einsum('lbdn,bln->bld', hs, Cm)
            y = y + m_D * xm
            y = y * jax.nn.silu(z)
            return y @ m_out_w

        def _reference_tuple_inner(x, nodevec1, nodevec2, norm1_w, norm1_b, norm2_w, norm2_b, gcn_w, gcn_b, conv_w, conv_b, gate_gcn_w, gate_gcn_b, gate_mamba_w, gate_mamba_b, out_w, out_b, m_in_w, m_conv_w, m_conv_b, m_xproj_w, m_dt_w, m_dt_b, m_A_log, m_D, m_out_w):
            residual = x
            adj = jax.nn.sigmoid(nodevec1 @ nodevec2)
            adj = adj * (1.0 - jnp.eye(ENC_IN, dtype=adj.dtype))
            xn = _layernorm(x, norm1_w, norm1_b)
            x_gcn = xn @ gcn_w + gcn_b
            pad = (K_SP - 1) // 2
            xc = lax.conv_general_dilated(jnp.swapaxes(xn, 1, 2), conv_w, window_strides=(1,), padding=[(pad, K_SP - 1 - pad)], dimension_numbers=('NCH', 'OIH', 'NCH'))
            xc = xc + conv_b[None, :, None]
            x_gcn = x_gcn + jnp.swapaxes(xc, 1, 2)
            x_mamba = _mamba(xn, m_in_w, m_conv_w, m_conv_b, m_xproj_w, m_dt_w, m_dt_b, m_A_log, m_D, m_out_w)
            gate = jax.nn.sigmoid(x_gcn @ gate_gcn_w + gate_gcn_b + (x_mamba @ gate_mamba_w + gate_mamba_b))
            fused = gate * x_gcn + (1.0 - gate) * x_mamba
            out = fused @ out_w + out_b
            out = _layernorm(out + residual, norm2_w, norm2_b)
            return (out, adj)
        return _reference_tuple_inner(x, nodevec1, nodevec2, norm1_w, norm1_b, norm2_w, norm2_b, gcn_w, gcn_b, conv_w, conv_b, gate_gcn_w, gate_gcn_b, gate_mamba_w, gate_mamba_b, out_w, out_b, m_in_w, m_conv_w, m_conv_b, m_xproj_w, m_dt_w, m_dt_b, m_A_log, m_D, m_out_w)[0]

    def _L1_ffn_ref(hidden_states, ln_gamma, ln_beta, router_w, w1, w2):
        import jax, jax.numpy as jnp
        import numpy as np
        D_MODEL, D_FF, N_EXPERTS, TOP_K = (192, 768, 8, 2)
        B, S = (2, 256)
        LN_EPS = 1e-05

        def _layernorm(x, gamma, beta):
            mu = jnp.mean(x, axis=-1, keepdims=True)
            var = jnp.mean(jnp.square(x - mu), axis=-1, keepdims=True)
            return (x - mu) * jax.lax.rsqrt(var + LN_EPS) * gamma + beta
        Bz, Sz, D = hidden_states.shape
        residual = hidden_states
        x = _layernorm(hidden_states, ln_gamma, ln_beta)
        tokens = x.reshape(-1, D)
        T = tokens.shape[0]
        logits = tokens @ router_w
        probs = jax.nn.softmax(logits, axis=-1)
        topw, topi = jax.lax.top_k(probs, TOP_K)
        topw = topw / jnp.sum(topw, axis=-1, keepdims=True)
        gates = jnp.zeros((T, N_EXPERTS), dtype=tokens.dtype)
        gates = gates.at[jnp.arange(T)[:, None], topi].set(topw)
        h = jnp.einsum('td,edf->etf', tokens, w1)
        h = jax.nn.silu(h)
        y = jnp.einsum('etf,efd->etd', h, w2)
        out = jnp.einsum('te,etd->td', gates, y)
        return residual + out.reshape(Bz, Sz, D)
    h = _L0_tok_ref(x, L0_tok_wte, L0_tok_W_proj, L0_tok_ln_w, L0_tok_ln_b, L0_tok_W_val, L0_tok_W_out, L0_tok_trace0)
    h = h + _L0_attn_ref(_layernorm(h, axis=-1), L0_attn_Wq, L0_attn_Wk, L0_attn_Wv, L0_attn_Wo)
    h = h + _L0_ffn_ref(_layernorm(h, axis=-1), L0_ffn_w_fc, L0_ffn_b_fc, L0_ffn_w_proj, L0_ffn_b_proj, L0_ffn_alpha_e, L0_ffn_alpha_r)
    h = h + _L1_attn_ref(_layernorm(h, axis=-1), L1_attn_nodevec1, L1_attn_nodevec2, L1_attn_norm1_w, L1_attn_norm1_b, L1_attn_norm2_w, L1_attn_norm2_b, L1_attn_gcn_w, L1_attn_gcn_b, L1_attn_conv_w, L1_attn_conv_b, L1_attn_gate_gcn_w, L1_attn_gate_gcn_b, L1_attn_gate_mamba_w, L1_attn_gate_mamba_b, L1_attn_out_w, L1_attn_out_b, L1_attn_m_in_w, L1_attn_m_conv_w, L1_attn_m_conv_b, L1_attn_m_xproj_w, L1_attn_m_dt_w, L1_attn_m_dt_b, L1_attn_m_A_log, L1_attn_m_D, L1_attn_m_out_w)
    h = h + _L1_ffn_ref(_layernorm(h, axis=-1), L1_ffn_ln_gamma, L1_ffn_ln_beta, L1_ffn_router_w, L1_ffn_w1, L1_ffn_w2)
    return h

_drawn_inputs = setup_inputs


def setup_inputs(seed=0):
    import zlib

    import numpy as np

    out = dict(_drawn_inputs(seed))
    spreads = {'L0_tok_ln_w': (1.0, 0.2),
     'L0_tok_ln_b': (0.0, 0.1),
     'L0_ffn_b_fc': (0.0, 0.1),
     'L0_ffn_b_proj': (0.0, 0.1),
     'L1_attn_norm1_w': (1.0, 0.6),
     'L1_attn_norm1_b': (0.0, 0.8),
     'L1_attn_norm2_w': (1.0, 0.2),
     'L1_attn_norm2_b': (0.0, 0.1),
     'L1_attn_gcn_b': (0.0, 2.0),
     'L1_attn_conv_b': (0.0, 2.0),
     'L1_attn_gate_gcn_b': (0.0, 2.0),
     'L1_attn_gate_mamba_b': (0.0, 2.0),
     'L1_attn_out_b': (0.0, 0.8),
     'L1_attn_m_conv_b': (0.0, 0.8),
     'L1_attn_m_dt_b': (0.5, 0.6),
     'L1_attn_m_D': (1.0, 0.6),
     'L1_ffn_ln_gamma': (1.0, 0.6),
     'L1_ffn_ln_beta': (0.0, 0.787)}
    factors = {'L0_tok_W_val': 8.0,
     'L1_attn_gate_gcn_w': 4.967,
     'L1_attn_gate_mamba_w': 8.0,
     'L1_attn_m_in_w': 8.0,
     'L1_attn_m_conv_w': 8.0,
     'L1_attn_m_xproj_w': 8.0,
     'L1_attn_m_dt_w': 8.0,
     'L1_attn_m_A_log': 8.0,
     'L1_attn_m_out_w': 8.0,
     'L1_attn_gcn_w': 4.53}
    for name, (base, spread) in spreads.items():
        noise = np.random.default_rng([zlib.crc32(name.encode()), seed]).standard_normal(out[name].shape)
        drawn = base * np.exp(spread * noise) if base else spread * noise
        out[name] = jnp.asarray(drawn.astype(out[name].dtype))
    for name, factor in factors.items():
        out[name] = (out[name] * factor).astype(out[name].dtype)
    return out
```

```python
import concourse.bass as bass
from concourse import mybir
from contextlib import ExitStack

F32 = mybir.dt.float32
BF16 = mybir.dt.bfloat16
I32 = mybir.dt.int32
ACT = mybir.ActivationFunctionType
ALU = mybir.AluOpType
AX = mybir.AxisListType

BATCH, SEQ, D = 32, 256, 192
T = BATCH * SEQ
P = 128
NT = T // P
TPB = 4
BT = TPB * P
NB = T // BT
SETUP_DMAS = 12
SPB = BT // SEQ
KP, KT = 96, 2
HEADS, DTR = 8, 64
HD = HEADS * DTR
KV = 64
FF = 768
FT = FF // P
DI = 384
DT3 = DI // P
NS = 16
RANK = 12
TAPS, CTAPS = 7, 4
EXP, TOPK = 8, 2
EPS = 1e-5
TRACE_LR, TRACE_DECAY = 0.1, 0.99
CREDIT = 3

PE_STEPS = ["bias_outer", "x1", "update", "readout", "g", "scores", "probT", "b0", "b1", "c0", "c1"]
ACT_STEPS = ["x1", "readout", "g", "exp0", "exp1", "probT"]
DVE_STEPS = ["ones", "sum_row", "alpha", "scaled_mask", "m0w", "m0", "m1w", "m1", "decayed", "trace", "max",
             "negmax", "recip", "prob0", "prob1", "b0", "b1", "w0", "w1"]


def nth(steps, name):
    return steps.index(name) + 1


class Event:

    def __init__(self, sem, per, ahead=CREDIT):
        self.sem, self.per, self.ahead = sem, per, ahead

    def at(self, block, nth=None):
        return (block + self.ahead) * self.per + (self.per if nth is None else nth)


def build(nc, d, out):
    ctx = ExitStack()
    with ctx:
        def sb(name, shape, dt=F32):
            return ctx.enter_context(nc.sbuf_tensor(name, shape, dt))

        def sem(name):
            return ctx.enter_context(nc.semaphore(name))

        events = []

        def event(name, per=1, ahead=CREDIT):
            e = Event(sem(name), per, ahead)
            events.append(e)
            return e

        H = sb("H", [P, NT, D])
        ARENA = 31840
        arena = sb("arena", [P, ARENA])
        top = [0]

        def carve(p, *shape, dt=F32):
            n = 1
            for s in shape:
                n *= s
            words = (n + 1) // 2 if dt == BF16 else n
            at = top[0]
            top[0] += (words + 3) // 4 * 4
            assert top[0] <= ARENA, top[0]
            v = arena[0:p, at:at + words]
            if dt != F32:
                v = v.bitcast(dt)
            if len(shape) == 1:
                return v
            names = "abcd"[:len(shape)]
            kw = {names[q]: shape[q] for q in range(1, len(shape))}
            return v.rearrange(f"p ({' '.join(names)}) -> p {' '.join(names)}", **kw)

        ident = sb("ident", [P, P])
        ps = ctx.enter_context(nc.psum_tensor("ps", [P, 8, 512], F32))

        def tiles_of(bank):
            return ps[:, bank:bank + 2, 0:2 * D]

        def tile_in(bank, t):
            return ps[:, bank + t // 2, (t % 2) * D:(t % 2 + 1) * D]

        exps_half = sb("exps_half", [P, 8])

        wconv = sb("wconv", [KP, KT, TAPS, D])
        win = sb("win", [KP, KT, 2 * DI])
        wxp = sb("wxp", [P, DT3, 3 * 32 + RANK])
        wdt = sb("wdt", [P, DI])
        wmo = sb("wmo", [P, DT3, D])
        wgg = sb("wgg", [KP, KT, D])
        wgm = sb("wgm", [KP, KT, D])
        wout = sb("wout", [KP, KT, D])
        pick32 = sb("pick32", [KP, 32])
        vc = sb("vc", [P, 80])
        n1w, n1b = vc[0:KP, 0:2], vc[0:KP, 2:4]
        gcb, cvb = vc[0:KP, 4:6], vc[0:KP, 6:8]
        ggb, gmb = vc[0:KP, 8:10], vc[0:KP, 10:12]
        cw = vc[:, 12:24].rearrange("p (a b) -> p a b", b=CTAPS)
        cb, dtb, dskip = vc[:, 24:27], vc[:, 27:30], vc[:, 30:33]
        xgb, gateb = vc[0:KP, 34:36], vc[0:KP, 36:38]
        nega = sb("nega", [P, DT3, NS])
        va = sb("va", [P, 40])
        lnw, lnb = va[0:KP, 0:2], va[0:KP, 2:4]
        mow, mob = va[0:KP, 4:6], va[0:KP, 6:8]
        bfc, b0 = va[:, 8:14], va[:, 14:20]
        wa2, wa = va[0:9, 20:22], va[0:9, 22:23]
        lnbrow = sb("lnbrow", [KP + 1, D])
        b1row = sb("b1row", [1, D])
        ones = sb("ones", [1, P])

        s_const = sem("constants_loaded")
        s_wc = sem("phase_c_weights_loaded")
        s_wc2 = sem("phase_c_late_weights_loaded")
        s_wa = sem("setup_weights_loaded")
        s_ids = sem("ids_loaded")
        tok_loaded = [event(f"tok{j}_gathered", 4 * 16, ahead=0) for j in range(2)]
        shifted = [event(f"tok{j}_shifted", 2 * 16) for j in range(2)]
        s_alone = sem("waits_alone")
        s_zero = sem("outer_banks_zero")
        s_setup = sem("setup_steps_vector")
        s_setup_pe = sem("setup_steps_tensor")
        s_setup_act = sem("setup_steps_scalar")
        s_setup_gp = sem("xs_zero_column")

        top[0] = 0
        XT = carve(KP, KT, T)
        w0 = carve(KP, KT, FF)
        w1 = carve(P, FT, D)
        base_b = top[0]
        ids = carve(P, NT, dt=I32)
        tok = [carve(P, TPB, D) for _ in range(2)]
        tok2 = [carve(P, TPB, D) for _ in range(2)]
        nrm = [carve(P, TPB, D + 1) for _ in range(2)]
        stA = carve(P, TPB, 6)
        mvA = carve(P, TPB, 2)
        veA = carve(P, TPB)
        rsA = [carve(P, TPB) for _ in range(2)]
        WpT = carve(KP, KT, HD)
        WvT = carve(KP, KT, HD)
        WpH = carve(DTR, HEADS, D)
        WoH = carve(DTR, HEADS, D)
        tr = carve(DTR, HEADS, DTR)
        MS = carve(KP, KT, D)
        srow = carve(KP + 1, D)
        X1 = WpT
        minp = carve(9, D)
        mins = carve(9, D)
        mout = carve(9, FF)
        rope = carve(KP, KT, SEQ)
        smax = carve(P, 2)
        ssum = carve(P, 2)
        prob = tok[0].rearrange("p a b -> p (a b)")[:, 0:2 * SEQ].rearrange("p (q k) -> p q k", q=2)

        idn = [sb(f"idn{j}", [P, TPB], I32)[:, :] for j in range(2)]
        ids_staged = [event(f"ids_staged{j}") for j in range(2)]
        stats_a = event("stats_a")
        mv_a = event("mean_var_a")
        var_a = event("variance_a")
        rstd_a = event("rstd_a")
        nrm_a = event("normed_a")
        nrmT_a = event("transposed_a")
        xt_a = event("xt_stored_a")
        outer_a = event("outer_product_a")

        G = sb("G", [KP, KT, D])
        PT = sb("PT", [P, 2, SEQ])
        wv = sb("wv", [KP, KT, KV])
        wo = sb("wo", [KV, D])
        top[0] = base_b
        xs = carve(KP, KT, SPB, SEQ)
        h0c = carve(P, TPB, D)
        hA = carve(P, TPB, D)
        xn1 = carve(P, TPB, D)
        xn2 = carve(P, TPB, D)
        x1T = carve(KP, KT, BT)
        x2T = carve(KP, KT, BT)
        vs = carve(P, TPB, KV)
        oTs = carve(KV, BT)
        hT = carve(P, FT, BT)
        stB = carve(P, TPB, 6)
        mvB = carve(P, TPB, 2)
        veB = carve(P, TPB)
        rsB = carve(P, TPB)

        xs_loaded = event("xs_loaded", 16 * KT)
        h0_ready = event("h0_ready")
        h0_kept = event("h0_kept")
        t1_ready = event("t1_ready")
        x1T_kept = event("x1T_kept")
        v_ready = event("v_ready")
        v_kept = event("v_kept")
        oT_ready = event("oT_ready")
        oT_kept = event("oT_kept")
        att_ready = event("att_ready")
        hA_kept = event("hA_kept")
        st_b = event("stats_b", 2)
        mv_b = event("mean_var_b", 2)
        ve_b = event("var_eps_b", 2)
        rs_b = event("rstd_b", 2)
        xn1_kept = event("xn1_kept")
        xn2_kept = event("xn2_kept")
        t2_ready = event("t2_ready")
        x2T_kept = event("x2T_kept")
        up_ready = event("up_ready", FT)
        gelu_kept = event("gelu_kept", FT)
        down_ready = event("down_ready")
        hB_kept = event("hB_kept")

        top[0] = 0
        wgcn = carve(KP, KT, D)
        n2w, n2b, outb = (carve(P, D) for _ in range(3))
        pick = carve(KP, 32, P, dt=BF16)
        dtp = [carve(P, DT3, BT) for _ in range(2)]
        up_ = [carve(P, DT3, BT) for _ in range(2)]
        xm = [carve(P, DT3, BT) for _ in range(2)]
        zs = [carve(P, DT3, BT) for _ in range(2)]
        xg = [carve(KP, KT, BT) for _ in range(2)]
        xnC = carve(P, TPB, D)
        PADX = SEQ + TAPS - 1
        xnT = carve(KP, KT, SPB, PADX)
        PADC = SEQ + CTAPS - 1
        xi = carve(P, DT3, SPB, PADC)
        bc = [carve(KP, BT, dt=BF16) for _ in range(2)]
        xr = carve(P, TPB, D)
        flat = lambda v: v.rearrange("p a b -> p (a b)")
        rest = flat(xr)[0:KP, 0:BT]
        mid = flat(xr)[0:KP, BT:BT + BT // 2].bitcast(BF16)
        dtl = carve(P, BT)
        sp1 = carve(P, DT3, BT)
        dA = [carve(P, DT3, SPB, SEQ) for _ in range(2)]
        hs = [carve(P, DT3, BT) for _ in range(2)]
        xmb = carve(KP, KT, BT)
        gate = sp1[0:KP, 0:KT, :]
        o = xnC
        stC = carve(P, TPB, 6)
        mvC = [carve(P, TPB, 2) for _ in range(2)]
        pvC = carve(P, 2, TPB)
        rsC = [carve(P, 2, TPB) for _ in range(2)]
        stO = carve(P, TPB, 6)
        mvO = carve(P, TPB, 2)
        veO = carve(P, TPB)
        rsO = carve(P, TPB)
        s_cset = sem("phase_c_ready")
        s_cact = sem("decay_rates_exp")

        st_c = event("stats_c")
        mv_c = event("mean_var_c")
        pv_c = event("var_eps_c")
        rs_c = event("rstd_c")
        xn_c = event("xn_c")
        xnT_ready = event("xnT_ready")
        xnT_kept = event("xnT_kept", KT)
        in_ready = event("in_proj_ready", 2 * DT3)
        in_kept = event("in_proj_kept", 2 * DT3)
        conv_ch = event("channel_conv", DT3 * CTAPS)
        silu_kept = event("silu_kept", 2 * DT3)
        xp_ready = event("x_proj_ready")
        dtl_kept = event("dt_low_kept")
        split = event("bc_split", 5)
        dt_ready = event("dt_ready", DT3)
        sp_abs = event("softplus_abs", DT3)
        sp_exp = event("softplus_exp", DT3)
        sp_log = event("softplus_log", DT3)
        sp_max = event("softplus_max", DT3)
        dt_kept = event("dt_kept", DT3)
        u_kept = event("u_kept", DT3)
        gcn_ready = event("gcn_ready", KT)
        gcn_kept = event("gcn_kept", KT)
        b_ready = event("b_broadcast", NS)
        c_ready = event("c_broadcast", NS)
        da_ready = event("decay_ready", NS * DT3)
        dbx = event("dbx", NS * DT3)
        scan = event("scan", NS * DT3)
        hc = event("h_times_c", NS * DT3)
        nsum = event("state_sum", NS)
        ysk = event("y_skip", DT3)
        yz = event("y_gated", DT3)
        mo_ready = event("mamba_out_ready", KT)
        mo_kept = event("mamba_out_kept", KT)
        gt_ready = event("gate_ready", KT)
        gt_kept = event("gate_kept", KT)
        gt_tanh = event("gate_tanh", KT)
        fuse = event("fuse", 3)
        out_ready = event("out_ready")
        o_kept = event("o_kept", 3)
        st_o = event("stats_o")
        mv_o = event("mean_var_o")
        ve_o = event("var_eps_o")
        rs_o = event("rstd_o")
        on_o = event("o_normed")
        tail_o = event("o_affine", 3)

        top[0] = 0
        tokT = carve(KP, KT, T)
        w1e = [carve(KP, KT, FF) for _ in range(2)]
        w2e = [carve(P, FT, D) for _ in range(2)]
        hE = [carve(P, FT, BT) for _ in range(2)]
        base_d = top[0]
        rout = carve(KP, KT, EXP)
        tri = carve(P, EXP, EXP)
        gates = carve(P, NT, EXP)
        top[0] = base_d - 2 * FT * BT
        xnD = carve(P, TPB, D)
        xrD = carve(P, TPB, D)
        xTs = carve(KP, KT, BT)
        stD = carve(P, TPB, 6)
        mvD = carve(P, TPB, 2)
        pvD = carve(P, 2, TPB)
        rsD = carve(P, 2, TPB)
        lg = carve(P, TPB, EXP)
        lmax = carve(P, TPB)
        pr = carve(P, TPB, EXP)
        psm = carve(P, TPB)
        cmp1 = carve(P, TPB, EXP, EXP)
        cmp2 = carve(P, TPB, EXP, EXP)
        rank = carve(P, TPB, EXP)
        assert top[0] <= base_d

        s_wd = sem("router_loaded")
        st_d = event("stats_d")
        mv_d = event("mean_var_d")
        pv_d = event("var_eps_d")
        rs_d = event("rstd_d")
        xn_d = event("xn_d")
        dT_ready = event("dT_ready")
        dT_kept = event("dT_kept", KT)
        tokT_stored = event("tokT_stored", 16)
        lg_ready = event("logits_ready")
        NG = 15
        gsteps = event("gating_steps", NG)
        gexp = event("gating_exp")
        res_d = event("residual_d", 5)
        we_loaded = [event(f"expert{j}_loaded", 32) for j in range(2)]
        e_up = event("expert_up", FT)
        e_silu = event("expert_silu", FT)
        e_down = event("expert_down")
        e_acc = event("expert_added", TPB)
        s_out = sem("output_stored")

        block = ctx.enter_context(nc.Block())
        V = nc.vector

        def wait(eng, ev, b, nth=None):
            eng.wait_ge(ev.sem, ev.at(b, nth))

        def wait_alone(eng, ev, b, nth=None):
            eng.wait_ge(ev.sem, ev.at(b, nth))
            eng.sem_inc(s_alone, 1)


        def load_expert(sp, e, j):
            n = KP * KT * FF
            sp.dma_start(w1e[j], d["w1"][bass.ds(e * KP, KP), :].rearrange("p (k f) -> p k f", k=KT))\
                .then_inc(we_loaded[j].sem, 16)
            sp.dma_start(w2e[j], d["w2"][bass.ds(e * P, P), :].rearrange("p (k f) -> p k f", k=FT))\
                .then_inc(we_loaded[j].sem, 16)

        def shift(sp, i, q, j):
            wait_alone(sp, tok_loaded[j], q)
            wait_alone(sp, outer_a, i - 2)
            sp.dma_start(tok2[j][0:P - 2, :, :], tok[j][2:P, :, :]).then_inc(shifted[j].sem, 16)
            sp.dma_start(tok2[j][P - 2:P, 0:TPB:2, :], tok[j][0:2, 1:TPB:2, :]).then_inc(shifted[j].sem, 16)

        def load_xs(sp, i):
            wait_alone(sp, h0_ready, i - 1)
            for k in range(KT):
                sp.dma_start(xs[:, k, :, 1:SEQ],
                             XT[:, k, bass.ds(i * BT, BT)].rearrange("p (s t) -> p s t", s=SPB)[:, :, 0:SEQ - 1])\
                    .then_inc(xs_loaded.sem, 16)

        @block.sync
        def _(sp):
            sp.dma_start(ids, d["ids"]).then_inc(s_ids, 16)
            sp.dma_start(ident[:, :], d["ident"]).then_inc(s_const, 16)
            sp.dma_start(exps_half[:, :], d["mhalf"]).then_inc(s_const, 16)
            sp.dma_start(va[0:KP, 0:8], d["va_fm"]).then_inc(s_const, 16)
            sp.dma_start(va[:, 8:14], d["b_fc"]).then_inc(s_const, 16)
            sp.dma_start(wa2, d["alphas"]).then_inc(s_const, 16)
            sp.dma_start(lnbrow[KP:KP + 1, :], d["ln_b_row"]).then_inc(s_const, 16)
            sp.dma_start(b1row[:, :], d["b_proj_row"]).then_inc(s_const, 16)
            for dst, name in ((WpT, "WpT"), (WvT, "WvT"), (WpH, "WpH"), (WoH, "WoH"), (tr, "traceT"),
                              (minp, "mask_in"), (mout, "mask_out"), (rope, "rope"), (w0, "W0T"), (w1, "W1T")):
                sp.dma_start(dst, d[name]).then_inc(s_wa, 16)
            sp.dma_start(wv[:, :, :], d["Wv"]).then_inc(s_wa, 16)
            sp.dma_start(wo[:, :], d["Wo"]).then_inc(s_wa, 16)
            with sp.Fori(0, NB // 2) as q:
                for j in (0, 1):
                    shift(sp, 2 * q + j, q, j)
            for dst, name in ((wconv, "wconv"), (win, "win"), (wxp, "wxp"), (wmo, "wmo"), (wgg, "wgg"),
                              (wgm, "wgm"), (wout, "wout")):
                sp.dma_start(dst[:, :] if len(dst.shape) == 2 else
                             (dst[:, :, :] if len(dst.shape) == 3 else dst[:, :, :, :]),
                             d[name]).then_inc(s_wc, 16)
            sp.dma_start(wdt[96:96 + RANK, :], d["wdt"]).then_inc(s_wc, 16)
            sp.dma_start(pick32[:, :], d["pick"]).then_inc(s_wc, 16)
            sp.dma_start(vc[0:KP, 0:12], d["vc_fm"]).then_inc(s_wc, 16)
            sp.dma_start(vc[:, 12:33], d["vc_ch"]).then_inc(s_wc, 16)
            sp.dma_start(nega[:, :, :], d["A_log"]).then_inc(s_wc, 16)
            sp.wait_ge(s_setup_gp, 1)
            load_xs(sp, 0)
            with sp.Fori(1, NB) as i:
                load_xs(sp, i)
            wait_alone(sp, hB_kept, NB - 1)
            sp.dma_start(wgcn, d["wgcn"]).then_inc(s_wc2, 16)
            for dst, name in ((n2w, "n2w"), (n2b, "n2b"), (outb, "outb")):
                sp.dma_start(dst, d[name].partition_broadcast(P)).then_inc(s_wc2, 16)
            wait_alone(sp, tail_o, NB - 1)
            sp.dma_start(rout, d["router"]).then_inc(s_wd, 16)
            sp.dma_start(tri, d["tri"]).then_inc(s_wd, 16)
            for j in (0, 1):
                load_expert(sp, j, j)
            with sp.Fori(0, NB) as i:
                wait_alone(sp, dT_kept, i)
                sp.dma_start(tokT[:, :, bass.ds(i * BT, BT)], xTs).then_inc(tokT_stored.sem, 16)
            with sp.Fori(0, EXP // 2 - 1) as ee:
                for j in (0, 1):
                    wait_alone(sp, e_down, (2 * ee + j) * NB + NB - 1)
                    load_expert(sp, 2 * ee + 2 + j, j)
            with sp.Fori(0, NB) as i:
                wait_alone(sp, e_acc, i + (EXP - 1) * NB)
                sp.dma_start(out[bass.ds(i * BT, BT), :].rearrange("(t p) f -> p t f", p=P),
                             H[:, bass.ds(i * TPB, TPB), :]).then_inc(s_out, 16)
            sp.wait_ge(s_out, 16 * NB)

        def inv_root_a(gp, i, j):
            wait(gp, var_a, i)
            wait(gp, nrm_a, i - 2)
            nc.gpsimd.tensor_tensor(rsA[j], veA, exps_half[:, 0:TPB], ALU.pow).then_inc(rstd_a.sem, 1)

        def gather(gp, i, q, j):
            wait(gp, nrm_a, i - 2)
            wait(gp, shifted[j], q - 1)
            nc.gpsimd.tensor_copy(idn[j], ids[:, bass.ds(i * TPB, TPB)]).then_inc(ids_staged[j].sem, 1)
            wait_alone(gp, ids_staged[j], q)
            for t in range(TPB):
                gp.indirect_dma_start(
                    out=tok[j][:, t, :], out_offset=None, in_=d["wte"],
                    in_offset=bass.IndirectOffsetOnAxis(ap=idn[j][:, t:t + 1], axis=0))\
                    .then_inc(tok_loaded[j].sem, 16)

        def rs_c_step(gp, i, j):
            wait(gp, pv_c, i)
            nc.gpsimd.tensor_tensor(rsC[j], pvC, exps_half[:, 0:8].rearrange("p (a b) -> p a b", a=2),
                                    ALU.pow).then_inc(rs_c.sem, 1)

        def back_gp(gp, i):
            wait(gp, ve_o, i)
            nc.gpsimd.tensor_tensor(rsO, veO, exps_half[:, 0:TPB], ALU.pow).then_inc(rs_o.sem, 1)
            wait(gp, on_o, i)
            nc.gpsimd.tensor_tensor(o, o, n2w.unsqueeze(1).broadcast_to([P, TPB, D]), ALU.mult)\
                .then_inc(tail_o.sem, 1)
            wait(gp, tail_o, i, 1)
            nc.gpsimd.tensor_tensor(o, o, n2b.unsqueeze(1).broadcast_to([P, TPB, D]), ALU.add)\
                .then_inc(tail_o.sem, 1)
            wait(gp, tail_o, i, 2)
            Hi = H[:, bass.ds(i * TPB, TPB), :]
            nc.gpsimd.tensor_tensor(Hi, Hi, o, ALU.add).then_inc(tail_o.sem, 1)

        def body_gp(gp, i, j, front=True, back=True):
            if front:
                rs_c_step(gp, i + 1, 1 - j)
            if back:
                back_gp(gp, i - 1)

        @block.gpsimd
        def _(gp):
            for e in events:
                if e.ahead:
                    gp.sem_inc(e.sem, e.ahead * e.per)
            gp.wait_ge(s_ids, 16)
            for j in (0, 1):
                gather(gp, j, 0, j)
            gp.wait_ge(s_const, 16 * 7)
            with gp.Fori(1, NB // 2) as q:
                for j in (0, 1):
                    inv_root_a(gp, 2 * q - 2 + j, j)
                    gather(gp, 2 * q + j, q, j)
            for j in (0, 1):
                inv_root_a(gp, NB - 2 + j, j)
            gp.wait_ge(s_setup, nth(DVE_STEPS, "w1"))
            nc.gpsimd.memset(xs[:, :, :, 0:1], 0.0).then_inc(s_setup_gp, 1)
            with gp.Fori(0, NB) as i:
                for q in (1, 2):
                    wait(gp, ve_b, i, q)
                    nc.gpsimd.tensor_tensor(rsB, veB, exps_half[:, 0:TPB], ALU.pow).then_inc(rs_b.sem, 1)
            rs_c_step(gp, 0, 0)
            body_gp(gp, 0, 0, back=False)
            with gp.Fori(0, NB // 2 - 1) as ii:
                for j in (1, 0):
                    body_gp(gp, 2 * ii + (1 if j else 2), j)
            body_gp(gp, NB - 1, 1, front=False)
            back_gp(gp, NB - 1)
            with gp.Fori(0, NB) as i:
                wait(gp, pv_d, i)
                nc.gpsimd.tensor_tensor(rsD, pvD, exps_half[:, 0:8].rearrange("p (a b) -> p a b", a=2),
                                        ALU.pow).then_inc(rs_d.sem, 1)

        def up_e(pe, g, b, j, h):
            for f in range(FT):
                if f >= 4:
                    wait(pe, e_silu, g, f - 3)
                else:
                    wait(pe, e_silu, g - 1, FT + f - 3)
                for k in range(KT):
                    last = nc.tensor.matmul(ps[:, ubank(f, h), :], w1e[j][:, k, f * P:(f + 1) * P],
                                            tokT[:, k, bass.ds(b * BT, BT)], start=(k == 0), stop=(k == KT - 1))
                last.then_inc(e_up.sem, 1)

        def ubank(f, h):
            return (f + FT * h) % 4

        def down_e(pe, g, j, h):
            wait(pe, e_silu, g)
            wait(pe, e_acc, g - 2)
            for t in range(TPB):
                for f in range(FT):
                    last = nc.tensor.matmul(tile_in(4 + 2 * h, t), hE[h][:, f, t * P:(t + 1) * P],
                                            w2e[j][:, f, :], start=(f == 0), stop=(f == FT - 1))
            last.then_inc(e_down.sem, 1)

        def setup_pe(pe):
            steps = iter(PE_STEPS)

            def done(name, ins):
                assert next(steps) == name
                ins.then_inc(s_setup_pe, 1)

            pe.wait_ge(s_setup, nth(DVE_STEPS, "sum_row"))
            for k in range(KT):
                last = nc.tensor.matmul(ps[0:KP, 6, k * D:(k + 1) * D], lnbrow[KP:KP + 1, k * KP:(k + 1) * KP],
                                        srow[KP:KP + 1, :], start=True, stop=True)
            done("bias_outer", last)
            pe.wait_ge(s_wa, 16 * SETUP_DMAS)
            wait(pe, xt_a, NB - 1)
            pe.wait_ge(s_setup, nth(DVE_STEPS, "m1"))
            for m in range(KT):
                for k in range(KT):
                    last = nc.tensor.matmul(ps[0:KP, m, :], MS[:, k, m * KP:(m + 1) * KP], WpT[:, k, :],
                                            start=(k == 0), stop=(k == KT - 1))
            done("x1", last)
            pe.wait_ge(s_setup_act, nth(ACT_STEPS, "x1"))
            for h in range(HEADS):
                for k in range(KT):
                    last = nc.tensor.matmul(ps[0:DTR, 2, h * DTR:(h + 1) * DTR], WvT[:, k, h * DTR:(h + 1) * DTR],
                                            X1[:, k, h * DTR:(h + 1) * DTR], start=(k == 0), stop=(k == KT - 1))
            done("update", last)
            pe.wait_ge(s_setup, nth(DVE_STEPS, "trace"))
            for h in range(HEADS):
                last = nc.tensor.matmul(ps[0:DTR, 4 + h // 2, (h % 2) * D:(h % 2 + 1) * D], tr[:, h, :],
                                        WoH[:, h, :], start=True, stop=True)
            done("readout", last)
            pe.wait_ge(s_setup_act, nth(ACT_STEPS, "readout"))
            for k in range(KT):
                for h in range(HEADS):
                    last = nc.tensor.matmul(ps[0:KP, k, 0:D], WpH[:, h, k * KP:(k + 1) * KP], WoH[:, h, :],
                                            start=(h == 0), stop=(h == HEADS - 1))
            done("g", last)
            for q in range(2):
                for k in range(KT):
                    last = nc.tensor.matmul(ps[:, 2 + q, 0:SEQ], rope[:, k, q * P:(q + 1) * P], rope[:, k, :],
                                            start=(k == 0), stop=(k == KT - 1))
            done("scores", last)
            pe.wait_ge(s_setup, nth(DVE_STEPS, "prob1"))
            for q in range(2):
                for k in range(2):
                    last = nc.tensor.transpose(ps[:, 4 + k, q * P:(q + 1) * P], prob[:, q, k * P:(k + 1) * P],
                                               ident[:, :])
            done("probT", last)
            for f in range(FT):
                last = nc.tensor.matmul(ps[:, 6, f:f + 1], mout[:, f * P:(f + 1) * P], wa, start=True, stop=True)
            done("b0", last)
            last = nc.tensor.matmul(ps[0:1, 7, 0:D], wa, minp, start=True, stop=True)
            done("b1", last)
            pe.wait_ge(s_setup_act, nth(ACT_STEPS, "g"))
            for k in range(KT):
                for n in range(2):
                    last = nc.tensor.matmul(ps[0:KP, 2 * k + n, 0:FF // 2], mins[:, k * KP:(k + 1) * KP],
                                            mout[:, n * (FF // 2):(n + 1) * (FF // 2)], start=True, stop=True)
            done("c0", last)
            pe.wait_ge(s_setup, nth(DVE_STEPS, "w0"))
            for f in range(FT):
                last = nc.tensor.matmul(ps[:, f // 2, (f % 2) * D:(f % 2 + 1) * D], mout[:, f * P:(f + 1) * P],
                                        mins, start=True, stop=True)
            done("c1", last)

        def att_front_pe(pe, i, ffn):
            ffn = ffn or (lambda part: None)
            wait(pe, xs_loaded, i)
            wait(pe, hA_kept, i - 1)
            for t in range(TPB):
                for k in range(KT):
                    last = nc.tensor.matmul(tile_in(0, t), xs[:, k, t // 2, (t % 2) * P:(t % 2 + 1) * P],
                                            G[:, k, :], start=(k == 0), stop=(k == KT - 1))
            last.then_inc(h0_ready.sem, 1)
            ffn(0)
            wait(pe, xn1_kept, i)
            wait(pe, x2T_kept, i - 1)
            for t in range(TPB):
                for k in range(KT):
                    last = nc.tensor.transpose(ps[0:KP, 2 + k, t * P:(t + 1) * P], xn1[:, t, k * KP:(k + 1) * KP],
                                               ident[:, :])
            last.then_inc(t1_ready.sem, 1)
            ffn(1)
            wait(pe, x1T_kept, i)
            for t in range(TPB):
                for k in range(KT):
                    last = nc.tensor.matmul(ps[:, 2, t * KV:(t + 1) * KV], x1T[:, k, t * P:(t + 1) * P], wv[:, k, :],
                                            start=(k == 0), stop=(k == KT - 1))
            last.then_inc(v_ready.sem, 1)
            ffn(2)
            wait(pe, v_kept, i)
            for s in range(SPB):
                for k in range(2):
                    last = nc.tensor.matmul(ps[0:KV, 3, s * SEQ:(s + 1) * SEQ], vs[:, 2 * s + k, :], PT[:, k, :],
                                            start=(k == 0), stop=(k == 1))
            last.then_inc(oT_ready.sem, 1)
            ffn(3)
            wait(pe, oT_kept, i)
            wait(pe, h0_kept, i)
            for t in range(TPB):
                last = nc.tensor.matmul(tile_in(0, t), oTs[:, t * P:(t + 1) * P], wo[:, :], start=True, stop=True)
            last.then_inc(att_ready.sem, 1)

        def body_b_pe(pe, i, more=True):
            def ffn(part):
                if part == 0:
                    wait(pe, xn2_kept, i)
                    wait(pe, oT_kept, i)
                    for t in range(TPB):
                        for k in range(KT):
                            last = nc.tensor.transpose(ps[0:KP, 2 + k, t * P:(t + 1) * P],
                                                       xn2[:, t, k * KP:(k + 1) * KP], ident[:, :])
                    last.then_inc(t2_ready.sem, 1)
                    wait(pe, x2T_kept, i)
                if part in (0, 1):
                    for f in range(3 * part, 3 * part + 3):
                        if f >= 2:
                            wait(pe, gelu_kept, i, f - 1)
                        else:
                            wait(pe, gelu_kept, i - 1, FT + f - 1)
                        for k in range(KT):
                            last = nc.tensor.matmul(ps[:, 6 + f % 2, :], w0[:, k, f * P:(f + 1) * P], x2T[:, k, :],
                                                    start=(k == 0), stop=(k == KT - 1))
                        last.then_inc(up_ready.sem, 1)
                if part in (2, 3):
                    if part == 2:
                        wait(pe, gelu_kept, i)
                        wait(pe, hB_kept, i - 1)
                    for t in (0, 1) if part == 2 else (2, 3):
                        for f in range(FT):
                            nc.tensor.matmul(tile_in(4, t), hT[:, f, t * P:(t + 1) * P], w1[:, f, :],
                                             start=(f == 0), stop=False)
                        last = nc.tensor.matmul(tile_in(4, t), ones[:, :], b1row[:, :], start=False, stop=True)
                    if part == 3:
                        last.then_inc(down_ready.sem, 1)

            if more:
                att_front_pe(pe, i + 1, ffn)
            else:
                for part in range(4):
                    ffn(part)

        def transposes_c(pe, i):
            wait(pe, xn_c, i)
            wait(pe, mo_kept, i - 2)
            wait(pe, sp_abs, i - 1)
            wait(pe, gt_kept, i - 2, 1)
            wait(pe, gcn_kept, i - 1)
            for t in range(TPB):
                for k in range(KT):
                    last = nc.tensor.transpose(ps[0:KP, 6 + k, t * P:(t + 1) * P], xnC[:, t, k * KP:(k + 1) * KP],
                                               ident[:, :])
            last.then_inc(xnT_ready.sem, 1)

        def in_proj(pe, i, f):
            if f == 0:
                wait(pe, xnT_kept, i)
                wait(pe, gt_kept, i - 2)
            if f >= 2:
                wait(pe, in_kept, i, f - 1)
            for k in range(KT):
                last = nc.tensor.matmul(ps[:, 5 + f % 2, :], win[:, k, f * P:(f + 1) * P],
                                        xnT[:, k, :, TAPS // 2:TAPS // 2 + SEQ], start=(k == 0), stop=(k == KT - 1))
            last.then_inc(in_ready.sem, 1)

        def x_proj(pe, i, j):
            wait(pe, silu_kept, i, DT3)
            wait(pe, in_kept, i)
            wait(pe, o_kept, i - 2, 3)
            for k in range(DT3):
                last = nc.tensor.matmul(ps[0:108, 5, :], wxp[:, k, :], xm[j][:, k, :],
                                        start=(k == 0), stop=(k == DT3 - 1))
            last.then_inc(xp_ready.sem, 1)

        def dt_proj(pe, i):
            wait(pe, dtl_kept, i)
            for f in range(DT3):
                if f == 1:
                    wait(pe, split, i, 2)
                if f == 2:
                    wait(pe, sp_abs, i, 1)
                last = nc.tensor.matmul(ps[:, 6 - f % 2, :], wdt[96:96 + RANK, f * P:(f + 1) * P],
                                        dtl[96:96 + RANK, :], start=True, stop=True)
                last.then_inc(dt_ready.sem, 1)

        def gcn(pe, i, a, b):
            for n in range(a, b):
                m, r = divmod(n, KT * TAPS)
                if n == 0:
                    wait(pe, xnT_kept, i)
                elif r == 0:
                    wait(pe, gcn_kept, i, 1)
                tap, k = divmod(r, KT)
                last = nc.tensor.matmul(ps[0:KP, 7, :], wconv[:, k, tap, m * KP:(m + 1) * KP],
                                        xnT[:, k, :, tap:tap + SEQ], start=(r == 0), stop=(r == KT * TAPS - 1))
                if r == KT * TAPS - 1:
                    last.then_inc(gcn_ready.sem, 1)

        def front_pe(pe, i, j):
            transposes_c(pe, i)
            for f in range(2 * DT3):
                in_proj(pe, i, f)
            x_proj(pe, i, j)
            dt_proj(pe, i)
            gcn(pe, i, 0, 28)

        def mamba_out(pe, i, j, m, last_block):
            if m == 0:
                wait(pe, yz, i)
            if not last_block:
                wait(pe, sp_abs, i + 1)
            wait(pe, o_kept, i - 1, 3)
            for k in range(DT3):
                last = nc.tensor.matmul(ps[0:KP, 5 + m, :], wmo[:, k, m * KP:(m + 1) * KP], zs[j][:, k, :],
                                        start=(k == 0), stop=(k == DT3 - 1))
            last.then_inc(mo_ready.sem, 1)

        def gate_pe(pe, i, j, m, last_block):
            wait(pe, mo_kept, i)
            wait(pe, gcn_kept, i if last_block else i + 1)
            ops = [(wgg, xg[j]), (wgm, xmb)]
            n = 0
            for w, x in ops:
                for k in range(KT):
                    last = nc.tensor.matmul(ps[0:KP, 7 - 2 * m, :], w[:, k, m * KP:(m + 1) * KP], x[:, k, :],
                                            start=(n == 0), stop=(n == 3))
                    n += 1
            last.then_inc(gt_ready.sem, 1)

        def out_pe(pe, i, last_block):
            wait(pe, fuse, i)
            wait(pe, gt_kept, i)
            if not last_block:
                wait(pe, in_kept, i + 2)
            for t in range(TPB):
                for k in range(KT):
                    last = nc.tensor.matmul(tile_in(5, t), gate[:, k, t * P:(t + 1) * P], wout[:, k, :],
                                            start=(k == 0), stop=(k == KT - 1))
            last.then_inc(out_ready.sem, 1)

        def back_pe(pe, i, j, last):
            for m in range(KT):
                mamba_out(pe, i, j, m, last)
            for m in range(KT):
                gate_pe(pe, i, j, m, last)
            out_pe(pe, i, last)

        def bcast(pe, i, j, n, which):
            if n == 0:
                wait(pe, split, i, 5)
            ev = dbx if which == 0 else hc
            if n:
                wait(pe, ev, i, n * DT3)
            else:
                wait(pe, ev, i - 1)
            nc.tensor.matmul(ps[:, 3 + which, :], pick[:, which * NS + n, :], bc[j], start=True, stop=True)\
                .then_inc((b_ready, c_ready)[which].sem, 1)

        def body_pe(pe, i, j, front=True, back=True):
            bcast(pe, i, j, 0, 0)
            bcast(pe, i, j, 0, 1)
            for n in range(NS):
                if n + 1 < NS:
                    bcast(pe, i, j, n + 1, 0)
                if back:
                    if n in (0, 1):
                        mamba_out(pe, i - 1, 1 - j, n, False)
                    if n in (2, 3):
                        gate_pe(pe, i - 1, 1 - j, n - 2, False)
                    if n == 10:
                        out_pe(pe, i - 1, not front)
                if front:
                    if n == 4:
                        transposes_c(pe, i + 1)
                    if n in (5, 6, 7):
                        in_proj(pe, i + 1, 2 * (n - 5))
                        in_proj(pe, i + 1, 2 * (n - 5) + 1)
                    if n == 8:
                        gcn(pe, i + 1, 0, 4)
                    if n == 9:
                        gcn(pe, i + 1, 4, 8)
                    if n == 11:
                        x_proj(pe, i + 1, 1 - j)
                        gcn(pe, i + 1, 8, 12)
                    if n == 12:
                        gcn(pe, i + 1, 12, 16)
                    if n == 14:
                        gcn(pe, i + 1, 16, 22)
                    if n == 15:
                        gcn(pe, i + 1, 22, 28)
                if n + 1 < NS:
                    bcast(pe, i, j, n + 1, 1)
                for f in range(DT3):
                    wait(pe, hc, i, n * DT3 + f + 1)
                    if n == 0:
                        wait(pe, ysk, i - 1, f + 1)
                    last = nc.tensor.matmul(ps[:, f, :], ident[:, :], hs[n % 2][:, f, :],
                                            start=(n == 0), stop=(n == NS - 1))
                last.then_inc(nsum.sem, 1)
                if front and n == 12:
                    dt_proj(pe, i + 1)

        @block.tensor
        def _(pe):
            pe.wait_ge(s_const, 16 * 7)
            pe.wait_ge(s_zero, 1)
            with pe.Fori(0, NB // 2) as ii:
                for j in (0, 1):
                    i = 2 * ii + j
                    wait(pe, nrm_a, i)
                    wait(pe, xt_a, i - 2)
                    for t in range(TPB):
                        for k in range(KT):
                            last = nc.tensor.transpose(ps[0:KP, 2 * j + k, t * P:(t + 1) * P],
                                                       nrm[j][:, t, k * KP:(k + 1) * KP], ident[:, :])
                    last.then_inc(nrmT_a.sem, 1)
                    wait(pe, shifted[j], ii)
                    for t in range(TPB):
                        rows = P if t % 2 == 0 else P - 2
                        for k in range(KT):
                            m = KP + k
                            last = nc.tensor.matmul(ps[0:m, 4 + k, 0:D], nrm[j][0:rows, t, k * KP:k * KP + m],
                                                    tok2[j][0:rows, t, :], start=False, stop=False,
                                                    skip_group_check=True)
                    last.then_inc(outer_a.sem, 1)
            setup_pe(pe)
            pe.wait_ge(s_setup, nth(DVE_STEPS, "w1"))
            att_front_pe(pe, 0, None)
            with pe.Fori(0, NB - 1) as i:
                body_b_pe(pe, i)
            body_b_pe(pe, NB - 1, False)
            pe.wait_ge(s_cset, 1)
            front_pe(pe, 0, 0)
            body_pe(pe, 0, 0, back=False)
            with pe.Fori(0, NB // 2 - 1) as ii:
                for j in (1, 0):
                    body_pe(pe, 2 * ii + (1 if j else 2), j)
            body_pe(pe, NB - 1, 1, front=False)
            back_pe(pe, NB - 1, 1, last=True)
            pe.wait_ge(s_wd, 32)
            with pe.Fori(0, NB) as i:
                wait(pe, xn_d, i)
                wait(pe, dT_kept, i - 1)
                for t in range(TPB):
                    for k in range(KT):
                        last = nc.tensor.transpose(ps[0:KP, k, t * P:(t + 1) * P],
                                                   xnD[:, t, k * KP:(k + 1) * KP], ident[:, :])
                last.then_inc(dT_ready.sem, 1)
                wait(pe, dT_kept, i)
                wait(pe, gsteps, i - 1, 1)
                for t in range(TPB):
                    for k in range(KT):
                        last = nc.tensor.matmul(ps[:, 2, t * EXP:(t + 1) * EXP], xTs[:, k, t * P:(t + 1) * P],
                                                rout[:, k, :], start=(k == 0), stop=(k == KT - 1))
                last.then_inc(lg_ready.sem, 1)
            wait(pe, tokT_stored, NB - 1)
            wait(pe, gsteps, NB - 1)
            with pe.Fori(0, EXP // 2) as ee:
                for j in (0, 1):
                    wait(pe, we_loaded[j], ee)
                    e0 = (2 * ee + j) * NB
                    up_e(pe, e0, 0, j, 0)
                    with pe.Fori(0, NB // 2 - 1) as bb:
                        up_e(pe, e0 + 2 * bb + 1, 2 * bb + 1, j, 1)
                        down_e(pe, e0 + 2 * bb, j, 0)
                        up_e(pe, e0 + 2 * bb + 2, 2 * bb + 2, j, 0)
                        down_e(pe, e0 + 2 * bb + 1, j, 1)
                    up_e(pe, e0 + NB - 1, NB - 1, j, 1)
                    down_e(pe, e0 + NB - 2, j, 0)
                    down_e(pe, e0 + NB - 1, j, 1)

        def att_act(act, i, ffn=None):
            ffn = ffn or (lambda part: None)
            ffn(0)
            wait(act, t1_ready, i)
            wait(act, v_ready, i - 1)
            nc.scalar.activation(x1T, ps[0:KP, 2:4, :], ACT.Copy).then_inc(x1T_kept.sem, 1)
            ffn(1)
            wait(act, v_ready, i)
            wait(act, oT_ready, i - 1)
            nc.scalar.activation(vs, ps[:, 2, 0:TPB * KV].rearrange("p (t f) -> p t f", t=TPB), ACT.Copy)\
                .then_inc(v_kept.sem, 1)
            wait(act, oT_ready, i)
            wait(act, att_ready, i - 1)
            nc.scalar.activation(oTs, ps[0:KV, 3, :], ACT.Copy).then_inc(oT_kept.sem, 1)

        def body_b_act(act, i, more=True):
            def ffn(part):
                if part == 0:
                    wait(act, t2_ready, i)
                    wait(act, up_ready, i - 1)
                    nc.scalar.activation(x2T, ps[0:KP, 2:4, :], ACT.Copy).then_inc(x2T_kept.sem, 1)
                    wait(act, down_ready, i - 1)
                for f in range(3 * part, 3 * part + 3):
                    wait(act, up_ready, i, f + 1)
                    nc.scalar.activation(hT[:, f, :], ps[:, 6 + f % 2, :], ACT.Gelu_apprx_tanh,
                                         bias=b0[:, f:f + 1]).then_inc(gelu_kept.sem, 1)

            if more:
                att_act(act, i + 1, ffn)
            else:
                ffn(0)
                ffn(1)

        def decay(act, i, j, n):
            if n >= 2:
                wait(act, scan, i, (n - 1) * DT3)
            else:
                wait(act, scan, i - 1, (NS - 1 + n) * DT3)
            for f in range(DT3):
                if n == 0:
                    wait(act, dt_kept, i, f + 1)
                nc.scalar.activation(dA[n % 2][:, f, :, 1:SEQ],
                                     dtp[j][:, f, :].rearrange("p (s t) -> p s t", s=SPB)[:, :, 1:SEQ],
                                     ACT.Exp, scale=nega[:, f, n:n + 1]).then_inc(da_ready.sem, 1)

        def xnT_act(act, i):
            wait(act, xnT_ready, i)
            wait(act, in_ready, i - 1)
            wait(act, gcn_ready, i - 1)
            for k in range(KT):
                nc.scalar.activation(xnT[:, k, :, TAPS // 2:TAPS // 2 + SEQ],
                                     ps[0:KP, 6 + k, :].rearrange("p (s t) -> p s t", s=SPB),
                                     ACT.Identity, bias=n1b[:, k:k + 1], scale=n1w[:, k:k + 1])\
                    .then_inc(xnT_kept.sem, 1)

        def in_act(act, i, j, f):
            wait(act, in_ready, i, f + 1)
            src = ps[:, 5 + f % 2, :]
            if f < DT3:
                if f == 0:
                    wait(act, conv_ch, i - 1)
                nc.scalar.activation(xi[:, f, :, CTAPS - 1:PADC], src.rearrange("p (s t) -> p s t", s=SPB),
                                     ACT.Copy).then_inc(in_kept.sem, 1)
            else:
                if f == DT3:
                    wait(act, mo_ready, i - 2)
                nc.scalar.activation(zs[j][:, f - DT3, :], src, ACT.Copy).then_inc(in_kept.sem, 1)

        def silus_act(act, i, j):
            wait(act, conv_ch, i)
            for f in range(DT3):
                nc.scalar.activation(xm[j][:, f, :], xm[j][:, f, :], ACT.Silu).then_inc(silu_kept.sem, 1)
            for f in range(DT3):
                if f == 0:
                    wait(act, in_kept, i)
                nc.scalar.activation(zs[j][:, f, :], zs[j][:, f, :], ACT.Silu).then_inc(silu_kept.sem, 1)

        def dtl_act(act, i):
            wait(act, xp_ready, i)
            wait(act, dt_ready, i - 1)
            nc.scalar.activation(dtl[96:96 + RANK, :], ps[96:96 + RANK, 5, :], ACT.Copy).then_inc(dtl_kept.sem, 1)

        def softplus_act(act, i, f):
            wait(act, dt_ready, i, f + 1)
            wait(act, sp_max, i, f + 1)
            wait(act, out_ready, i - 2)
            s = sp1[:, f, :]
            nc.scalar.activation(s, ps[:, 6 - f % 2, :], ACT.Abs, bias=dtb[:, f:f + 1]).then_inc(sp_abs.sem, 1)
            wait(act, sp_abs, i, f + 1)
            nc.scalar.activation(s, s, ACT.Exp, scale=-1.0).then_inc(sp_exp.sem, 1)
            wait(act, sp_exp, i, f + 1)
            nc.scalar.activation(s, s, ACT.Ln, bias=1.0).then_inc(sp_log.sem, 1)

        def gcn_act(act, i, j, m):
            wait(act, gcn_ready, i, m + 1)
            wait(act, fuse, i - 2)
            nc.scalar.activation(xg[j][:, m, :], ps[0:KP, 7, :], ACT.Identity, bias=xgb[:, m:m + 1])\
                .then_inc(gcn_kept.sem, 1)

        def mo_act(act, i, m):
            wait(act, mo_ready, i, m + 1)
            wait(act, gt_ready, i - 1)
            wait(act, fuse, i - 1)
            nc.scalar.activation(xmb[:, m, :], ps[0:KP, 5 + m, :], ACT.Copy).then_inc(mo_kept.sem, 1)

        def gate_act(act, i, m, last=False):
            wait(act, gt_ready, i, m + 1)
            wait(act, dt_kept, i if last else i + 1)
            nc.scalar.activation(gate[:, m, :], ps[0:KP, 7 - 2 * m, :], ACT.Identity, bias=gateb[:, m:m + 1])\
                .then_inc(gt_kept.sem, 1)

        def tanh_act(act, i):
            wait(act, gt_kept, i)
            for m in range(KT):
                nc.scalar.activation(gate[:, m, :], gate[:, m, :], ACT.Tanh, scale=0.5).then_inc(gt_tanh.sem, 1)

        def front_act(act, i, j):
            xnT_act(act, i)
            for f in range(2 * DT3):
                in_act(act, i, j, f)
            silus_act(act, i, j)
            dtl_act(act, i)
            for f in range(DT3):
                softplus_act(act, i, f)
            for m in range(KT):
                gcn_act(act, i, j, m)

        def body_act(act, i, j, front=True, back=True):
            decay(act, i, j, 0)
            decay(act, i, j, 1)
            for n in range(NS):
                if back:
                    if n in (0, 1):
                        mo_act(act, i - 1, n)
                    if n in (2, 3):
                        gate_act(act, i - 1, n - 2)
                if front:
                    if n == 4:
                        xnT_act(act, i + 1)
                    if n in (5, 6, 7):
                        in_act(act, i + 1, 1 - j, 2 * (n - 5))
                        in_act(act, i + 1, 1 - j, 2 * (n - 5) + 1)
                if n == 9:
                    if back:
                        tanh_act(act, i - 1)
                    if front:
                        silus_act(act, i + 1, 1 - j)
                if front:
                    if n == 11:
                        dtl_act(act, i + 1)
                    if n == 12:
                        gcn_act(act, i + 1, 1 - j, 0)
                    if n in (13, 14, 15):
                        softplus_act(act, i + 1, n - 13)
                    if n == 15:
                        gcn_act(act, i + 1, 1 - j, 1)
                if n + 2 < NS:
                    decay(act, i, j, n + 2)
            if not front:
                for m in range(KT):
                    mo_act(act, i, m)
                for m in range(KT):
                    gate_act(act, i, m, last=True)
                tanh_act(act, i)

        @block.scalar
        def _(act):
            act.wait_ge(s_const, 16 * 7)
            with act.Fori(0, NB // 2) as ii:
                for j in (0, 1):
                    i = 2 * ii + j
                    wait(act, nrmT_a, i)
                    for k in range(KT):
                        last = nc.scalar.activation(XT[:, k, bass.ds(i * BT, BT)], ps[0:KP, 2 * j + k, :],
                                                    ACT.Identity, bias=lnb[:, k:k + 1], scale=lnw[:, k:k + 1])
                    last.then_inc(xt_a.sem, 1)
            act.wait_ge(s_setup_pe, nth(PE_STEPS, "x1"))
            nc.scalar.activation(X1, ps[0:KP, 0:2, :], ACT.Copy).then_inc(s_setup_act, 1)
            act.wait_ge(s_setup_pe, nth(PE_STEPS, "readout"))
            nc.scalar.activation(WoH[:, :, :].rearrange("p (a b) o -> p a (b o)", b=2), ps[0:DTR, 4:8, 0:2 * D],
                                 ACT.Copy).then_inc(s_setup_act, 1)
            act.wait_ge(s_setup_pe, nth(PE_STEPS, "g"))
            nc.scalar.activation(G[:, :, :], ps[0:KP, 0:2, 0:D], ACT.Copy).then_inc(s_setup_act, 1)
            act.wait_ge(s_setup, nth(DVE_STEPS, "negmax"))
            for q in range(2):
                nc.scalar.activation(prob[:, q, :], ps[:, 2 + q, 0:SEQ], ACT.Exp, bias=smax[:, q:q + 1],
                                     accum_out=ssum[:, q:q + 1]).then_inc(s_setup_act, 1)
            act.wait_ge(s_setup_pe, nth(PE_STEPS, "probT"))
            nc.scalar.activation(PT[:, :, :], ps[:, 4:6, 0:SEQ], ACT.Copy).then_inc(s_setup_act, 1)
            att_act(act, 0)
            with act.Fori(0, NB - 1) as i:
                body_b_act(act, i)
            body_b_act(act, NB - 1, False)
            act.wait_ge(s_wc, 16 * 12)
            nc.scalar.activation(nega[:, :, :], nega[:, :, :], ACT.Exp).then_inc(s_cact, 1)
            wait(act, hB_kept, NB - 1)
            front_act(act, 0, 0)
            body_act(act, 0, 0, back=False)
            with act.Fori(0, NB // 2 - 1) as ii:
                for j in (1, 0):
                    body_act(act, 2 * ii + (1 if j else 2), j)
            body_act(act, NB - 1, 1, front=False)
            act.wait_ge(s_wd, 32)
            with act.Fori(0, NB) as i:
                wait(act, dT_ready, i)
                wait(act, tokT_stored, i - 1)
                for k in range(KT):
                    nc.scalar.activation(xTs[:, k, :], ps[0:KP, k, :], ACT.Identity, bias=mob[:, k:k + 1],
                                         scale=mow[:, k:k + 1]).then_inc(dT_kept.sem, 1)
                wait(act, gsteps, i, 3)
                nc.scalar.activation(pr, lg, ACT.Exp).then_inc(gexp.sem, 1)
            with act.Fori(0, EXP) as e:
                with act.Fori(0, NB // 2) as bb:
                    for h in (0, 1):
                        g = e * NB + 2 * bb + h
                        wait(act, e_down, g - 2)
                        for f in range(FT):
                            wait(act, e_up, g, f + 1)
                            nc.scalar.activation(hE[h][:, f, :], ps[:, ubank(f, h), :], ACT.Silu)\
                                .then_inc(e_silu.sem, 1)

        def setup_dve(dve):
            steps = iter(DVE_STEPS)
            assert next(steps) == "ones"

            def step(name, ins):
                assert next(steps) == name
                ins.then_inc(s_setup, 1)
                dve.wait_ge(s_setup, nth(DVE_STEPS, name))

            def pe_done(name):
                dve.wait_ge(s_setup_pe, nth(PE_STEPS, name))

            wait(dve, outer_a, NB - 1)
            step("sum_row", V.tensor_copy(srow[KP:KP + 1, :], ps[KP:KP + 1, 5, 0:D]))
            step("alpha", V.tensor_tensor(wa, wa2[:, 0:1], wa2[:, 1:2], ALU.mult))
            dve.wait_ge(s_wa, 16 * SETUP_DMAS)
            step("scaled_mask", V.tensor_scalar(mins, minp, wa, None, ALU.mult))
            pe_done("bias_outer")
            for k in range(KT):
                step(f"m{k}w", V.tensor_scalar(MS[:, k, :], ps[0:KP, 4 + k, 0:D], lnw[:, k:k + 1], None, ALU.mult))
                step(f"m{k}", V.tensor_tensor(MS[:, k, :], MS[:, k, :], ps[0:KP, 6, k * D:(k + 1) * D], ALU.add))
            step("decayed", V.tensor_scalar(tr, tr, TRACE_DECAY, None, ALU.mult))
            pe_done("update")
            trf = tr.rearrange("p h q -> p (h q)")
            step("trace", V.scalar_tensor_tensor(out=trf, in0=ps[0:DTR, 2, :],
                                                 scalar=TRACE_LR / (BATCH * (SEQ - 2)), in1=trf,
                                                 op0=ALU.mult, op1=ALU.add))
            pe_done("scores")
            step("max", V.tensor_reduce(smax, ps[:, 2:4, 0:SEQ], AX.X, ALU.max))
            step("negmax", V.tensor_scalar(smax, smax, -1.0, None, ALU.mult))
            dve.wait_ge(s_setup_act, nth(ACT_STEPS, "exp1"))
            step("recip", V.reciprocal(ssum, ssum))
            for q in range(2):
                step(f"prob{q}", V.tensor_scalar(prob[:, q, :], prob[:, q, :], ssum[:, q:q + 1], None, ALU.mult))
            pe_done("b1")
            step("b0", V.tensor_tensor(b0, bfc, ps[:, 6, 0:FT], ALU.mult))
            step("b1", V.tensor_tensor(b1row[:, :], b1row[:, :], ps[0:1, 7, 0:D], ALU.mult))
            pe_done("c0")
            w0v = w0.rearrange("p k (n f) -> p (k n) f", n=2)
            step("w0", V.tensor_tensor(w0v, w0v, ps[0:KP, 0:4, 0:FF // 2], ALU.mult))
            pe_done("c1")
            w1v = w1.rearrange("p (a b) e -> p a (b e)", b=2)
            step("w1", V.tensor_tensor(w1v, w1v, ps[:, 0:3, 0:2 * D], ALU.mult))

        def norm_b(dve, i, q, src, dst, dst_free, done):
            for t in range(TPB):
                last = V.bn_stats(stB[:, t, :], src[:, t, :])
            last.then_inc(st_b.sem, 1)
            wait_alone(dve, st_b, i, q)
            for t in range(TPB):
                last = V.bn_aggr(mvB[:, t, :], stB[:, t, :])
            last.then_inc(mv_b.sem, 1)
            wait(dve, mv_b, i, q)
            V.tensor_scalar(veB, mvB[:, :, 1], EPS, None, ALU.add).then_inc(ve_b.sem, 1)
            wait(dve, rs_b, i, q)
            wait(dve, dst_free, i - 1)
            for t in range(TPB):
                last = V.tensor_scalar(dst[:, t, :], src[:, t, :], mvB[:, t, 0:1], rsB[:, t:t + 1],
                                       ALU.subtract, ALU.mult)
            last.then_inc(done.sem, 1)

        def att_dve(dve, i, resid=None):
            wait(dve, h0_ready, i)
            V.tensor_copy(h0c.rearrange("p (a b) f -> p a (b f)", b=2), tiles_of(0)).then_inc(h0_kept.sem, 1)
            wait(dve, h0_kept, i)
            norm_b(dve, i, 1, h0c, xn1, t1_ready, xn1_kept)
            if resid:
                resid()
            wait(dve, hB_kept, i - 1)
            wait(dve, att_ready, i)
            V.tensor_tensor(hA.rearrange("p (a b) f -> p a (b f)", b=2), h0c.rearrange("p (a b) f -> p a (b f)", b=2),
                            tiles_of(0), ALU.add).then_inc(hA_kept.sem, 1)
            wait(dve, hA_kept, i)
            norm_b(dve, i, 2, hA, xn2, t2_ready, xn2_kept)

        def body_b_dve(dve, i, more=True):
            def resid():
                wait(dve, down_ready, i)
                V.tensor_tensor(H[:, bass.ds(i * TPB, TPB), :].rearrange("p (a b) f -> p a (b f)", b=2),
                                hA.rearrange("p (a b) f -> p a (b f)", b=2), tiles_of(4), ALU.add)\
                    .then_inc(hB_kept.sem, 1)

            if more:
                att_dve(dve, i + 1, resid)
            else:
                resid()

        def norm_c(dve, i, j):
            Hi = lambda t: H[:, bass.ds(i * TPB + t, 1), :].rearrange("p t f -> p (t f)")
            if isinstance(i, int) and i == 0:
                wait(dve, hB_kept, NB - 1)
            for t in range(TPB):
                last = V.bn_stats(stC[:, t, :], Hi(t))
            last.then_inc(st_c.sem, 1)
            wait_alone(dve, st_c, i)
            for t in range(TPB):
                last = V.bn_aggr(mvC[j][:, t, :], stC[:, t, :])
            last.then_inc(mv_c.sem, 1)
            wait(dve, mv_c, i)
            wait(dve, rs_c, i - 1)
            V.tensor_scalar(pvC[:, 0, :], mvC[j][:, :, 1], EPS, None, ALU.add)
            V.tensor_scalar(pvC[:, 1, :], mvC[j][:, :, 1], 1.0 + EPS, EPS * EPS, ALU.mult, ALU.add)\
                .then_inc(pv_c.sem, 1)

        def xn_dve(dve, i, j):
            wait(dve, rs_c, i)
            wait(dve, xnT_ready, i - 1)
            wait(dve, tail_o, i - 3)
            for t in range(TPB):
                last = V.tensor_scalar(xnC[:, t, :], H[:, bass.ds(i * TPB + t, 1), :].rearrange("p t f -> p (t f)"),
                                       mvC[j][:, t, 0:1], rsC[j][:, 1, t:t + 1], ALU.subtract, ALU.mult)
            last.then_inc(xn_c.sem, 1)

        def conv_dve(dve, i, j, f):
            wait(dve, in_kept, i, f + 1)
            x3 = xm[j][:, f, :].rearrange("p (s t) -> p s t", s=SPB)
            for tap in range(CTAPS):
                src = xi[:, f, :, tap:tap + SEQ]
                if tap == 0:
                    ins = V.tensor_scalar(x3, src, cw[:, f, 0:1], cb[:, f:f + 1], ALU.mult, ALU.add)
                else:
                    wait(dve, conv_ch, i, f * CTAPS + tap)
                    ins = V.scalar_tensor_tensor(out=x3, in0=src, scalar=cw[:, f, tap:tap + 1], in1=x3,
                                                 op0=ALU.mult, op1=ALU.add)
                ins.then_inc(conv_ch.sem, 1)

        def split_dve(dve, i, j):
            wait(dve, xp_ready, i)
            src = ps[0:96, 5, :]
            bcp = bc[j]
            V.tensor_copy(bcp, src).then_inc(split.sem, 1)
            wait(dve, split, i, 1)
            V.tensor_tensor(rest, src, bcp, ALU.subtract).then_inc(split.sem, 1)
            wait(dve, split, i, 2)
            V.tensor_copy(mid, rest).then_inc(split.sem, 1)
            wait(dve, split, i, 3)
            V.tensor_copy(bcp[32:64, :], mid[32:64, :]).then_inc(split.sem, 1)
            V.tensor_tensor(bcp[64:96, :], rest[64:96, :], mid[64:96, :], ALU.subtract).then_inc(split.sem, 1)

        def softplus_max_dve(dve, i, j, f):
            wait(dve, dt_ready, i, f + 1)
            V.tensor_scalar(dtp[j][:, f, :], ps[:, 6 - f % 2, :], dtb[:, f:f + 1], 0.0, ALU.add, ALU.max)\
                .then_inc(sp_max.sem, 1)

        def softplus_dve(dve, i, j, f):
            wait(dve, sp_max, i, f + 1)
            wait(dve, sp_log, i, f + 1)
            V.tensor_tensor(dtp[j][:, f, :], dtp[j][:, f, :], sp1[:, f, :], ALU.add).then_inc(dt_kept.sem, 1)
            wait(dve, dt_kept, i, f + 1)
            wait(dve, silu_kept, i, f + 1)
            V.tensor_tensor(up_[j][:, f, :], dtp[j][:, f, :], xm[j][:, f, :], ALU.mult).then_inc(u_kept.sem, 1)

        def front_dve(dve, i, j):
            norm_c(dve, i, j)
            xn_dve(dve, i, j)
            for f in range(DT3):
                conv_dve(dve, i, j, f)
            split_dve(dve, i, j)
            for f in range(DT3):
                softplus_max_dve(dve, i, j, f)
                softplus_dve(dve, i, j, f)

        def fuse_dve(dve, i, j):
            wait(dve, gt_tanh, i)
            wait(dve, gcn_kept, i)
            V.tensor_tensor(xg[j], xg[j], xmb, ALU.subtract).then_inc(fuse.sem, 1)
            wait(dve, fuse, i, 1)
            V.scalar_tensor_tensor(out=xg[j], in0=gate, scalar=1.0, in1=xg[j], op0=ALU.add, op1=ALU.mult)\
                .then_inc(fuse.sem, 1)
            wait(dve, fuse, i, 2)
            V.scalar_tensor_tensor(out=gate, in0=xg[j], scalar=0.5, in1=xmb, op0=ALU.mult, op1=ALU.add)\
                .then_inc(fuse.sem, 1)

        def xr_dve(dve, i, j):
            wait(dve, o_kept, i - 1, 3)
            for t in range(TPB):
                last = V.tensor_scalar(xr[:, t, :], H[:, bass.ds(i * TPB + t, 1), :].rearrange("p t f -> p (t f)"),
                                       mvC[j][:, t, 0:1], rsC[j][:, 0, t:t + 1], ALU.subtract, ALU.mult)
            last.then_inc(o_kept.sem, 1)
            wait(dve, o_kept, i, 1)
            V.tensor_tensor(xr, xr, outb.unsqueeze(1).broadcast_to([P, TPB, D]), ALU.add)\
                .then_inc(o_kept.sem, 1)

        def out_dve(dve, i, last=False):
            wait(dve, xnT_ready, i if last else i + 2)
            wait(dve, out_ready, i)
            wait(dve, o_kept, i, 2)
            wait(dve, tail_o, i - 1)
            V.tensor_tensor(o.rearrange("p (a b) f -> p a (b f)", b=2), xr.rearrange("p (a b) f -> p a (b f)", b=2),
                            tiles_of(5), ALU.add).then_inc(o_kept.sem, 1)
            wait(dve, o_kept, i, 3)
            for t in range(TPB):
                last = V.bn_stats(stO[:, t, :], o[:, t, :])
            last.then_inc(st_o.sem, 1)
            wait_alone(dve, st_o, i)
            for t in range(TPB):
                last = V.bn_aggr(mvO[:, t, :], stO[:, t, :])
            last.then_inc(mv_o.sem, 1)
            wait(dve, mv_o, i)
            V.tensor_scalar(veO, mvO[:, :, 1], EPS, None, ALU.add).then_inc(ve_o.sem, 1)

        def onorm_dve(dve, i):
            wait(dve, rs_o, i)
            for t in range(TPB):
                last = V.tensor_scalar(o[:, t, :], o[:, t, :], mvO[:, t, 0:1], rsO[:, t:t + 1],
                                       ALU.subtract, ALU.mult)
            last.then_inc(on_o.sem, 1)

        def body_dve(dve, i, j, front=True, back=True):
            for n in range(NS):
                buf = hs[n % 2]
                for f in range(DT3):
                    if n == 0:
                        wait(dve, u_kept, i, f + 1)
                    if f == 0:
                        wait(dve, b_ready, i, n + 1)
                        if n >= 2:
                            wait(dve, nsum, i, n - 1)
                        else:
                            wait(dve, nsum, i - 1, NS - 1 + n)
                    V.tensor_tensor(buf[:, f, :], up_[j][:, f, :], ps[:, 3, :], ALU.mult).then_inc(dbx.sem, 1)
                for f in range(DT3):
                    c = n * DT3 + f + 1
                    wait(dve, dbx, i, c)
                    wait(dve, da_ready, i, c)
                    V.tensor_tensor_scan(out=buf[:, f, :], data0=dA[n % 2][:, f, :, :].rearrange("p s t -> p (s t)"),
                                         data1=buf[:, f, :], initial=0.0, op0=ALU.mult, op1=ALU.add)\
                        .then_inc(scan.sem, 1)
                for f in range(DT3):
                    c = n * DT3 + f + 1
                    wait(dve, scan, i, c)
                    if f == 0:
                        wait(dve, c_ready, i, n + 1)
                    V.tensor_tensor(buf[:, f, :], buf[:, f, :], ps[:, 4, :], ALU.mult).then_inc(hc.sem, 1)
                if back and n == 0:
                    xr_dve(dve, i - 1, 1 - j)
                if front:
                    if n == 0:
                        norm_c(dve, i + 1, 1 - j)
                    if n == 2:
                        xn_dve(dve, i + 1, 1 - j)
                    if n in (6, 7, 8):
                        conv_dve(dve, i + 1, 1 - j, n - 6)
                if back:
                    if n == 9:
                        fuse_dve(dve, i - 1, 1 - j)
                    if n == 10:
                        out_dve(dve, i - 1, last=not front)
                    if n == 12:
                        onorm_dve(dve, i - 1)
                if front:
                    if n == 11:
                        split_dve(dve, i + 1, 1 - j)
                    if n == 13:
                        softplus_max_dve(dve, i + 1, 1 - j, 0)
                        softplus_max_dve(dve, i + 1, 1 - j, 1)
                    if n == 14:
                        softplus_max_dve(dve, i + 1, 1 - j, 2)
                    if n == 15:
                        softplus_dve(dve, i + 1, 1 - j, 0)
            if front:
                softplus_dve(dve, i + 1, 1 - j, 1)
                softplus_dve(dve, i + 1, 1 - j, 2)
            wait(dve, nsum, i)
            for f in range(DT3):
                V.scalar_tensor_tensor(out=xm[j][:, f, :], in0=xm[j][:, f, :], scalar=dskip[:, f:f + 1],
                                       in1=ps[:, f, :], op0=ALU.mult, op1=ALU.add).then_inc(ysk.sem, 1)
            for f in range(DT3):
                wait(dve, ysk, i, f + 1)
                V.tensor_tensor(zs[j][:, f, :], xm[j][:, f, :], zs[j][:, f, :], ALU.mult).then_inc(yz.sem, 1)

        def gating_dve(dve, i):
            n = [0]

            def step(ins):
                n[0] += 1
                ins.then_inc(gsteps.sem, 1)
                wait(dve, gsteps, i, n[0])

            Hi = H[:, bass.ds(i * TPB, TPB), :]
            for t in range(TPB):
                last = V.bn_stats(stD[:, t, :], H[:, bass.ds(i * TPB + t, 1), :].rearrange("p t f -> p (t f)"))
            last.then_inc(st_d.sem, 1)
            wait_alone(dve, st_d, i)
            for t in range(TPB):
                last = V.bn_aggr(mvD[:, t, :], stD[:, t, :])
            last.then_inc(mv_d.sem, 1)
            wait(dve, mv_d, i)
            V.tensor_scalar(pvD[:, 0, :], mvD[:, :, 1], EPS, None, ALU.add)
            V.tensor_scalar(pvD[:, 1, :], mvD[:, :, 1], 1.0 + EPS, EPS * EPS, ALU.mult, ALU.add)\
                .then_inc(pv_d.sem, 1)
            wait(dve, rs_d, i)
            wait(dve, dT_ready, i - 1)
            for t in range(TPB):
                last = V.tensor_scalar(xnD[:, t, :], H[:, bass.ds(i * TPB + t, 1), :].rearrange("p t f -> p (t f)"),
                                       mvD[:, t, 0:1], rsD[:, 1, t:t + 1], ALU.subtract, ALU.mult)
            last.then_inc(xn_d.sem, 1)
            for t in range(TPB):
                V.tensor_scalar(xrD[:, t, :], H[:, bass.ds(i * TPB + t, 1), :].rearrange("p t f -> p (t f)"),
                                mvD[:, t, 0:1], rsD[:, 0, t:t + 1], ALU.subtract, ALU.mult).then_inc(res_d.sem, 1)
            wait(dve, res_d, i, TPB)
            V.tensor_tensor(Hi, Hi, xrD, ALU.add).then_inc(res_d.sem, 1)
            wait(dve, lg_ready, i)
            step(V.tensor_copy(lg, ps[:, 2, 0:TPB * EXP].rearrange("p (t e) -> p t e", t=TPB)))
            step(V.tensor_reduce(lmax, lg, AX.X, ALU.max))
            step(V.tensor_tensor(lg, lg, lmax.unsqueeze(2).broadcast_to([P, TPB, EXP]), ALU.subtract))
            wait(dve, gexp, i)
            step(V.tensor_reduce(psm, pr, AX.X, ALU.add))
            step(V.reciprocal(psm, psm))
            step(V.tensor_tensor(pr, pr, psm.unsqueeze(2).broadcast_to([P, TPB, EXP]), ALU.mult))
            pe_ = pr.unsqueeze(3).broadcast_to([P, TPB, EXP, EXP])
            pj_ = pr.unsqueeze(2).broadcast_to([P, TPB, EXP, EXP])
            step(V.tensor_tensor(cmp1, pj_, pe_, ALU.is_gt))
            step(V.tensor_tensor(cmp2, pj_, pe_, ALU.is_equal))
            step(V.tensor_tensor(cmp2, cmp2, tri.unsqueeze(1).broadcast_to([P, TPB, EXP, EXP]), ALU.mult))
            step(V.tensor_tensor(cmp1, cmp1, cmp2, ALU.add))
            step(V.tensor_reduce(rank, cmp1, AX.X, ALU.add))
            step(V.scalar_tensor_tensor(out=pr, in0=rank, scalar=TOPK - 0.5, in1=pr, op0=ALU.is_lt, op1=ALU.mult))
            step(V.tensor_reduce(psm, pr, AX.X, ALU.add))
            step(V.reciprocal(psm, psm))
            step(V.tensor_tensor(gates[:, bass.ds(i * TPB, TPB), :], pr,
                                 psm.unsqueeze(2).broadcast_to([P, TPB, EXP]), ALU.mult))
            assert n[0] == NG

        @block.vector
        def _(dve):
            V.memset(ones[:, :], 1.0).then_inc(s_setup, 1)
            for j in (0, 1):
                V.memset(nrm[j][:, :, D:D + 1], 1.0)
            V.memset(ps[:, 4:6, 0:D], 0.0).then_inc(s_zero, 1)
            dve.wait_ge(s_const, 16 * 7)
            with dve.Fori(0, NB // 2) as ii:
                for j in (0, 1):
                    i = 2 * ii + j
                    wait(dve, tok_loaded[j], ii)
                    for t in range(TPB):
                        last = V.bn_stats(stA[:, t, :], tok[j][:, t, :])
                    last.then_inc(stats_a.sem, 1)
                    wait_alone(dve, stats_a, i)
                    for t in range(TPB):
                        last = V.bn_aggr(mvA[:, t, :], stA[:, t, :])
                    last.then_inc(mv_a.sem, 1)
                    wait(dve, mv_a, i)
                    wait(dve, rstd_a, i - 1)
                    V.tensor_scalar(veA, mvA[:, :, 1], EPS, None, ALU.add).then_inc(var_a.sem, 1)
                    wait(dve, rstd_a, i)
                    wait(dve, outer_a, i - 2)
                    wait(dve, nrmT_a, i - 2)
                    for t in range(TPB):
                        last = V.tensor_scalar(nrm[j][:, t, 0:D], tok[j][:, t, :], mvA[:, t, 0:1],
                                               rsA[j][:, t:t + 1], ALU.subtract, ALU.mult)
                    last.then_inc(nrm_a.sem, 1)
            setup_dve(dve)
            att_dve(dve, 0)
            with dve.Fori(0, NB - 1) as i:
                body_b_dve(dve, i)
            body_b_dve(dve, NB - 1, False)
            dve.wait_ge(s_wc2, 16 * 4)
            dve.wait_ge(s_wc, 16 * 12)
            for buf in dA:
                V.memset(buf[:, :, :, 0:1], 0.0)
            V.memset(xnT[:, :, :, 0:TAPS // 2], 0.0)
            V.memset(xnT[:, :, :, TAPS // 2 + SEQ:PADX], 0.0)
            V.memset(xi[:, :, :, 0:CTAPS - 1], 0.0)
            V.tensor_tensor(wconv[:, :, TAPS // 2, :], wconv[:, :, TAPS // 2, :], wgcn, ALU.add)
            V.tensor_tensor(xgb, gcb, cvb, ALU.add)
            V.tensor_tensor(gateb, ggb, gmb, ALU.add)
            V.tensor_copy(pick[:, :, :], pick32[:, :].unsqueeze(2).broadcast_to([KP, 32, P]))
            dve.wait_ge(s_cact, 1)
            V.tensor_scalar(nega[:, :, :], nega[:, :, :], -1.0, None, ALU.mult).then_inc(s_cset, 1)
            front_dve(dve, 0, 0)
            body_dve(dve, 0, 0, back=False)
            with dve.Fori(0, NB // 2 - 1) as ii:
                for j in (1, 0):
                    body_dve(dve, 2 * ii + (1 if j else 2), j)
            body_dve(dve, NB - 1, 1, front=False)
            xr_dve(dve, NB - 1, 1)
            fuse_dve(dve, NB - 1, 1)
            out_dve(dve, NB - 1, last=True)
            onorm_dve(dve, NB - 1)
            wait(dve, tail_o, NB - 1)
            dve.wait_ge(s_wd, 32)
            with dve.Fori(0, NB) as i:
                gating_dve(dve, i)
            with dve.Fori(0, EXP) as e:
                with dve.Fori(0, NB // 2) as bb:
                    for h in (0, 1):
                        b = 2 * bb + h
                        wait(dve, e_down, e * NB + b)
                        wait(dve, e_acc, e * NB + b - 1)
                        for t in range(TPB):
                            Ht = H[:, bass.ds(b * TPB + t, 1), :].rearrange("p t f -> p (t f)")
                            gt = gates[:, :, :].rearrange("p t e -> p (t e)")[:, bass.ds((b * TPB + t) * EXP + e, 1)]
                            V.scalar_tensor_tensor(out=Ht, in0=tile_in(4 + 2 * h, t), scalar=gt, in1=Ht,
                                                   op0=ALU.mult, op1=ALU.add).then_inc(e_acc.sem, 1)



def kernel(**inputs):
    import numpy as np
    import concourse.bacc as bacc
    from concourse.bass_utils import run_bass_kernel_spmd

    a = {k: np.asarray(v) for k, v in inputs.items()}

    def halves(w, tail):
        return w.reshape(KT, KP, *tail).swapaxes(0, 1)

    def tiles(w, n, tail):
        return w.reshape(n, P, *tail).swapaxes(0, 1)

    col = lambda v: v.reshape(KT, KP).T
    ch = lambda v: v.reshape(DT3, P).T
    freqs = 10000.0 ** (-np.arange(0, D, 2, dtype=np.float32) / np.float32(D))
    ang = np.arange(SEQ, dtype=np.float32)[:, None] * freqs[None].astype(np.float32)
    rope = np.concatenate([np.sin(ang), np.cos(ang)], axis=-1).astype(np.float32)
    widths, ratios = (96, 144, 192), (2, 3, 4)
    mask_in = np.array([[float(x < w) for x in range(D)] for w in widths for _ in ratios], np.float32)
    mask_out = np.array([[float(x < w * r) for x in range(FF)] for w in widths for r in ratios], np.float32)
    heads = lambda w: w.reshape(HEADS, DTR, -1).swapaxes(0, 1)
    xp = a["L1_attn_m_xproj_w"]
    bcw = xp[:, RANK:]
    ae, ar = a["L0_ffn_alpha_e"], a["L0_ffn_alpha_r"]
    arrays = {
        "ids": a["x"].reshape(NT, P).T,
        "wte": a["L0_tok_wte"],
        "ident": np.eye(P, dtype=np.float32),
        "mhalf": np.full((P, 8), -0.5, np.float32),
        "va_fm": np.concatenate([col(a[k]) for k in ("L0_tok_ln_w", "L0_tok_ln_b", "L1_ffn_ln_gamma",
                                                     "L1_ffn_ln_beta")], axis=1),
        "b_fc": a["L0_ffn_b_fc"].reshape(FT, P).T,
        "alphas": np.stack([np.broadcast_to(ae[:, None], (3, 3)).reshape(9),
                            np.broadcast_to(ar[None], (3, 3)).reshape(9)], axis=1),
        "ln_b_row": a["L0_tok_ln_b"].reshape(1, D),
        "b_proj_row": a["L0_ffn_b_proj"].reshape(1, D),
        "WpT": halves(a["L0_tok_W_proj"].T, (HD,)),
        "WvT": halves(a["L0_tok_W_val"].T, (HD,)),
        "WpH": heads(a["L0_tok_W_proj"]),
        "WoH": heads(a["L0_tok_W_out"].T),
        "traceT": a["L0_tok_trace0"].transpose(2, 0, 1),
        "mask_in": mask_in,
        "mask_out": mask_out,
        "rope": halves(rope.T, (SEQ,)),
        "W0T": halves(a["L0_ffn_w_fc"].T, (FF,)),
        "W1T": tiles(a["L0_ffn_w_proj"].T, FT, (D,)),
        "Wv": halves(a["L0_attn_Wv"].T, (KV,)),
        "Wo": a["L0_attn_Wo"].T,
        "wconv": a["L1_attn_conv_w"].transpose(1, 2, 0).reshape(KT, KP, TAPS, D).swapaxes(0, 1),
        "wgcn": halves(a["L1_attn_gcn_w"], (D,)),
        "win": halves(a["L1_attn_m_in_w"], (2 * DI,)),
        "wxp": tiles(np.concatenate([bcw, bcw, bcw, xp[:, :RANK]], axis=1), DT3, (3 * 32 + RANK,)),
        "wdt": a["L1_attn_m_dt_w"],
        "wmo": tiles(a["L1_attn_m_out_w"], DT3, (D,)),
        "wgg": halves(a["L1_attn_gate_gcn_w"], (D,)),
        "wgm": halves(a["L1_attn_gate_mamba_w"], (D,)),
        "wout": halves(a["L1_attn_out_w"], (D,)),
        "pick": np.tile(np.eye(32, dtype=np.float32), (3, 1)),
        "vc_fm": np.concatenate([col(a["L1_attn_" + k]) for k in (
            "norm1_w", "norm1_b", "gcn_b", "conv_b", "gate_gcn_b", "gate_mamba_b")], axis=1),
        "vc_ch": np.concatenate([a["L1_attn_m_conv_w"].reshape(DT3, P, CTAPS).swapaxes(0, 1).reshape(P, -1),
                                 ch(a["L1_attn_m_conv_b"]), ch(a["L1_attn_m_dt_b"]), ch(a["L1_attn_m_D"])], axis=1),
        "A_log": tiles(a["L1_attn_m_A_log"], DT3, (NS,)),
        "n2w": a["L1_attn_norm2_w"],
        "n2b": a["L1_attn_norm2_b"],
        "outb": a["L1_attn_out_b"],
        "router": halves(a["L1_ffn_router_w"], (EXP,)),
        "tri": np.broadcast_to(np.tril(np.ones((EXP, EXP), np.float32), -1), (P, EXP, EXP)),
        "w1": a["L1_ffn_w1"].reshape(EXP, KT, KP, FF).swapaxes(1, 2).reshape(EXP * KP, KT * FF),
        "w2": a["L1_ffn_w2"].reshape(EXP, FT, P, D).swapaxes(1, 2).reshape(EXP * P, FT * D),
    }
    nc = bacc.Bacc("TRN2", target_bir_lowering=False, num_devices=1)
    arrays = {k + "_dram": np.ascontiguousarray(v) for k, v in arrays.items()}
    aps = {k[:-5]: nc.dram_tensor(k, v.shape, mybir.dt.from_np(v.dtype), kind="ExternalInput").ap()
           for k, v in arrays.items()}
    out = nc.dram_tensor("out_dram", (T, D), F32, kind="ExternalOutput").ap()
    build(nc, aps, out)
    r = run_bass_kernel_spmd(nc, [arrays], core_ids=[0])
    return r.results[0]["out_dram"].reshape(BATCH, SEQ, D)
```

```python
import concourse.bass as bass
from concourse import mybir
from contextlib import ExitStack

F32 = mybir.dt.float32
BF16 = mybir.dt.bfloat16
I32 = mybir.dt.int32
ACT = mybir.ActivationFunctionType
ALU = mybir.AluOpType
AX = mybir.AxisListType

BATCH, SEQ, D = 32, 256, 192
T = BATCH * SEQ
P = 128
NT = T // P
TPB = 4
BT = TPB * P
NB = T // BT
SETUP_DMAS = 12
SPB = BT // SEQ
KP, KT = 96, 2
HEADS, DTR = 8, 64
HD = HEADS * DTR
KV = 64
FF = 768
FT = FF // P
DI = 384
DT3 = DI // P
NS = 16
RANK = 12
TAPS, CTAPS = 7, 4
EXP, TOPK = 8, 2
CAP = T + P
NSB = (TOPK * T + EXP * (P - 1)) // P
NSB += -NSB % 4
RING = 4
ROW = D + 2
EPS = 1e-5
TRACE_LR, TRACE_DECAY = 0.1, 0.99
CREDIT = 3

PE_STEPS = ["bias_outer", "x1", "update", "readout", "g", "scores", "probT", "b0", "b1", "c0", "c1"]
ACT_STEPS = ["x1", "readout", "g", "exp0", "exp1", "probT"]
DVE_STEPS = ["ones", "sum_row", "alpha", "scaled_mask", "m0w", "m0", "m1w", "m1", "decayed", "trace", "max",
             "negmax", "recip", "prob0", "prob1", "b0", "b1", "w0", "w1"]


def nth(steps, name):
    return steps.index(name) + 1


class Event:

    def __init__(self, sem, per, ahead=CREDIT):
        self.sem, self.per, self.ahead = sem, per, ahead

    def at(self, block, nth=None):
        return (block + self.ahead) * self.per + (self.per if nth is None else nth)


def build(nc, d, out):
    ctx = ExitStack()
    with ctx:
        def sb(name, shape, dt=F32):
            return ctx.enter_context(nc.sbuf_tensor(name, shape, dt))

        def sem(name):
            return ctx.enter_context(nc.semaphore(name))

        events = []

        def event(name, per=1, ahead=CREDIT):
            e = Event(sem(name), per, ahead)
            events.append(e)
            return e

        H = sb("H", [P, NT, D])
        ARENA = 31840
        arena = sb("arena", [P, ARENA])
        top = [0]

        def carve(p, *shape, dt=F32):
            n = 1
            for s in shape:
                n *= s
            words = (n + 1) // 2 if dt == BF16 else n
            at = top[0]
            top[0] += (words + 3) // 4 * 4
            assert top[0] <= ARENA, top[0]
            v = arena[0:p, at:at + words]
            if dt != F32:
                v = v.bitcast(dt)
            if len(shape) == 1:
                return v
            names = "abcd"[:len(shape)]
            kw = {names[q]: shape[q] for q in range(1, len(shape))}
            return v.rearrange(f"p ({' '.join(names)}) -> p {' '.join(names)}", **kw)

        ident = sb("ident", [P, P])
        ps = ctx.enter_context(nc.psum_tensor("ps", [P, 8, 512], F32))

        def tiles_of(bank):
            return ps[:, bank:bank + 2, 0:2 * D]

        def tile_in(bank, t):
            return ps[:, bank + t // 2, (t % 2) * D:(t % 2 + 1) * D]

        exps_half = sb("exps_half", [P, 8])

        wconv = sb("wconv", [KP, KT, TAPS, D])
        win = sb("win", [KP, KT, 2 * DI])
        wxp = sb("wxp", [P, DT3, 3 * 32 + RANK])
        wdt = sb("wdt", [P, DI])
        wmo = sb("wmo", [P, DT3, D])
        wgg = sb("wgg", [KP, KT, D])
        wgm = sb("wgm", [KP, KT, D])
        wout = sb("wout", [KP, KT, D])
        pick32 = sb("pick32", [KP, 32])
        vc = sb("vc", [P, 80])
        n1w, n1b = vc[0:KP, 0:2], vc[0:KP, 2:4]
        gcb, cvb = vc[0:KP, 4:6], vc[0:KP, 6:8]
        ggb, gmb = vc[0:KP, 8:10], vc[0:KP, 10:12]
        cw = vc[:, 12:24].rearrange("p (a b) -> p a b", b=CTAPS)
        cb, dtb, dskip = vc[:, 24:27], vc[:, 27:30], vc[:, 30:33]
        xgb, gateb = vc[0:KP, 34:36], vc[0:KP, 36:38]
        nega = sb("nega", [P, DT3, NS])
        va = sb("va", [P, 40])
        lnw, lnb = va[0:KP, 0:2], va[0:KP, 2:4]
        mow, mob = va[0:KP, 4:6], va[0:KP, 6:8]
        bfc, b0 = va[:, 8:14], va[:, 14:20]
        wa2, wa = va[0:9, 20:22], va[0:9, 22:23]
        lnbrow = sb("lnbrow", [KP + 1, D])
        b1row = sb("b1row", [1, D])
        ones = sb("ones", [1, P])

        s_const = sem("constants_loaded")
        s_wc = sem("phase_c_weights_loaded")
        s_wc2 = sem("phase_c_late_weights_loaded")
        s_wa = sem("setup_weights_loaded")
        s_ids = sem("ids_loaded")
        tok_loaded = [event(f"tok{j}_gathered", 4 * 16, ahead=0) for j in range(2)]
        shifted = [event(f"tok{j}_shifted", 2 * 16) for j in range(2)]
        s_alone = sem("waits_alone")
        s_zero = sem("outer_banks_zero")
        s_setup = sem("setup_steps_vector")
        s_setup_pe = sem("setup_steps_tensor")
        s_setup_act = sem("setup_steps_scalar")
        s_setup_gp = sem("xs_zero_column")

        top[0] = 0
        XT = carve(KP, KT, T)
        w0 = carve(KP, KT, FF)
        w1 = carve(P, FT, D)
        base_b = top[0]
        ids = carve(P, NT, dt=I32)
        tok = [carve(P, TPB, D) for _ in range(2)]
        tok2 = [carve(P, TPB, D) for _ in range(2)]
        nrm = [carve(P, TPB, D + 1) for _ in range(2)]
        stA = carve(P, TPB, 6)
        mvA = carve(P, TPB, 2)
        veA = carve(P, TPB)
        rsA = [carve(P, TPB) for _ in range(2)]
        WpT = carve(KP, KT, HD)
        WvT = carve(KP, KT, HD)
        WpH = carve(DTR, HEADS, D)
        WoH = carve(DTR, HEADS, D)
        tr = carve(DTR, HEADS, DTR)
        MS = carve(KP, KT, D)
        srow = carve(KP + 1, D)
        X1 = WpT
        minp = carve(9, D)
        mins = carve(9, D)
        mout = carve(9, FF)
        rope = carve(KP, KT, SEQ)
        smax = carve(P, 2)
        ssum = carve(P, 2)
        prob = tok[0].rearrange("p a b -> p (a b)")[:, 0:2 * SEQ].rearrange("p (q k) -> p q k", q=2)

        idn = [sb(f"idn{j}", [P, TPB], I32)[:, :] for j in range(2)]
        ids_staged = [event(f"ids_staged{j}") for j in range(2)]
        stats_a = event("stats_a")
        mv_a = event("mean_var_a")
        var_a = event("variance_a")
        rstd_a = event("rstd_a")
        nrm_a = event("normed_a")
        nrmT_a = event("transposed_a")
        xt_a = event("xt_stored_a")
        outer_a = event("outer_product_a")

        G = sb("G", [KP, KT, D])
        PT = sb("PT", [P, 2, SEQ])
        wv = sb("wv", [KP, KT, KV])
        wo = sb("wo", [KV, D])
        top[0] = base_b
        xs = carve(KP, KT, SPB, SEQ)
        h0c = carve(P, TPB, D)
        hA = carve(P, TPB, D)
        xn1 = carve(P, TPB, D)
        xn2 = carve(P, TPB, D)
        x1T = carve(KP, KT, BT)
        x2T = carve(KP, KT, BT)
        vs = carve(P, TPB, KV)
        oTs = carve(KV, BT)
        hT = carve(P, FT, BT)
        stB = carve(P, TPB, 6)
        mvB = carve(P, TPB, 2)
        veB = carve(P, TPB)
        rsB = carve(P, TPB)

        xs_loaded = event("xs_loaded", 16 * KT)
        h0_ready = event("h0_ready")
        h0_kept = event("h0_kept")
        t1_ready = event("t1_ready")
        x1T_kept = event("x1T_kept")
        v_ready = event("v_ready")
        v_kept = event("v_kept")
        oT_ready = event("oT_ready")
        oT_kept = event("oT_kept")
        att_ready = event("att_ready")
        hA_kept = event("hA_kept")
        st_b = event("stats_b", 2)
        mv_b = event("mean_var_b", 2)
        ve_b = event("var_eps_b", 2)
        rs_b = event("rstd_b", 2)
        xn1_kept = event("xn1_kept")
        xn2_kept = event("xn2_kept")
        t2_ready = event("t2_ready")
        x2T_kept = event("x2T_kept")
        up_ready = event("up_ready", FT)
        gelu_kept = event("gelu_kept", FT)
        down_ready = event("down_ready")
        hB_kept = event("hB_kept")

        top[0] = 0
        wgcn = carve(KP, KT, D)
        n2w, n2b, outb = (carve(P, D) for _ in range(3))
        pick = carve(KP, 32, P, dt=BF16)
        dtp = [carve(P, DT3, BT) for _ in range(2)]
        up_ = [carve(P, DT3, BT) for _ in range(2)]
        xm = [carve(P, DT3, BT) for _ in range(2)]
        zs = [carve(P, DT3, BT) for _ in range(2)]
        xg = [carve(KP, KT, BT) for _ in range(2)]
        xnC = carve(P, TPB, D)
        PADX = SEQ + TAPS - 1
        xnT = carve(KP, KT, SPB, PADX)
        PADC = SEQ + CTAPS - 1
        xi = carve(P, DT3, SPB, PADC)
        bc = [carve(KP, BT, dt=BF16) for _ in range(2)]
        xr = carve(P, TPB, D)
        flat = lambda v: v.rearrange("p a b -> p (a b)")
        rest = flat(xr)[0:KP, 0:BT]
        mid = flat(xr)[0:KP, BT:BT + BT // 2].bitcast(BF16)
        dtl = carve(P, BT)
        sp1 = carve(P, DT3, BT)
        dA = [carve(P, DT3, SPB, SEQ) for _ in range(2)]
        hs = [carve(P, DT3, BT) for _ in range(2)]
        xmb = carve(KP, KT, BT)
        gate = sp1[0:KP, 0:KT, :]
        o = xnC
        stC = carve(P, TPB, 6)
        mvC = [carve(P, TPB, 2) for _ in range(2)]
        pvC = carve(P, 2, TPB)
        rsC = [carve(P, 2, TPB) for _ in range(2)]
        stO = carve(P, TPB, 6)
        mvO = carve(P, TPB, 2)
        veO = carve(P, TPB)
        rsO = carve(P, TPB)
        s_cset = sem("phase_c_ready")
        s_cact = sem("decay_rates_exp")

        st_c = event("stats_c")
        mv_c = event("mean_var_c")
        pv_c = event("var_eps_c")
        rs_c = event("rstd_c")
        xn_c = event("xn_c")
        xnT_ready = event("xnT_ready")
        xnT_kept = event("xnT_kept", KT)
        in_ready = event("in_proj_ready", 2 * DT3)
        in_kept = event("in_proj_kept", 2 * DT3)
        conv_ch = event("channel_conv", DT3 * CTAPS)
        silu_kept = event("silu_kept", 2 * DT3)
        xp_ready = event("x_proj_ready")
        dtl_kept = event("dt_low_kept")
        split = event("bc_split", 5)
        dt_ready = event("dt_ready", DT3)
        sp_abs = event("softplus_abs", DT3)
        sp_exp = event("softplus_exp", DT3)
        sp_log = event("softplus_log", DT3)
        sp_max = event("softplus_max", DT3)
        dt_kept = event("dt_kept", DT3)
        u_kept = event("u_kept", DT3)
        gcn_ready = event("gcn_ready", KT)
        gcn_kept = event("gcn_kept", KT)
        b_ready = event("b_broadcast", NS)
        c_ready = event("c_broadcast", NS)
        da_ready = event("decay_ready", NS * DT3)
        dbx = event("dbx", NS * DT3)
        scan = event("scan", NS * DT3)
        hc = event("h_times_c", NS * DT3)
        nsum = event("state_sum", NS)
        ysk = event("y_skip", DT3)
        yz = event("y_gated", DT3)
        mo_ready = event("mamba_out_ready", KT)
        mo_kept = event("mamba_out_kept", KT)
        gt_ready = event("gate_ready", KT)
        gt_kept = event("gate_kept", KT)
        gt_tanh = event("gate_tanh", KT)
        fuse = event("fuse", 3)
        out_ready = event("out_ready")
        o_kept = event("o_kept", 3)
        st_o = event("stats_o")
        mv_o = event("mean_var_o")
        ve_o = event("var_eps_o")
        rs_o = event("rstd_o")
        on_o = event("o_normed")
        tail_o = event("o_affine", 3)

        top[0] = 0
        w1e = carve(KP, EXP, KT, FF)
        w2e = carve(P, EXP, FT, D)
        rout = carve(KP, KT, EXP)
        tri = carve(P, EXP, EXP)
        below = carve(P, P)
        allones = carve(P, P)
        tokno = carve(P, TPB)
        run = carve(P, EXP)
        caps = carve(P, EXP)
        padrow = carve(P, ROW)
        expert_of = carve(1, NSB, dt=I32)
        slot_of = carve(1, NSB, dt=I32)
        pad_of = carve(1, EXP, dt=I32)
        blockno = carve(1, NSB)
        send = [carve(P, TPB, TOPK, ROW) for _ in range(2)]
        slots_i = [carve(P, TOPK, TPB, dt=I32) for _ in range(2)]
        xTs = carve(KP, KT, BT)
        base_d = top[0]
        hS = [carve(P, FF) for _ in range(2)]
        hTs = [carve(P, FT, P) for _ in range(2)]
        xt = [carve(P, ROW) for _ in range(RING)]
        xT = [carve(KP, KT, P) for _ in range(2)]
        ys = [carve(P, D) for _ in range(RING)]
        gate_s = [carve(P, 1) for _ in range(RING)]
        tok_s = [carve(P, 1, dt=I32) for _ in range(RING)]
        end_d = top[0]
        top[0] = base_d
        xrD = carve(P, TPB, D)
        stD = carve(P, TPB, 6)
        mvD = carve(P, TPB, 2)
        pvD = carve(P, 2, TPB)
        rsD = carve(P, 2, TPB)
        lg = carve(P, TPB, EXP)
        lmax = carve(P, TPB)
        pr = carve(P, TPB, EXP)
        psm = carve(P, TPB)
        cmp1 = carve(P, TPB, EXP, EXP)
        cmp2 = carve(P, TPB, EXP, EXP)
        rank = carve(P, TPB, EXP)
        pick_k = carve(P, TOPK, TPB, EXP)
        sel = carve(P, TPB, EXP)
        pos = carve(P, TPB, EXP)
        gk = carve(P, TOPK, TPB)
        wk = carve(P, TOPK, TPB, EXP)
        sk = carve(P, TOPK, TPB)
        assert top[0] <= end_d
        top[0] = base_d
        cnt = carve(1, EXP)
        cnti = carve(1, EXP, dt=I32)
        nblk = carve(1, EXP)
        lastb = carve(1, EXP)
        firstb = carve(1, EXP)
        rowv = carve(1, EXP)
        ge_end = carve(1, NSB, EXP)
        ge_first = carve(1, NSB, EXP)
        eno = carve(1, NSB)
        sno = carve(1, NSB)
        assert top[0] <= end_d
        slots = nc.dram_tensor("slots_scratch", (EXP * CAP + P, ROW), F32).ap()

        s_wd = sem("router_loaded")
        s_we = sem("experts_loaded")
        st_d = event("stats_d")
        mv_d = event("mean_var_d")
        pv_d = event("var_eps_d")
        rs_d = event("rstd_d")
        xn_d = event("xn_d")
        xn2_d = event("xn_copied")
        dT_ready = event("dT_ready")
        dT_kept = event("dT_kept", KT)
        lg_ready = event("logits_ready")
        NG = 22
        SEL_STEP = 14
        gsteps = event("routing_steps", NG)
        gexp = event("routing_exp")
        pos_ready = event("positions_ready")
        res_d = event("residual_d", 5)
        res_out = event("residual_stored", 16)
        sent = [event(f"slots{j}_written", TOPK * TPB * 16, ahead=0) for j in range(2)]
        s_tab = sem("table_steps")
        s_tables = sem("tables_ready")
        s_pads = sem("padding_written")
        xt_loaded = [event(f"slot_rows{j}_loaded", 16) for j in range(RING)]
        xt_T = event("slot_rows_transposed", ahead=RING)
        xT_kept = event("slot_T_kept", KT)
        meta = event("slot_gate_token_kept", 2, ahead=RING)
        e_up = event("expert_up")
        e_silu = event("expert_silu")
        e_hT = event("hidden_transposed")
        e_hTk = event("hidden_T_kept")
        e_down = event("expert_down")
        e_y = event("gated_output")
        added = event("outputs_added", 16, ahead=0)

        block = ctx.enter_context(nc.Block())
        V = nc.vector

        def wait(eng, ev, b, nth=None):
            eng.wait_ge(ev.sem, ev.at(b, nth))

        def wait_alone(eng, ev, b, nth=None):
            eng.wait_ge(ev.sem, ev.at(b, nth))
            eng.sem_inc(s_alone, 1)


        def shift(sp, i, q, j):
            wait_alone(sp, tok_loaded[j], q)
            wait_alone(sp, outer_a, i - 2)
            sp.dma_start(tok2[j][0:P - 2, :, :], tok[j][2:P, :, :]).then_inc(shifted[j].sem, 16)
            sp.dma_start(tok2[j][P - 2:P, 0:TPB:2, :], tok[j][0:2, 1:TPB:2, :]).then_inc(shifted[j].sem, 16)

        def load_xs(sp, i):
            wait_alone(sp, h0_ready, i - 1)
            for k in range(KT):
                sp.dma_start(xs[:, k, :, 1:SEQ],
                             XT[:, k, bass.ds(i * BT, BT)].rearrange("p (s t) -> p s t", s=SPB)[:, :, 0:SEQ - 1])\
                    .then_inc(xs_loaded.sem, 16)

        @block.sync
        def _(sp):
            sp.dma_start(ids, d["ids"]).then_inc(s_ids, 16)
            sp.dma_start(ident[:, :], d["ident"]).then_inc(s_const, 16)
            sp.dma_start(exps_half[:, :], d["mhalf"]).then_inc(s_const, 16)
            sp.dma_start(va[0:KP, 0:8], d["va_fm"]).then_inc(s_const, 16)
            sp.dma_start(va[:, 8:14], d["b_fc"]).then_inc(s_const, 16)
            sp.dma_start(wa2, d["alphas"]).then_inc(s_const, 16)
            sp.dma_start(lnbrow[KP:KP + 1, :], d["ln_b_row"]).then_inc(s_const, 16)
            sp.dma_start(b1row[:, :], d["b_proj_row"]).then_inc(s_const, 16)
            for dst, name in ((WpT, "WpT"), (WvT, "WvT"), (WpH, "WpH"), (WoH, "WoH"), (tr, "traceT"),
                              (minp, "mask_in"), (mout, "mask_out"), (rope, "rope"), (w0, "W0T"), (w1, "W1T")):
                sp.dma_start(dst, d[name]).then_inc(s_wa, 16)
            sp.dma_start(wv[:, :, :], d["Wv"]).then_inc(s_wa, 16)
            sp.dma_start(wo[:, :], d["Wo"]).then_inc(s_wa, 16)
            with sp.Fori(0, NB // 2) as q:
                for j in (0, 1):
                    shift(sp, 2 * q + j, q, j)
            for dst, name in ((wconv, "wconv"), (win, "win"), (wxp, "wxp"), (wmo, "wmo"), (wgg, "wgg"),
                              (wgm, "wgm"), (wout, "wout")):
                sp.dma_start(dst[:, :] if len(dst.shape) == 2 else
                             (dst[:, :, :] if len(dst.shape) == 3 else dst[:, :, :, :]),
                             d[name]).then_inc(s_wc, 16)
            sp.dma_start(wdt[96:96 + RANK, :], d["wdt"]).then_inc(s_wc, 16)
            sp.dma_start(pick32[:, :], d["pick"]).then_inc(s_wc, 16)
            sp.dma_start(vc[0:KP, 0:12], d["vc_fm"]).then_inc(s_wc, 16)
            sp.dma_start(vc[:, 12:33], d["vc_ch"]).then_inc(s_wc, 16)
            sp.dma_start(nega[:, :, :], d["A_log"]).then_inc(s_wc, 16)
            sp.wait_ge(s_setup_gp, 1)
            load_xs(sp, 0)
            with sp.Fori(1, NB) as i:
                load_xs(sp, i)
            wait_alone(sp, hB_kept, NB - 1)
            sp.dma_start(wgcn, d["wgcn"]).then_inc(s_wc2, 16)
            for dst, name in ((n2w, "n2w"), (n2b, "n2b"), (outb, "outb")):
                sp.dma_start(dst, d[name].partition_broadcast(P)).then_inc(s_wc2, 16)
            wait_alone(sp, tail_o, NB - 1)
            for dst, name in ((rout, "router"), (tri, "tri"), (below, "below"), (allones, "allones"),
                              (tokno, "tokno"), (run, "first_slots"), (caps, "first_slots"), (padrow, "padrow"), (blockno, "blockno")):
                sp.dma_start(dst, d[name]).then_inc(s_wd, 16)
            sp.dma_start(w1e, d["w1"]).then_inc(s_we, 16)
            sp.dma_start(w2e, d["w2"]).then_inc(s_we, 16)
            with sp.Fori(0, NB) as i:
                wait_alone(sp, res_d, i)
                sp.dma_start(out[bass.ds(i * BT, BT), :].rearrange("(t p) f -> p t f", p=P),
                             H[:, bass.ds(i * TPB, TPB), :]).then_inc(res_out.sem, 16)
            sp.wait_ge(s_tables, 1)
            for e in range(EXP):
                row = sp.value_load(pad_of[0:1, e:e + 1], min_val=0, max_val=EXP * CAP)
                sp.dma_start(slots[bass.ds(row, P), :], padrow).then_inc(s_pads, 16)
            sp.dma_start(slots[EXP * CAP:EXP * CAP + P, :], padrow).then_inc(s_pads, 16)
            sp.wait_ge(s_pads, 16 * (EXP + 1))
            for j in (0, 1):
                wait_alone(sp, sent[j], NB // 2 - 1)
            with sp.Fori(0, NSB // RING) as q:
                for j in range(RING):
                    b = RING * q + j
                    wait_alone(sp, xt_T, b - RING)
                    wait_alone(sp, meta, b - RING)
                    row = sp.value_load(slot_of[0:1, bass.ds(b, 1)], min_val=0, max_val=EXP * CAP)
                    sp.dma_start(xt[j], slots[bass.ds(row, P), :]).then_inc(xt_loaded[j].sem, 16)
            sp.wait_ge(added.sem, added.at(NSB - 1))

        def inv_root_a(gp, i, j):
            wait(gp, var_a, i)
            wait(gp, nrm_a, i - 2)
            nc.gpsimd.tensor_tensor(rsA[j], veA, exps_half[:, 0:TPB], ALU.pow).then_inc(rstd_a.sem, 1)

        def root_d(gp, i):
            wait(gp, pv_d, i)
            nc.gpsimd.tensor_tensor(rsD, pvD, exps_half[:, 0:8].rearrange("p (a b) -> p a b", a=2),
                                    ALU.pow).then_inc(rs_d.sem, 1)

        def send_slots(gp, i, q, j):
            wait_alone(gp, gsteps, i)
            wait_alone(gp, xn2_d, i)
            for t in range(TPB):
                for k in range(TOPK):
                    gp.indirect_dma_start(
                        out=slots, out_offset=bass.IndirectOffsetOnAxis(ap=slots_i[j][:, k, t:t + 1], axis=0),
                        in_=send[j][:, t, k, :], in_offset=None).then_inc(sent[j].sem, 16)

        def add_outputs(gp, b, j, first=False):
            wait_alone(gp, e_y, b)
            if not first:
                wait_alone(gp, added, b - 1)
            gp.indirect_dma_start(out=out, out_offset=bass.IndirectOffsetOnAxis(ap=tok_s[j], axis=0),
                                  in_=ys[j], in_offset=None, compute_op=ALU.add).then_inc(added.sem, 16)

        def gather(gp, i, q, j):
            wait(gp, nrm_a, i - 2)
            wait(gp, shifted[j], q - 1)
            nc.gpsimd.tensor_copy(idn[j], ids[:, bass.ds(i * TPB, TPB)]).then_inc(ids_staged[j].sem, 1)
            wait_alone(gp, ids_staged[j], q)
            for t in range(TPB):
                gp.indirect_dma_start(
                    out=tok[j][:, t, :], out_offset=None, in_=d["wte"],
                    in_offset=bass.IndirectOffsetOnAxis(ap=idn[j][:, t:t + 1], axis=0))\
                    .then_inc(tok_loaded[j].sem, 16)

        def rs_c_step(gp, i, j):
            wait(gp, pv_c, i)
            nc.gpsimd.tensor_tensor(rsC[j], pvC, exps_half[:, 0:8].rearrange("p (a b) -> p a b", a=2),
                                    ALU.pow).then_inc(rs_c.sem, 1)

        def back_gp(gp, i):
            wait(gp, ve_o, i)
            nc.gpsimd.tensor_tensor(rsO, veO, exps_half[:, 0:TPB], ALU.pow).then_inc(rs_o.sem, 1)
            wait(gp, on_o, i)
            nc.gpsimd.tensor_tensor(o, o, n2w.unsqueeze(1).broadcast_to([P, TPB, D]), ALU.mult)\
                .then_inc(tail_o.sem, 1)
            wait(gp, tail_o, i, 1)
            nc.gpsimd.tensor_tensor(o, o, n2b.unsqueeze(1).broadcast_to([P, TPB, D]), ALU.add)\
                .then_inc(tail_o.sem, 1)
            wait(gp, tail_o, i, 2)
            Hi = H[:, bass.ds(i * TPB, TPB), :]
            nc.gpsimd.tensor_tensor(Hi, Hi, o, ALU.add).then_inc(tail_o.sem, 1)

        def body_gp(gp, i, j, front=True, back=True):
            if front:
                rs_c_step(gp, i + 1, 1 - j)
            if back:
                back_gp(gp, i - 1)

        @block.gpsimd
        def _(gp):
            for e in events:
                if e.ahead:
                    gp.sem_inc(e.sem, e.ahead * e.per)
            gp.wait_ge(s_ids, 16)
            for j in (0, 1):
                gather(gp, j, 0, j)
            gp.wait_ge(s_const, 16 * 7)
            with gp.Fori(1, NB // 2) as q:
                for j in (0, 1):
                    inv_root_a(gp, 2 * q - 2 + j, j)
                    gather(gp, 2 * q + j, q, j)
            for j in (0, 1):
                inv_root_a(gp, NB - 2 + j, j)
            gp.wait_ge(s_setup, nth(DVE_STEPS, "w1"))
            nc.gpsimd.memset(xs[:, :, :, 0:1], 0.0).then_inc(s_setup_gp, 1)
            with gp.Fori(0, NB) as i:
                for q in (1, 2):
                    wait(gp, ve_b, i, q)
                    nc.gpsimd.tensor_tensor(rsB, veB, exps_half[:, 0:TPB], ALU.pow).then_inc(rs_b.sem, 1)
            rs_c_step(gp, 0, 0)
            body_gp(gp, 0, 0, back=False)
            with gp.Fori(0, NB // 2 - 1) as ii:
                for j in (1, 0):
                    body_gp(gp, 2 * ii + (1 if j else 2), j)
            body_gp(gp, NB - 1, 1, front=False)
            back_gp(gp, NB - 1)
            root_d(gp, 0)
            with gp.Fori(0, NB // 2 - 1) as q:
                for j in (0, 1):
                    root_d(gp, 2 * q + j + 1)
                    send_slots(gp, 2 * q + j, q, j)
            root_d(gp, NB - 1)
            for j in (0, 1):
                send_slots(gp, NB - 2 + j, NB // 2 - 1, j)
            gp.wait_ge(res_out.sem, res_out.at(NB - 1))
            for j in range(RING):
                add_outputs(gp, j, j, first=j == 0)
            with gp.Fori(1, NSB // RING) as q:
                for j in range(RING):
                    add_outputs(gp, RING * q + j, j)

        def route_pe(pe, i, j):
            wait(pe, xn_d, i)
            wait(pe, dT_kept, i - 1)
            for t in range(TPB):
                for k in range(KT):
                    last = nc.tensor.transpose(ps[0:KP, k, t * P:(t + 1) * P],
                                               send[j][:, t, 0, k * KP:(k + 1) * KP], ident[:, :])
            last.then_inc(dT_ready.sem, 1)
            wait(pe, dT_kept, i)
            wait(pe, gsteps, i - 1, 1)
            for t in range(TPB):
                for k in range(KT):
                    last = nc.tensor.matmul(ps[:, 2, t * EXP:(t + 1) * EXP], xTs[:, k, t * P:(t + 1) * P],
                                            rout[:, k, :], start=(k == 0), stop=(k == KT - 1))
            last.then_inc(lg_ready.sem, 1)
            wait(pe, gsteps, i, SEL_STEP)
            wait(pe, gsteps, i - 1)
            for t in range(TPB + 1):
                lhs = [allones] * t + ([below] if t < TPB else [])
                for n, w in enumerate(lhs):
                    last = nc.tensor.matmul(ps[:, 3, t * EXP:(t + 1) * EXP], w, sel[:, n, :],
                                            start=(n == 0), stop=(n == len(lhs) - 1))
            last.then_inc(pos_ready.sem, 1)

        def slot_transpose(pe, b, q, r):
            wait(pe, xt_loaded[r], q)
            wait(pe, xT_kept, b - 1)
            for k in range(KT):
                last = nc.tensor.transpose(ps[0:KP, 7, k * P:(k + 1) * P], xt[r][:, k * KP:(k + 1) * KP], ident[:, :])
            last.then_inc(xt_T.sem, 1)

        def expert_up(pe, b, j):
            j = j % 2
            e = pe.value_load(expert_of[0:1, bass.ds(b, 1)], min_val=0, max_val=EXP - 1)
            wait(pe, xT_kept, b)
            wait(pe, e_silu, b - 2)
            for n in range(2):
                for k in range(KT):
                    w = w1e[:, bass.ds(e, 1), k, n * (FF // 2):(n + 1) * (FF // 2)].rearrange("p e f -> p (e f)")
                    last = nc.tensor.matmul(ps[:, 2 * j + n, 0:FF // 2], xT[j][:, k, :], w,
                                            start=(k == 0), stop=(k == KT - 1))
            last.then_inc(e_up.sem, 1)

        def expert_block(pe, b, q, j, last=0):
            h = j % 2
            wait(pe, e_silu, b)
            wait(pe, e_hTk, b - 1)
            for f in range(FT):
                ins = nc.tensor.transpose(ps[:, 4 + f // 3, (f % 3) * P:(f % 3 + 1) * P],
                                          hS[h][:, f * P:(f + 1) * P], ident[:, :])
            ins.then_inc(e_hT.sem, 1)
            if last < 2:
                expert_up(pe, b + 1, j + 1)
            if not last:
                slot_transpose(pe, b + 2, q + (j + 2) // RING, (j + 2) % RING)
            e = pe.value_load(expert_of[0:1, bass.ds(b, 1)], min_val=0, max_val=EXP - 1)
            wait(pe, e_hTk, b)
            wait(pe, e_y, b - 1)
            for f in range(FT):
                w = w2e[:, bass.ds(e, 1), f, :].rearrange("p e f -> p (e f)")
                ins = nc.tensor.matmul(ps[:, 6, 0:D], hTs[h][:, f, :], w, start=(f == 0), stop=(f == FT - 1))
            ins.then_inc(e_down.sem, 1)

        def setup_pe(pe):
            steps = iter(PE_STEPS)

            def done(name, ins):
                assert next(steps) == name
                ins.then_inc(s_setup_pe, 1)

            pe.wait_ge(s_setup, nth(DVE_STEPS, "sum_row"))
            for k in range(KT):
                last = nc.tensor.matmul(ps[0:KP, 6, k * D:(k + 1) * D], lnbrow[KP:KP + 1, k * KP:(k + 1) * KP],
                                        srow[KP:KP + 1, :], start=True, stop=True)
            done("bias_outer", last)
            pe.wait_ge(s_wa, 16 * SETUP_DMAS)
            wait(pe, xt_a, NB - 1)
            pe.wait_ge(s_setup, nth(DVE_STEPS, "m1"))
            for m in range(KT):
                for k in range(KT):
                    last = nc.tensor.matmul(ps[0:KP, m, :], MS[:, k, m * KP:(m + 1) * KP], WpT[:, k, :],
                                            start=(k == 0), stop=(k == KT - 1))
            done("x1", last)
            pe.wait_ge(s_setup_act, nth(ACT_STEPS, "x1"))
            for h in range(HEADS):
                for k in range(KT):
                    last = nc.tensor.matmul(ps[0:DTR, 2, h * DTR:(h + 1) * DTR], WvT[:, k, h * DTR:(h + 1) * DTR],
                                            X1[:, k, h * DTR:(h + 1) * DTR], start=(k == 0), stop=(k == KT - 1))
            done("update", last)
            pe.wait_ge(s_setup, nth(DVE_STEPS, "trace"))
            for h in range(HEADS):
                last = nc.tensor.matmul(ps[0:DTR, 4 + h // 2, (h % 2) * D:(h % 2 + 1) * D], tr[:, h, :],
                                        WoH[:, h, :], start=True, stop=True)
            done("readout", last)
            pe.wait_ge(s_setup_act, nth(ACT_STEPS, "readout"))
            for k in range(KT):
                for h in range(HEADS):
                    last = nc.tensor.matmul(ps[0:KP, k, 0:D], WpH[:, h, k * KP:(k + 1) * KP], WoH[:, h, :],
                                            start=(h == 0), stop=(h == HEADS - 1))
            done("g", last)
            for q in range(2):
                for k in range(KT):
                    last = nc.tensor.matmul(ps[:, 2 + q, 0:SEQ], rope[:, k, q * P:(q + 1) * P], rope[:, k, :],
                                            start=(k == 0), stop=(k == KT - 1))
            done("scores", last)
            pe.wait_ge(s_setup, nth(DVE_STEPS, "prob1"))
            for q in range(2):
                for k in range(2):
                    last = nc.tensor.transpose(ps[:, 4 + k, q * P:(q + 1) * P], prob[:, q, k * P:(k + 1) * P],
                                               ident[:, :])
            done("probT", last)
            for f in range(FT):
                last = nc.tensor.matmul(ps[:, 6, f:f + 1], mout[:, f * P:(f + 1) * P], wa, start=True, stop=True)
            done("b0", last)
            last = nc.tensor.matmul(ps[0:1, 7, 0:D], wa, minp, start=True, stop=True)
            done("b1", last)
            pe.wait_ge(s_setup_act, nth(ACT_STEPS, "g"))
            for k in range(KT):
                for n in range(2):
                    last = nc.tensor.matmul(ps[0:KP, 2 * k + n, 0:FF // 2], mins[:, k * KP:(k + 1) * KP],
                                            mout[:, n * (FF // 2):(n + 1) * (FF // 2)], start=True, stop=True)
            done("c0", last)
            pe.wait_ge(s_setup, nth(DVE_STEPS, "w0"))
            for f in range(FT):
                last = nc.tensor.matmul(ps[:, f // 2, (f % 2) * D:(f % 2 + 1) * D], mout[:, f * P:(f + 1) * P],
                                        mins, start=True, stop=True)
            done("c1", last)

        def att_front_pe(pe, i, ffn):
            ffn = ffn or (lambda part: None)
            wait(pe, xs_loaded, i)
            wait(pe, hA_kept, i - 1)
            for t in range(TPB):
                for k in range(KT):
                    last = nc.tensor.matmul(tile_in(0, t), xs[:, k, t // 2, (t % 2) * P:(t % 2 + 1) * P],
                                            G[:, k, :], start=(k == 0), stop=(k == KT - 1))
            last.then_inc(h0_ready.sem, 1)
            ffn(0)
            wait(pe, xn1_kept, i)
            wait(pe, x2T_kept, i - 1)
            for t in range(TPB):
                for k in range(KT):
                    last = nc.tensor.transpose(ps[0:KP, 2 + k, t * P:(t + 1) * P], xn1[:, t, k * KP:(k + 1) * KP],
                                               ident[:, :])
            last.then_inc(t1_ready.sem, 1)
            ffn(1)
            wait(pe, x1T_kept, i)
            for t in range(TPB):
                for k in range(KT):
                    last = nc.tensor.matmul(ps[:, 2, t * KV:(t + 1) * KV], x1T[:, k, t * P:(t + 1) * P], wv[:, k, :],
                                            start=(k == 0), stop=(k == KT - 1))
            last.then_inc(v_ready.sem, 1)
            ffn(2)
            wait(pe, v_kept, i)
            for s in range(SPB):
                for k in range(2):
                    last = nc.tensor.matmul(ps[0:KV, 3, s * SEQ:(s + 1) * SEQ], vs[:, 2 * s + k, :], PT[:, k, :],
                                            start=(k == 0), stop=(k == 1))
            last.then_inc(oT_ready.sem, 1)
            ffn(3)
            wait(pe, oT_kept, i)
            wait(pe, h0_kept, i)
            for t in range(TPB):
                last = nc.tensor.matmul(tile_in(0, t), oTs[:, t * P:(t + 1) * P], wo[:, :], start=True, stop=True)
            last.then_inc(att_ready.sem, 1)

        def body_b_pe(pe, i, more=True):
            def ffn(part):
                if part == 0:
                    wait(pe, xn2_kept, i)
                    wait(pe, oT_kept, i)
                    for t in range(TPB):
                        for k in range(KT):
                            last = nc.tensor.transpose(ps[0:KP, 2 + k, t * P:(t + 1) * P],
                                                       xn2[:, t, k * KP:(k + 1) * KP], ident[:, :])
                    last.then_inc(t2_ready.sem, 1)
                    wait(pe, x2T_kept, i)
                if part in (0, 1):
                    for f in range(3 * part, 3 * part + 3):
                        if f >= 2:
                            wait(pe, gelu_kept, i, f - 1)
                        else:
                            wait(pe, gelu_kept, i - 1, FT + f - 1)
                        for k in range(KT):
                            last = nc.tensor.matmul(ps[:, 6 + f % 2, :], w0[:, k, f * P:(f + 1) * P], x2T[:, k, :],
                                                    start=(k == 0), stop=(k == KT - 1))
                        last.then_inc(up_ready.sem, 1)
                if part in (2, 3):
                    if part == 2:
                        wait(pe, gelu_kept, i)
                        wait(pe, hB_kept, i - 1)
                    for t in (0, 1) if part == 2 else (2, 3):
                        for f in range(FT):
                            nc.tensor.matmul(tile_in(4, t), hT[:, f, t * P:(t + 1) * P], w1[:, f, :],
                                             start=(f == 0), stop=False)
                        last = nc.tensor.matmul(tile_in(4, t), ones[:, :], b1row[:, :], start=False, stop=True)
                    if part == 3:
                        last.then_inc(down_ready.sem, 1)

            if more:
                att_front_pe(pe, i + 1, ffn)
            else:
                for part in range(4):
                    ffn(part)

        def transposes_c(pe, i):
            wait(pe, xn_c, i)
            wait(pe, mo_kept, i - 2)
            wait(pe, sp_abs, i - 1)
            wait(pe, gt_kept, i - 2, 1)
            wait(pe, gcn_kept, i - 1)
            for t in range(TPB):
                for k in range(KT):
                    last = nc.tensor.transpose(ps[0:KP, 6 + k, t * P:(t + 1) * P], xnC[:, t, k * KP:(k + 1) * KP],
                                               ident[:, :])
            last.then_inc(xnT_ready.sem, 1)

        def in_proj(pe, i, f):
            if f == 0:
                wait(pe, xnT_kept, i)
                wait(pe, gt_kept, i - 2)
            if f >= 2:
                wait(pe, in_kept, i, f - 1)
            for k in range(KT):
                last = nc.tensor.matmul(ps[:, 5 + f % 2, :], win[:, k, f * P:(f + 1) * P],
                                        xnT[:, k, :, TAPS // 2:TAPS // 2 + SEQ], start=(k == 0), stop=(k == KT - 1))
            last.then_inc(in_ready.sem, 1)

        def x_proj(pe, i, j):
            wait(pe, silu_kept, i, DT3)
            wait(pe, in_kept, i)
            wait(pe, o_kept, i - 2, 3)
            for k in range(DT3):
                last = nc.tensor.matmul(ps[0:108, 5, :], wxp[:, k, :], xm[j][:, k, :],
                                        start=(k == 0), stop=(k == DT3 - 1))
            last.then_inc(xp_ready.sem, 1)

        def dt_proj(pe, i):
            wait(pe, dtl_kept, i)
            for f in range(DT3):
                if f == 1:
                    wait(pe, split, i, 2)
                if f == 2:
                    wait(pe, sp_abs, i, 1)
                last = nc.tensor.matmul(ps[:, 6 - f % 2, :], wdt[96:96 + RANK, f * P:(f + 1) * P],
                                        dtl[96:96 + RANK, :], start=True, stop=True)
                last.then_inc(dt_ready.sem, 1)

        def gcn(pe, i, a, b):
            for n in range(a, b):
                m, r = divmod(n, KT * TAPS)
                if n == 0:
                    wait(pe, xnT_kept, i)
                elif r == 0:
                    wait(pe, gcn_kept, i, 1)
                tap, k = divmod(r, KT)
                last = nc.tensor.matmul(ps[0:KP, 7, :], wconv[:, k, tap, m * KP:(m + 1) * KP],
                                        xnT[:, k, :, tap:tap + SEQ], start=(r == 0), stop=(r == KT * TAPS - 1))
                if r == KT * TAPS - 1:
                    last.then_inc(gcn_ready.sem, 1)

        def front_pe(pe, i, j):
            transposes_c(pe, i)
            for f in range(2 * DT3):
                in_proj(pe, i, f)
            x_proj(pe, i, j)
            dt_proj(pe, i)
            gcn(pe, i, 0, 28)

        def mamba_out(pe, i, j, m, last_block):
            if m == 0:
                wait(pe, yz, i)
            if not last_block:
                wait(pe, sp_abs, i + 1)
            wait(pe, o_kept, i - 1, 3)
            for k in range(DT3):
                last = nc.tensor.matmul(ps[0:KP, 5 + m, :], wmo[:, k, m * KP:(m + 1) * KP], zs[j][:, k, :],
                                        start=(k == 0), stop=(k == DT3 - 1))
            last.then_inc(mo_ready.sem, 1)

        def gate_pe(pe, i, j, m, last_block):
            wait(pe, mo_kept, i)
            wait(pe, gcn_kept, i if last_block else i + 1)
            ops = [(wgg, xg[j]), (wgm, xmb)]
            n = 0
            for w, x in ops:
                for k in range(KT):
                    last = nc.tensor.matmul(ps[0:KP, 7 - 2 * m, :], w[:, k, m * KP:(m + 1) * KP], x[:, k, :],
                                            start=(n == 0), stop=(n == 3))
                    n += 1
            last.then_inc(gt_ready.sem, 1)

        def out_pe(pe, i, last_block):
            wait(pe, fuse, i)
            wait(pe, gt_kept, i)
            if not last_block:
                wait(pe, in_kept, i + 2)
            for t in range(TPB):
                for k in range(KT):
                    last = nc.tensor.matmul(tile_in(5, t), gate[:, k, t * P:(t + 1) * P], wout[:, k, :],
                                            start=(k == 0), stop=(k == KT - 1))
            last.then_inc(out_ready.sem, 1)

        def back_pe(pe, i, j, last):
            for m in range(KT):
                mamba_out(pe, i, j, m, last)
            for m in range(KT):
                gate_pe(pe, i, j, m, last)
            out_pe(pe, i, last)

        def bcast(pe, i, j, n, which):
            if n == 0:
                wait(pe, split, i, 5)
            ev = dbx if which == 0 else hc
            if n:
                wait(pe, ev, i, n * DT3)
            else:
                wait(pe, ev, i - 1)
            nc.tensor.matmul(ps[:, 3 + which, :], pick[:, which * NS + n, :], bc[j], start=True, stop=True)\
                .then_inc((b_ready, c_ready)[which].sem, 1)

        def body_pe(pe, i, j, front=True, back=True):
            bcast(pe, i, j, 0, 0)
            bcast(pe, i, j, 0, 1)
            for n in range(NS):
                if n + 1 < NS:
                    bcast(pe, i, j, n + 1, 0)
                if back:
                    if n in (0, 1):
                        mamba_out(pe, i - 1, 1 - j, n, False)
                    if n in (2, 3):
                        gate_pe(pe, i - 1, 1 - j, n - 2, False)
                    if n == 10:
                        out_pe(pe, i - 1, not front)
                if front:
                    if n == 4:
                        transposes_c(pe, i + 1)
                    if n in (5, 6, 7):
                        in_proj(pe, i + 1, 2 * (n - 5))
                        in_proj(pe, i + 1, 2 * (n - 5) + 1)
                    if n == 8:
                        gcn(pe, i + 1, 0, 4)
                    if n == 9:
                        gcn(pe, i + 1, 4, 8)
                    if n == 11:
                        x_proj(pe, i + 1, 1 - j)
                        gcn(pe, i + 1, 8, 12)
                    if n == 12:
                        gcn(pe, i + 1, 12, 16)
                    if n == 14:
                        gcn(pe, i + 1, 16, 22)
                    if n == 15:
                        gcn(pe, i + 1, 22, 28)
                if n + 1 < NS:
                    bcast(pe, i, j, n + 1, 1)
                for f in range(DT3):
                    wait(pe, hc, i, n * DT3 + f + 1)
                    if n == 0:
                        wait(pe, ysk, i - 1, f + 1)
                    last = nc.tensor.matmul(ps[:, f, :], ident[:, :], hs[n % 2][:, f, :],
                                            start=(n == 0), stop=(n == NS - 1))
                last.then_inc(nsum.sem, 1)
                if front and n == 12:
                    dt_proj(pe, i + 1)

        @block.tensor
        def _(pe):
            pe.wait_ge(s_const, 16 * 7)
            pe.wait_ge(s_zero, 1)
            with pe.Fori(0, NB // 2) as ii:
                for j in (0, 1):
                    i = 2 * ii + j
                    wait(pe, nrm_a, i)
                    wait(pe, xt_a, i - 2)
                    for t in range(TPB):
                        for k in range(KT):
                            last = nc.tensor.transpose(ps[0:KP, 2 * j + k, t * P:(t + 1) * P],
                                                       nrm[j][:, t, k * KP:(k + 1) * KP], ident[:, :])
                    last.then_inc(nrmT_a.sem, 1)
                    wait(pe, shifted[j], ii)
                    for t in range(TPB):
                        rows = P if t % 2 == 0 else P - 2
                        for k in range(KT):
                            m = KP + k
                            last = nc.tensor.matmul(ps[0:m, 4 + k, 0:D], nrm[j][0:rows, t, k * KP:k * KP + m],
                                                    tok2[j][0:rows, t, :], start=False, stop=False,
                                                    skip_group_check=True)
                    last.then_inc(outer_a.sem, 1)
            setup_pe(pe)
            pe.wait_ge(s_setup, nth(DVE_STEPS, "w1"))
            att_front_pe(pe, 0, None)
            with pe.Fori(0, NB - 1) as i:
                body_b_pe(pe, i)
            body_b_pe(pe, NB - 1, False)
            pe.wait_ge(s_cset, 1)
            front_pe(pe, 0, 0)
            body_pe(pe, 0, 0, back=False)
            with pe.Fori(0, NB // 2 - 1) as ii:
                for j in (1, 0):
                    body_pe(pe, 2 * ii + (1 if j else 2), j)
            body_pe(pe, NB - 1, 1, front=False)
            back_pe(pe, NB - 1, 1, last=True)
            pe.wait_ge(s_wd, 16 * 9)
            with pe.Fori(0, NB // 2) as q:
                for j in (0, 1):
                    route_pe(pe, 2 * q + j, j)
            pe.wait_ge(s_we, 32)
            pe.wait_ge(s_tables, 1)
            slot_transpose(pe, 0, 0, 0)
            slot_transpose(pe, 1, 0, 1)
            expert_up(pe, 0, 0)
            with pe.Fori(0, NSB // RING - 1) as q:
                for j in range(RING):
                    expert_block(pe, RING * q + j, q, j)
            for j in range(RING):
                expert_block(pe, NSB - RING + j, NSB // RING - 1, j, last=max(0, j + 3 - RING))

        def slot_T_act(act, b, j):
            wait(act, xt_T, b)
            wait(act, e_up, b - 2)
            for k in range(KT):
                nc.scalar.activation(xT[j][:, k, :], ps[0:KP, 7, k * P:(k + 1) * P], ACT.Identity,
                                     bias=mob[:, k:k + 1], scale=mow[:, k:k + 1]).then_inc(xT_kept.sem, 1)

        def silu_e(act, b, j):
            wait(act, e_up, b)
            wait(act, e_hT, b - 2)
            nc.scalar.activation(hS[j].rearrange("p (n f) -> p n f", n=2), ps[:, 2 * j:2 * j + 2, 0:FF // 2],
                                 ACT.Silu).then_inc(e_silu.sem, 1)

        def att_act(act, i, ffn=None):
            ffn = ffn or (lambda part: None)
            ffn(0)
            wait(act, t1_ready, i)
            wait(act, v_ready, i - 1)
            nc.scalar.activation(x1T, ps[0:KP, 2:4, :], ACT.Copy).then_inc(x1T_kept.sem, 1)
            ffn(1)
            wait(act, v_ready, i)
            wait(act, oT_ready, i - 1)
            nc.scalar.activation(vs, ps[:, 2, 0:TPB * KV].rearrange("p (t f) -> p t f", t=TPB), ACT.Copy)\
                .then_inc(v_kept.sem, 1)
            wait(act, oT_ready, i)
            wait(act, att_ready, i - 1)
            nc.scalar.activation(oTs, ps[0:KV, 3, :], ACT.Copy).then_inc(oT_kept.sem, 1)

        def body_b_act(act, i, more=True):
            def ffn(part):
                if part == 0:
                    wait(act, t2_ready, i)
                    wait(act, up_ready, i - 1)
                    nc.scalar.activation(x2T, ps[0:KP, 2:4, :], ACT.Copy).then_inc(x2T_kept.sem, 1)
                    wait(act, down_ready, i - 1)
                for f in range(3 * part, 3 * part + 3):
                    wait(act, up_ready, i, f + 1)
                    nc.scalar.activation(hT[:, f, :], ps[:, 6 + f % 2, :], ACT.Gelu_apprx_tanh,
                                         bias=b0[:, f:f + 1]).then_inc(gelu_kept.sem, 1)

            if more:
                att_act(act, i + 1, ffn)
            else:
                ffn(0)
                ffn(1)

        def decay(act, i, j, n):
            if n >= 2:
                wait(act, scan, i, (n - 1) * DT3)
            else:
                wait(act, scan, i - 1, (NS - 1 + n) * DT3)
            for f in range(DT3):
                if n == 0:
                    wait(act, dt_kept, i, f + 1)
                nc.scalar.activation(dA[n % 2][:, f, :, 1:SEQ],
                                     dtp[j][:, f, :].rearrange("p (s t) -> p s t", s=SPB)[:, :, 1:SEQ],
                                     ACT.Exp, scale=nega[:, f, n:n + 1]).then_inc(da_ready.sem, 1)

        def xnT_act(act, i):
            wait(act, xnT_ready, i)
            wait(act, in_ready, i - 1)
            wait(act, gcn_ready, i - 1)
            for k in range(KT):
                nc.scalar.activation(xnT[:, k, :, TAPS // 2:TAPS // 2 + SEQ],
                                     ps[0:KP, 6 + k, :].rearrange("p (s t) -> p s t", s=SPB),
                                     ACT.Identity, bias=n1b[:, k:k + 1], scale=n1w[:, k:k + 1])\
                    .then_inc(xnT_kept.sem, 1)

        def in_act(act, i, j, f):
            wait(act, in_ready, i, f + 1)
            src = ps[:, 5 + f % 2, :]
            if f < DT3:
                if f == 0:
                    wait(act, conv_ch, i - 1)
                nc.scalar.activation(xi[:, f, :, CTAPS - 1:PADC], src.rearrange("p (s t) -> p s t", s=SPB),
                                     ACT.Copy).then_inc(in_kept.sem, 1)
            else:
                if f == DT3:
                    wait(act, mo_ready, i - 2)
                nc.scalar.activation(zs[j][:, f - DT3, :], src, ACT.Copy).then_inc(in_kept.sem, 1)

        def silus_act(act, i, j):
            wait(act, conv_ch, i)
            for f in range(DT3):
                nc.scalar.activation(xm[j][:, f, :], xm[j][:, f, :], ACT.Silu).then_inc(silu_kept.sem, 1)
            for f in range(DT3):
                if f == 0:
                    wait(act, in_kept, i)
                nc.scalar.activation(zs[j][:, f, :], zs[j][:, f, :], ACT.Silu).then_inc(silu_kept.sem, 1)

        def dtl_act(act, i):
            wait(act, xp_ready, i)
            wait(act, dt_ready, i - 1)
            nc.scalar.activation(dtl[96:96 + RANK, :], ps[96:96 + RANK, 5, :], ACT.Copy).then_inc(dtl_kept.sem, 1)

        def softplus_act(act, i, f):
            wait(act, dt_ready, i, f + 1)
            wait(act, sp_max, i, f + 1)
            wait(act, out_ready, i - 2)
            s = sp1[:, f, :]
            nc.scalar.activation(s, ps[:, 6 - f % 2, :], ACT.Abs, bias=dtb[:, f:f + 1]).then_inc(sp_abs.sem, 1)
            wait(act, sp_abs, i, f + 1)
            nc.scalar.activation(s, s, ACT.Exp, scale=-1.0).then_inc(sp_exp.sem, 1)
            wait(act, sp_exp, i, f + 1)
            nc.scalar.activation(s, s, ACT.Ln, bias=1.0).then_inc(sp_log.sem, 1)

        def gcn_act(act, i, j, m):
            wait(act, gcn_ready, i, m + 1)
            wait(act, fuse, i - 2)
            nc.scalar.activation(xg[j][:, m, :], ps[0:KP, 7, :], ACT.Identity, bias=xgb[:, m:m + 1])\
                .then_inc(gcn_kept.sem, 1)

        def mo_act(act, i, m):
            wait(act, mo_ready, i, m + 1)
            wait(act, gt_ready, i - 1)
            wait(act, fuse, i - 1)
            nc.scalar.activation(xmb[:, m, :], ps[0:KP, 5 + m, :], ACT.Copy).then_inc(mo_kept.sem, 1)

        def gate_act(act, i, m, last=False):
            wait(act, gt_ready, i, m + 1)
            wait(act, dt_kept, i if last else i + 1)
            nc.scalar.activation(gate[:, m, :], ps[0:KP, 7 - 2 * m, :], ACT.Identity, bias=gateb[:, m:m + 1])\
                .then_inc(gt_kept.sem, 1)

        def tanh_act(act, i):
            wait(act, gt_kept, i)
            for m in range(KT):
                nc.scalar.activation(gate[:, m, :], gate[:, m, :], ACT.Tanh, scale=0.5).then_inc(gt_tanh.sem, 1)

        def front_act(act, i, j):
            xnT_act(act, i)
            for f in range(2 * DT3):
                in_act(act, i, j, f)
            silus_act(act, i, j)
            dtl_act(act, i)
            for f in range(DT3):
                softplus_act(act, i, f)
            for m in range(KT):
                gcn_act(act, i, j, m)

        def body_act(act, i, j, front=True, back=True):
            decay(act, i, j, 0)
            decay(act, i, j, 1)
            for n in range(NS):
                if back:
                    if n in (0, 1):
                        mo_act(act, i - 1, n)
                    if n in (2, 3):
                        gate_act(act, i - 1, n - 2)
                if front:
                    if n == 4:
                        xnT_act(act, i + 1)
                    if n in (5, 6, 7):
                        in_act(act, i + 1, 1 - j, 2 * (n - 5))
                        in_act(act, i + 1, 1 - j, 2 * (n - 5) + 1)
                if n == 9:
                    if back:
                        tanh_act(act, i - 1)
                    if front:
                        silus_act(act, i + 1, 1 - j)
                if front:
                    if n == 11:
                        dtl_act(act, i + 1)
                    if n == 12:
                        gcn_act(act, i + 1, 1 - j, 0)
                    if n in (13, 14, 15):
                        softplus_act(act, i + 1, n - 13)
                    if n == 15:
                        gcn_act(act, i + 1, 1 - j, 1)
                if n + 2 < NS:
                    decay(act, i, j, n + 2)
            if not front:
                for m in range(KT):
                    mo_act(act, i, m)
                for m in range(KT):
                    gate_act(act, i, m, last=True)
                tanh_act(act, i)

        @block.scalar
        def _(act):
            act.wait_ge(s_const, 16 * 7)
            with act.Fori(0, NB // 2) as ii:
                for j in (0, 1):
                    i = 2 * ii + j
                    wait(act, nrmT_a, i)
                    for k in range(KT):
                        last = nc.scalar.activation(XT[:, k, bass.ds(i * BT, BT)], ps[0:KP, 2 * j + k, :],
                                                    ACT.Identity, bias=lnb[:, k:k + 1], scale=lnw[:, k:k + 1])
                    last.then_inc(xt_a.sem, 1)
            act.wait_ge(s_setup_pe, nth(PE_STEPS, "x1"))
            nc.scalar.activation(X1, ps[0:KP, 0:2, :], ACT.Copy).then_inc(s_setup_act, 1)
            act.wait_ge(s_setup_pe, nth(PE_STEPS, "readout"))
            nc.scalar.activation(WoH[:, :, :].rearrange("p (a b) o -> p a (b o)", b=2), ps[0:DTR, 4:8, 0:2 * D],
                                 ACT.Copy).then_inc(s_setup_act, 1)
            act.wait_ge(s_setup_pe, nth(PE_STEPS, "g"))
            nc.scalar.activation(G[:, :, :], ps[0:KP, 0:2, 0:D], ACT.Copy).then_inc(s_setup_act, 1)
            act.wait_ge(s_setup, nth(DVE_STEPS, "negmax"))
            for q in range(2):
                nc.scalar.activation(prob[:, q, :], ps[:, 2 + q, 0:SEQ], ACT.Exp, bias=smax[:, q:q + 1],
                                     accum_out=ssum[:, q:q + 1]).then_inc(s_setup_act, 1)
            act.wait_ge(s_setup_pe, nth(PE_STEPS, "probT"))
            nc.scalar.activation(PT[:, :, :], ps[:, 4:6, 0:SEQ], ACT.Copy).then_inc(s_setup_act, 1)
            att_act(act, 0)
            with act.Fori(0, NB - 1) as i:
                body_b_act(act, i)
            body_b_act(act, NB - 1, False)
            act.wait_ge(s_wc, 16 * 12)
            nc.scalar.activation(nega[:, :, :], nega[:, :, :], ACT.Exp).then_inc(s_cact, 1)
            wait(act, hB_kept, NB - 1)
            front_act(act, 0, 0)
            body_act(act, 0, 0, back=False)
            with act.Fori(0, NB // 2 - 1) as ii:
                for j in (1, 0):
                    body_act(act, 2 * ii + (1 if j else 2), j)
            body_act(act, NB - 1, 1, front=False)
            act.wait_ge(s_wd, 16 * 9)
            with act.Fori(0, NB // 2) as q:
                for j in (0, 1):
                    i = 2 * q + j
                    wait(act, xn_d, i)
                    wait(act, gsteps, i - 1)
                    nc.scalar.activation(send[j][:, :, 1, 0:D], send[j][:, :, 0, 0:D], ACT.Copy)\
                        .then_inc(xn2_d.sem, 1)
                    wait(act, dT_ready, i)
                    wait(act, lg_ready, i - 1)
                    for k in range(KT):
                        nc.scalar.activation(xTs[:, k, :], ps[0:KP, k, :], ACT.Identity, bias=mob[:, k:k + 1],
                                             scale=mow[:, k:k + 1]).then_inc(dT_kept.sem, 1)
                    wait(act, gsteps, i, 3)
                    nc.scalar.activation(pr, lg, ACT.Exp).then_inc(gexp.sem, 1)
            act.wait_ge(s_tables, 1)
            slot_T_act(act, 0, 0)
            slot_T_act(act, 1, 1)
            silu_e(act, 0, 0)
            with act.Fori(0, NSB // 2 - 1) as q:
                for j in (0, 1):
                    silu_e(act, 2 * q + j + 1, 1 - j)
                    slot_T_act(act, 2 * q + j + 2, j)
            silu_e(act, NSB - 1, 1)

        def setup_dve(dve):
            steps = iter(DVE_STEPS)
            assert next(steps) == "ones"

            def step(name, ins):
                assert next(steps) == name
                ins.then_inc(s_setup, 1)
                dve.wait_ge(s_setup, nth(DVE_STEPS, name))

            def pe_done(name):
                dve.wait_ge(s_setup_pe, nth(PE_STEPS, name))

            wait(dve, outer_a, NB - 1)
            step("sum_row", V.tensor_copy(srow[KP:KP + 1, :], ps[KP:KP + 1, 5, 0:D]))
            step("alpha", V.tensor_tensor(wa, wa2[:, 0:1], wa2[:, 1:2], ALU.mult))
            dve.wait_ge(s_wa, 16 * SETUP_DMAS)
            step("scaled_mask", V.tensor_scalar(mins, minp, wa, None, ALU.mult))
            pe_done("bias_outer")
            for k in range(KT):
                step(f"m{k}w", V.tensor_scalar(MS[:, k, :], ps[0:KP, 4 + k, 0:D], lnw[:, k:k + 1], None, ALU.mult))
                step(f"m{k}", V.tensor_tensor(MS[:, k, :], MS[:, k, :], ps[0:KP, 6, k * D:(k + 1) * D], ALU.add))
            step("decayed", V.tensor_scalar(tr, tr, TRACE_DECAY, None, ALU.mult))
            pe_done("update")
            trf = tr.rearrange("p h q -> p (h q)")
            step("trace", V.scalar_tensor_tensor(out=trf, in0=ps[0:DTR, 2, :],
                                                 scalar=TRACE_LR / (BATCH * (SEQ - 2)), in1=trf,
                                                 op0=ALU.mult, op1=ALU.add))
            pe_done("scores")
            step("max", V.tensor_reduce(smax, ps[:, 2:4, 0:SEQ], AX.X, ALU.max))
            step("negmax", V.tensor_scalar(smax, smax, -1.0, None, ALU.mult))
            dve.wait_ge(s_setup_act, nth(ACT_STEPS, "exp1"))
            step("recip", V.reciprocal(ssum, ssum))
            for q in range(2):
                step(f"prob{q}", V.tensor_scalar(prob[:, q, :], prob[:, q, :], ssum[:, q:q + 1], None, ALU.mult))
            pe_done("b1")
            step("b0", V.tensor_tensor(b0, bfc, ps[:, 6, 0:FT], ALU.mult))
            step("b1", V.tensor_tensor(b1row[:, :], b1row[:, :], ps[0:1, 7, 0:D], ALU.mult))
            pe_done("c0")
            w0v = w0.rearrange("p k (n f) -> p (k n) f", n=2)
            step("w0", V.tensor_tensor(w0v, w0v, ps[0:KP, 0:4, 0:FF // 2], ALU.mult))
            pe_done("c1")
            w1v = w1.rearrange("p (a b) e -> p a (b e)", b=2)
            step("w1", V.tensor_tensor(w1v, w1v, ps[:, 0:3, 0:2 * D], ALU.mult))

        def norm_b(dve, i, q, src, dst, dst_free, done):
            for t in range(TPB):
                last = V.bn_stats(stB[:, t, :], src[:, t, :])
            last.then_inc(st_b.sem, 1)
            wait_alone(dve, st_b, i, q)
            for t in range(TPB):
                last = V.bn_aggr(mvB[:, t, :], stB[:, t, :])
            last.then_inc(mv_b.sem, 1)
            wait(dve, mv_b, i, q)
            V.tensor_scalar(veB, mvB[:, :, 1], EPS, None, ALU.add).then_inc(ve_b.sem, 1)
            wait(dve, rs_b, i, q)
            wait(dve, dst_free, i - 1)
            for t in range(TPB):
                last = V.tensor_scalar(dst[:, t, :], src[:, t, :], mvB[:, t, 0:1], rsB[:, t:t + 1],
                                       ALU.subtract, ALU.mult)
            last.then_inc(done.sem, 1)

        def att_dve(dve, i, resid=None):
            wait(dve, h0_ready, i)
            V.tensor_copy(h0c.rearrange("p (a b) f -> p a (b f)", b=2), tiles_of(0)).then_inc(h0_kept.sem, 1)
            wait(dve, h0_kept, i)
            norm_b(dve, i, 1, h0c, xn1, t1_ready, xn1_kept)
            if resid:
                resid()
            wait(dve, hB_kept, i - 1)
            wait(dve, att_ready, i)
            V.tensor_tensor(hA.rearrange("p (a b) f -> p a (b f)", b=2), h0c.rearrange("p (a b) f -> p a (b f)", b=2),
                            tiles_of(0), ALU.add).then_inc(hA_kept.sem, 1)
            wait(dve, hA_kept, i)
            norm_b(dve, i, 2, hA, xn2, t2_ready, xn2_kept)

        def body_b_dve(dve, i, more=True):
            def resid():
                wait(dve, down_ready, i)
                V.tensor_tensor(H[:, bass.ds(i * TPB, TPB), :].rearrange("p (a b) f -> p a (b f)", b=2),
                                hA.rearrange("p (a b) f -> p a (b f)", b=2), tiles_of(4), ALU.add)\
                    .then_inc(hB_kept.sem, 1)

            if more:
                att_dve(dve, i + 1, resid)
            else:
                resid()

        def norm_c(dve, i, j):
            Hi = lambda t: H[:, bass.ds(i * TPB + t, 1), :].rearrange("p t f -> p (t f)")
            if isinstance(i, int) and i == 0:
                wait(dve, hB_kept, NB - 1)
            for t in range(TPB):
                last = V.bn_stats(stC[:, t, :], Hi(t))
            last.then_inc(st_c.sem, 1)
            wait_alone(dve, st_c, i)
            for t in range(TPB):
                last = V.bn_aggr(mvC[j][:, t, :], stC[:, t, :])
            last.then_inc(mv_c.sem, 1)
            wait(dve, mv_c, i)
            wait(dve, rs_c, i - 1)
            V.tensor_scalar(pvC[:, 0, :], mvC[j][:, :, 1], EPS, None, ALU.add)
            V.tensor_scalar(pvC[:, 1, :], mvC[j][:, :, 1], 1.0 + EPS, EPS * EPS, ALU.mult, ALU.add)\
                .then_inc(pv_c.sem, 1)

        def xn_dve(dve, i, j):
            wait(dve, rs_c, i)
            wait(dve, xnT_ready, i - 1)
            wait(dve, tail_o, i - 3)
            for t in range(TPB):
                last = V.tensor_scalar(xnC[:, t, :], H[:, bass.ds(i * TPB + t, 1), :].rearrange("p t f -> p (t f)"),
                                       mvC[j][:, t, 0:1], rsC[j][:, 1, t:t + 1], ALU.subtract, ALU.mult)
            last.then_inc(xn_c.sem, 1)

        def conv_dve(dve, i, j, f):
            wait(dve, in_kept, i, f + 1)
            x3 = xm[j][:, f, :].rearrange("p (s t) -> p s t", s=SPB)
            for tap in range(CTAPS):
                src = xi[:, f, :, tap:tap + SEQ]
                if tap == 0:
                    ins = V.tensor_scalar(x3, src, cw[:, f, 0:1], cb[:, f:f + 1], ALU.mult, ALU.add)
                else:
                    wait(dve, conv_ch, i, f * CTAPS + tap)
                    ins = V.scalar_tensor_tensor(out=x3, in0=src, scalar=cw[:, f, tap:tap + 1], in1=x3,
                                                 op0=ALU.mult, op1=ALU.add)
                ins.then_inc(conv_ch.sem, 1)

        def split_dve(dve, i, j):
            wait(dve, xp_ready, i)
            src = ps[0:96, 5, :]
            bcp = bc[j]
            V.tensor_copy(bcp, src).then_inc(split.sem, 1)
            wait(dve, split, i, 1)
            V.tensor_tensor(rest, src, bcp, ALU.subtract).then_inc(split.sem, 1)
            wait(dve, split, i, 2)
            V.tensor_copy(mid, rest).then_inc(split.sem, 1)
            wait(dve, split, i, 3)
            V.tensor_copy(bcp[32:64, :], mid[32:64, :]).then_inc(split.sem, 1)
            V.tensor_tensor(bcp[64:96, :], rest[64:96, :], mid[64:96, :], ALU.subtract).then_inc(split.sem, 1)

        def softplus_max_dve(dve, i, j, f):
            wait(dve, dt_ready, i, f + 1)
            V.tensor_scalar(dtp[j][:, f, :], ps[:, 6 - f % 2, :], dtb[:, f:f + 1], 0.0, ALU.add, ALU.max)\
                .then_inc(sp_max.sem, 1)

        def softplus_dve(dve, i, j, f):
            wait(dve, sp_max, i, f + 1)
            wait(dve, sp_log, i, f + 1)
            V.tensor_tensor(dtp[j][:, f, :], dtp[j][:, f, :], sp1[:, f, :], ALU.add).then_inc(dt_kept.sem, 1)
            wait(dve, dt_kept, i, f + 1)
            wait(dve, silu_kept, i, f + 1)
            V.tensor_tensor(up_[j][:, f, :], dtp[j][:, f, :], xm[j][:, f, :], ALU.mult).then_inc(u_kept.sem, 1)

        def front_dve(dve, i, j):
            norm_c(dve, i, j)
            xn_dve(dve, i, j)
            for f in range(DT3):
                conv_dve(dve, i, j, f)
            split_dve(dve, i, j)
            for f in range(DT3):
                softplus_max_dve(dve, i, j, f)
                softplus_dve(dve, i, j, f)

        def fuse_dve(dve, i, j):
            wait(dve, gt_tanh, i)
            wait(dve, gcn_kept, i)
            V.tensor_tensor(xg[j], xg[j], xmb, ALU.subtract).then_inc(fuse.sem, 1)
            wait(dve, fuse, i, 1)
            V.scalar_tensor_tensor(out=xg[j], in0=gate, scalar=1.0, in1=xg[j], op0=ALU.add, op1=ALU.mult)\
                .then_inc(fuse.sem, 1)
            wait(dve, fuse, i, 2)
            V.scalar_tensor_tensor(out=gate, in0=xg[j], scalar=0.5, in1=xmb, op0=ALU.mult, op1=ALU.add)\
                .then_inc(fuse.sem, 1)

        def xr_dve(dve, i, j):
            wait(dve, o_kept, i - 1, 3)
            for t in range(TPB):
                last = V.tensor_scalar(xr[:, t, :], H[:, bass.ds(i * TPB + t, 1), :].rearrange("p t f -> p (t f)"),
                                       mvC[j][:, t, 0:1], rsC[j][:, 0, t:t + 1], ALU.subtract, ALU.mult)
            last.then_inc(o_kept.sem, 1)
            wait(dve, o_kept, i, 1)
            V.tensor_tensor(xr, xr, outb.unsqueeze(1).broadcast_to([P, TPB, D]), ALU.add)\
                .then_inc(o_kept.sem, 1)

        def out_dve(dve, i, last=False):
            wait(dve, xnT_ready, i if last else i + 2)
            wait(dve, out_ready, i)
            wait(dve, o_kept, i, 2)
            wait(dve, tail_o, i - 1)
            V.tensor_tensor(o.rearrange("p (a b) f -> p a (b f)", b=2), xr.rearrange("p (a b) f -> p a (b f)", b=2),
                            tiles_of(5), ALU.add).then_inc(o_kept.sem, 1)
            wait(dve, o_kept, i, 3)
            for t in range(TPB):
                last = V.bn_stats(stO[:, t, :], o[:, t, :])
            last.then_inc(st_o.sem, 1)
            wait_alone(dve, st_o, i)
            for t in range(TPB):
                last = V.bn_aggr(mvO[:, t, :], stO[:, t, :])
            last.then_inc(mv_o.sem, 1)
            wait(dve, mv_o, i)
            V.tensor_scalar(veO, mvO[:, :, 1], EPS, None, ALU.add).then_inc(ve_o.sem, 1)

        def onorm_dve(dve, i):
            wait(dve, rs_o, i)
            for t in range(TPB):
                last = V.tensor_scalar(o[:, t, :], o[:, t, :], mvO[:, t, 0:1], rsO[:, t:t + 1],
                                       ALU.subtract, ALU.mult)
            last.then_inc(on_o.sem, 1)

        def body_dve(dve, i, j, front=True, back=True):
            for n in range(NS):
                buf = hs[n % 2]
                for f in range(DT3):
                    if n == 0:
                        wait(dve, u_kept, i, f + 1)
                    if f == 0:
                        wait(dve, b_ready, i, n + 1)
                        if n >= 2:
                            wait(dve, nsum, i, n - 1)
                        else:
                            wait(dve, nsum, i - 1, NS - 1 + n)
                    V.tensor_tensor(buf[:, f, :], up_[j][:, f, :], ps[:, 3, :], ALU.mult).then_inc(dbx.sem, 1)
                for f in range(DT3):
                    c = n * DT3 + f + 1
                    wait(dve, dbx, i, c)
                    wait(dve, da_ready, i, c)
                    V.tensor_tensor_scan(out=buf[:, f, :], data0=dA[n % 2][:, f, :, :].rearrange("p s t -> p (s t)"),
                                         data1=buf[:, f, :], initial=0.0, op0=ALU.mult, op1=ALU.add)\
                        .then_inc(scan.sem, 1)
                for f in range(DT3):
                    c = n * DT3 + f + 1
                    wait(dve, scan, i, c)
                    if f == 0:
                        wait(dve, c_ready, i, n + 1)
                    V.tensor_tensor(buf[:, f, :], buf[:, f, :], ps[:, 4, :], ALU.mult).then_inc(hc.sem, 1)
                if back and n == 0:
                    xr_dve(dve, i - 1, 1 - j)
                if front:
                    if n == 0:
                        norm_c(dve, i + 1, 1 - j)
                    if n == 2:
                        xn_dve(dve, i + 1, 1 - j)
                    if n in (6, 7, 8):
                        conv_dve(dve, i + 1, 1 - j, n - 6)
                if back:
                    if n == 9:
                        fuse_dve(dve, i - 1, 1 - j)
                    if n == 10:
                        out_dve(dve, i - 1, last=not front)
                    if n == 12:
                        onorm_dve(dve, i - 1)
                if front:
                    if n == 11:
                        split_dve(dve, i + 1, 1 - j)
                    if n == 13:
                        softplus_max_dve(dve, i + 1, 1 - j, 0)
                        softplus_max_dve(dve, i + 1, 1 - j, 1)
                    if n == 14:
                        softplus_max_dve(dve, i + 1, 1 - j, 2)
                    if n == 15:
                        softplus_dve(dve, i + 1, 1 - j, 0)
            if front:
                softplus_dve(dve, i + 1, 1 - j, 1)
                softplus_dve(dve, i + 1, 1 - j, 2)
            wait(dve, nsum, i)
            for f in range(DT3):
                V.scalar_tensor_tensor(out=xm[j][:, f, :], in0=xm[j][:, f, :], scalar=dskip[:, f:f + 1],
                                       in1=ps[:, f, :], op0=ALU.mult, op1=ALU.add).then_inc(ysk.sem, 1)
            for f in range(DT3):
                wait(dve, ysk, i, f + 1)
                V.tensor_tensor(zs[j][:, f, :], xm[j][:, f, :], zs[j][:, f, :], ALU.mult).then_inc(yz.sem, 1)

        def meta_dve(dve, b, q, r, first=False):
            wait(dve, xt_loaded[r], q)
            if not first:
                wait(dve, added, b - RING)
            V.tensor_copy(gate_s[r], xt[r][:, D:D + 1]).then_inc(meta.sem, 1)
            V.tensor_copy(tok_s[r], xt[r][:, D + 1:D + 2]).then_inc(meta.sem, 1)

        def expert_dve(dve, b, q, r, first=False, last=False):
            j = r % 2
            wait(dve, e_hT, b)
            wait(dve, e_down, b - 2)
            V.tensor_copy(hTs[j].rearrange("p (a b) t -> p a (b t)", b=3), ps[:, 4:6, 0:3 * P])\
                .then_inc(e_hTk.sem, 1)
            if not last:
                meta_dve(dve, b + 2, q + (r + 2) // RING, (r + 2) % RING, first)
            wait(dve, e_down, b)
            wait(dve, meta, b)
            V.tensor_scalar(ys[r], ps[:, 6, 0:D], gate_s[r], None, ALU.mult).then_inc(e_y.sem, 1)

        def tables_dve(dve):
            n = [0]

            def step(ins):
                n[0] += 1
                ins.then_inc(s_tab, 1)
                dve.wait_ge(s_tab, n[0])

            r1 = run[0:1, :]
            first = caps[0:1, :]
            wait(dve, gsteps, NB - 1)
            wait(dve, xn_d, NB - 1)
            step(V.tensor_copy(pad_of, r1))
            step(V.tensor_tensor(cnt, r1, first, ALU.subtract))
            step(V.tensor_scalar(cnt, cnt, float(P - 1), None, ALU.add))
            step(V.tensor_copy(cnti, cnt))
            step(V.tensor_scalar(cnti, cnti, 7, None, ALU.arith_shift_right))
            step(V.tensor_copy(nblk, cnti))
            step(V.tensor_tensor_scan(out=lastb, data0=nblk, data1=nblk, initial=0.0, op0=ALU.add, op1=ALU.bypass))
            step(V.tensor_tensor(firstb, lastb, nblk, ALU.subtract))
            step(V.scalar_tensor_tensor(out=rowv, in0=firstb, scalar=-float(P), in1=first, op0=ALU.mult, op1=ALU.add))
            bb = blockno.unsqueeze(2).broadcast_to([1, NSB, EXP])
            over = lambda v: v.unsqueeze(1).broadcast_to([1, NSB, EXP])
            step(V.tensor_tensor(ge_end, bb, over(lastb), ALU.is_ge))
            step(V.tensor_tensor(ge_first, bb, over(firstb), ALU.is_ge))
            step(V.tensor_reduce(eno, ge_end, AX.X, ALU.add))
            step(V.tensor_scalar(eno, eno, float(EXP - 1), None, ALU.min))
            step(V.tensor_copy(expert_of, eno))
            step(V.tensor_tensor(ge_first, ge_first, ge_end, ALU.subtract))
            step(V.tensor_tensor(ge_first, ge_first, over(rowv), ALU.mult))
            step(V.tensor_reduce(sno, ge_first, AX.X, ALU.add))
            past = ge_end[:, :, EXP - 1]
            step(V.tensor_scalar(eno, past, -1.0, 1.0, ALU.mult, ALU.add))
            step(V.tensor_tensor(eno, eno, blockno, ALU.mult))
            step(V.scalar_tensor_tensor(out=sno, in0=eno, scalar=float(P), in1=sno, op0=ALU.mult, op1=ALU.add))
            step(V.scalar_tensor_tensor(out=sno, in0=past, scalar=float(EXP * CAP), in1=sno, op0=ALU.mult, op1=ALU.add))
            step(V.tensor_copy(slot_of, sno))
            dve.sem_inc(s_tables, 1)

        def gating_dve(dve, i, q, j):
            n = [0]

            def step(ins):
                n[0] += 1
                ins.then_inc(gsteps.sem, 1)
                wait(dve, gsteps, i, n[0])

            Hi = H[:, bass.ds(i * TPB, TPB), :]
            for t in range(TPB):
                last = V.bn_stats(stD[:, t, :], H[:, bass.ds(i * TPB + t, 1), :].rearrange("p t f -> p (t f)"))
            last.then_inc(st_d.sem, 1)
            wait_alone(dve, st_d, i)
            for t in range(TPB):
                last = V.bn_aggr(mvD[:, t, :], stD[:, t, :])
            last.then_inc(mv_d.sem, 1)
            wait(dve, mv_d, i)
            V.tensor_scalar(pvD[:, 0, :], mvD[:, :, 1], EPS, None, ALU.add)
            V.tensor_scalar(pvD[:, 1, :], mvD[:, :, 1], 1.0 + EPS, EPS * EPS, ALU.mult, ALU.add)\
                .then_inc(pv_d.sem, 1)
            wait(dve, rs_d, i)
            wait(dve, sent[j], q - 1)
            for t in range(TPB):
                last = V.tensor_scalar(send[j][:, t, 0, 0:D], H[:, bass.ds(i * TPB + t, 1), :].rearrange("p t f -> p (t f)"),
                                       mvD[:, t, 0:1], rsD[:, 1, t:t + 1], ALU.subtract, ALU.mult)
            last.then_inc(xn_d.sem, 1)
            wait(dve, res_d, i - 1)
            for t in range(TPB):
                V.tensor_scalar(xrD[:, t, :], H[:, bass.ds(i * TPB + t, 1), :].rearrange("p t f -> p (t f)"),
                                mvD[:, t, 0:1], rsD[:, 0, t:t + 1], ALU.subtract, ALU.mult).then_inc(res_d.sem, 1)
            wait(dve, res_d, i, TPB)
            V.tensor_tensor(Hi, Hi, xrD, ALU.add).then_inc(res_d.sem, 1)
            wait(dve, lg_ready, i)
            step(V.tensor_copy(lg, ps[:, 2, 0:TPB * EXP].rearrange("p (t e) -> p t e", t=TPB)))
            step(V.tensor_reduce(lmax, lg, AX.X, ALU.max))
            step(V.tensor_tensor(lg, lg, lmax.unsqueeze(2).broadcast_to([P, TPB, EXP]), ALU.subtract))
            wait(dve, gexp, i)
            step(V.tensor_reduce(psm, pr, AX.X, ALU.add))
            step(V.reciprocal(psm, psm))
            step(V.tensor_tensor(pr, pr, psm.unsqueeze(2).broadcast_to([P, TPB, EXP]), ALU.mult))
            pe_ = pr.unsqueeze(3).broadcast_to([P, TPB, EXP, EXP])
            pj_ = pr.unsqueeze(2).broadcast_to([P, TPB, EXP, EXP])
            step(V.tensor_tensor(cmp1, pj_, pe_, ALU.is_gt))
            step(V.tensor_tensor(cmp2, pj_, pe_, ALU.is_equal))
            step(V.tensor_tensor(cmp2, cmp2, tri.unsqueeze(1).broadcast_to([P, TPB, EXP, EXP]), ALU.mult))
            step(V.tensor_tensor(cmp1, cmp1, cmp2, ALU.add))
            step(V.tensor_reduce(rank, cmp1, AX.X, ALU.add))
            for k in range(TOPK):
                step(V.tensor_scalar(pick_k[:, k, :, :], rank, float(k), None, ALU.is_equal))
            step(V.tensor_tensor(sel, pick_k[:, 0, :, :], pick_k[:, 1, :, :], ALU.add))
            assert n[0] == SEL_STEP
            step(V.tensor_tensor(wk, pick_k, pr.unsqueeze(1).broadcast_to([P, TOPK, TPB, EXP]), ALU.mult))
            step(V.tensor_reduce(gk, wk, AX.X, ALU.add))
            step(V.tensor_tensor(psm, gk[:, 0, :], gk[:, 1, :], ALU.add))
            step(V.reciprocal(psm, psm))
            for k in range(TOPK):
                V.tensor_tensor(send[j][:, :, k, D], gk[:, k, :], psm, ALU.mult)
                V.tensor_copy(send[j][:, :, k, D + 1], tokno)
            wait(dve, pos_ready, i)
            step(V.tensor_tensor(pos, ps[:, 3, 0:TPB * EXP].rearrange("p (t e) -> p t e", t=TPB),
                                 run.unsqueeze(1).broadcast_to([P, TPB, EXP]), ALU.add))
            V.tensor_scalar(tokno, tokno, float(BT), None, ALU.add)
            V.tensor_tensor(run, run, ps[:, 3, TPB * EXP:(TPB + 1) * EXP], ALU.add)
            step(V.tensor_tensor(wk, pick_k, pos.unsqueeze(1).broadcast_to([P, TOPK, TPB, EXP]), ALU.mult))
            step(V.tensor_reduce(sk, wk, AX.X, ALU.add))
            step(V.tensor_copy(slots_i[j], sk))
            assert n[0] == NG

        @block.vector
        def _(dve):
            V.memset(ones[:, :], 1.0).then_inc(s_setup, 1)
            for j in (0, 1):
                V.memset(nrm[j][:, :, D:D + 1], 1.0)
            V.memset(ps[:, 4:6, 0:D], 0.0).then_inc(s_zero, 1)
            dve.wait_ge(s_const, 16 * 7)
            with dve.Fori(0, NB // 2) as ii:
                for j in (0, 1):
                    i = 2 * ii + j
                    wait(dve, tok_loaded[j], ii)
                    for t in range(TPB):
                        last = V.bn_stats(stA[:, t, :], tok[j][:, t, :])
                    last.then_inc(stats_a.sem, 1)
                    wait_alone(dve, stats_a, i)
                    for t in range(TPB):
                        last = V.bn_aggr(mvA[:, t, :], stA[:, t, :])
                    last.then_inc(mv_a.sem, 1)
                    wait(dve, mv_a, i)
                    wait(dve, rstd_a, i - 1)
                    V.tensor_scalar(veA, mvA[:, :, 1], EPS, None, ALU.add).then_inc(var_a.sem, 1)
                    wait(dve, rstd_a, i)
                    wait(dve, outer_a, i - 2)
                    wait(dve, nrmT_a, i - 2)
                    for t in range(TPB):
                        last = V.tensor_scalar(nrm[j][:, t, 0:D], tok[j][:, t, :], mvA[:, t, 0:1],
                                               rsA[j][:, t:t + 1], ALU.subtract, ALU.mult)
                    last.then_inc(nrm_a.sem, 1)
            setup_dve(dve)
            att_dve(dve, 0)
            with dve.Fori(0, NB - 1) as i:
                body_b_dve(dve, i)
            body_b_dve(dve, NB - 1, False)
            dve.wait_ge(s_wc2, 16 * 4)
            dve.wait_ge(s_wc, 16 * 12)
            for buf in dA:
                V.memset(buf[:, :, :, 0:1], 0.0)
            V.memset(xnT[:, :, :, 0:TAPS // 2], 0.0)
            V.memset(xnT[:, :, :, TAPS // 2 + SEQ:PADX], 0.0)
            V.memset(xi[:, :, :, 0:CTAPS - 1], 0.0)
            V.tensor_tensor(wconv[:, :, TAPS // 2, :], wconv[:, :, TAPS // 2, :], wgcn, ALU.add)
            V.tensor_tensor(xgb, gcb, cvb, ALU.add)
            V.tensor_tensor(gateb, ggb, gmb, ALU.add)
            V.tensor_copy(pick[:, :, :], pick32[:, :].unsqueeze(2).broadcast_to([KP, 32, P]))
            dve.wait_ge(s_cact, 1)
            V.tensor_scalar(nega[:, :, :], nega[:, :, :], -1.0, None, ALU.mult).then_inc(s_cset, 1)
            front_dve(dve, 0, 0)
            body_dve(dve, 0, 0, back=False)
            with dve.Fori(0, NB // 2 - 1) as ii:
                for j in (1, 0):
                    body_dve(dve, 2 * ii + (1 if j else 2), j)
            body_dve(dve, NB - 1, 1, front=False)
            xr_dve(dve, NB - 1, 1)
            fuse_dve(dve, NB - 1, 1)
            out_dve(dve, NB - 1, last=True)
            onorm_dve(dve, NB - 1)
            wait(dve, tail_o, NB - 1)
            dve.wait_ge(s_wd, 16 * 9)
            with dve.Fori(0, NB // 2) as q:
                for j in (0, 1):
                    gating_dve(dve, 2 * q + j, q, j)
            tables_dve(dve)
            for j in (0, 1):
                meta_dve(dve, j, 0, j, first=True)
            for j in range(RING):
                expert_dve(dve, j, 0, j, first=j + 2 < RING)
            with dve.Fori(1, NSB // RING - 1) as q:
                for j in range(RING):
                    expert_dve(dve, RING * q + j, q, j)
            for j in range(RING):
                expert_dve(dve, NSB - RING + j, NSB // RING - 1, j, last=j + 2 >= RING)


def kernel(**inputs):
    import numpy as np
    import concourse.bacc as bacc
    from concourse.bass_utils import run_bass_kernel_spmd

    a = {k: np.asarray(v) for k, v in inputs.items()}

    def halves(w, tail):
        return w.reshape(KT, KP, *tail).swapaxes(0, 1)

    def tiles(w, n, tail):
        return w.reshape(n, P, *tail).swapaxes(0, 1)

    col = lambda v: v.reshape(KT, KP).T
    ch = lambda v: v.reshape(DT3, P).T
    freqs = 10000.0 ** (-np.arange(0, D, 2, dtype=np.float32) / np.float32(D))
    ang = np.arange(SEQ, dtype=np.float32)[:, None] * freqs[None].astype(np.float32)
    rope = np.concatenate([np.sin(ang), np.cos(ang)], axis=-1).astype(np.float32)
    widths, ratios = (96, 144, 192), (2, 3, 4)
    mask_in = np.array([[float(x < w) for x in range(D)] for w in widths for _ in ratios], np.float32)
    mask_out = np.array([[float(x < w * r) for x in range(FF)] for w in widths for r in ratios], np.float32)
    heads = lambda w: w.reshape(HEADS, DTR, -1).swapaxes(0, 1)
    xp = a["L1_attn_m_xproj_w"]
    bcw = xp[:, RANK:]
    ae, ar = a["L0_ffn_alpha_e"], a["L0_ffn_alpha_r"]
    arrays = {
        "ids": a["x"].reshape(NT, P).T,
        "wte": a["L0_tok_wte"],
        "ident": np.eye(P, dtype=np.float32),
        "mhalf": np.full((P, 8), -0.5, np.float32),
        "va_fm": np.concatenate([col(a[k]) for k in ("L0_tok_ln_w", "L0_tok_ln_b", "L1_ffn_ln_gamma",
                                                     "L1_ffn_ln_beta")], axis=1),
        "b_fc": a["L0_ffn_b_fc"].reshape(FT, P).T,
        "alphas": np.stack([np.broadcast_to(ae[:, None], (3, 3)).reshape(9),
                            np.broadcast_to(ar[None], (3, 3)).reshape(9)], axis=1),
        "ln_b_row": a["L0_tok_ln_b"].reshape(1, D),
        "b_proj_row": a["L0_ffn_b_proj"].reshape(1, D),
        "WpT": halves(a["L0_tok_W_proj"].T, (HD,)),
        "WvT": halves(a["L0_tok_W_val"].T, (HD,)),
        "WpH": heads(a["L0_tok_W_proj"]),
        "WoH": heads(a["L0_tok_W_out"].T),
        "traceT": a["L0_tok_trace0"].transpose(2, 0, 1),
        "mask_in": mask_in,
        "mask_out": mask_out,
        "rope": halves(rope.T, (SEQ,)),
        "W0T": halves(a["L0_ffn_w_fc"].T, (FF,)),
        "W1T": tiles(a["L0_ffn_w_proj"].T, FT, (D,)),
        "Wv": halves(a["L0_attn_Wv"].T, (KV,)),
        "Wo": a["L0_attn_Wo"].T,
        "wconv": a["L1_attn_conv_w"].transpose(1, 2, 0).reshape(KT, KP, TAPS, D).swapaxes(0, 1),
        "wgcn": halves(a["L1_attn_gcn_w"], (D,)),
        "win": halves(a["L1_attn_m_in_w"], (2 * DI,)),
        "wxp": tiles(np.concatenate([bcw, bcw, bcw, xp[:, :RANK]], axis=1), DT3, (3 * 32 + RANK,)),
        "wdt": a["L1_attn_m_dt_w"],
        "wmo": tiles(a["L1_attn_m_out_w"], DT3, (D,)),
        "wgg": halves(a["L1_attn_gate_gcn_w"], (D,)),
        "wgm": halves(a["L1_attn_gate_mamba_w"], (D,)),
        "wout": halves(a["L1_attn_out_w"], (D,)),
        "pick": np.tile(np.eye(32, dtype=np.float32), (3, 1)),
        "vc_fm": np.concatenate([col(a["L1_attn_" + k]) for k in (
            "norm1_w", "norm1_b", "gcn_b", "conv_b", "gate_gcn_b", "gate_mamba_b")], axis=1),
        "vc_ch": np.concatenate([a["L1_attn_m_conv_w"].reshape(DT3, P, CTAPS).swapaxes(0, 1).reshape(P, -1),
                                 ch(a["L1_attn_m_conv_b"]), ch(a["L1_attn_m_dt_b"]), ch(a["L1_attn_m_D"])], axis=1),
        "A_log": tiles(a["L1_attn_m_A_log"], DT3, (NS,)),
        "n2w": a["L1_attn_norm2_w"],
        "n2b": a["L1_attn_norm2_b"],
        "outb": a["L1_attn_out_b"],
        "router": halves(a["L1_ffn_router_w"], (EXP,)),
        "tri": np.broadcast_to(np.tril(np.ones((EXP, EXP), np.float32), -1), (P, EXP, EXP)),
        "w1": a["L1_ffn_w1"].reshape(EXP, KT, KP, FF).transpose(2, 0, 1, 3),
        "w2": a["L1_ffn_w2"].reshape(EXP, FT, P, D).transpose(2, 0, 1, 3),
        "below": np.triu(np.ones((P, P), np.float32), 1),
        "allones": np.ones((P, P), np.float32),
        "tokno": (np.arange(TPB) * P + np.arange(P)[:, None]).astype(np.float32),
        "first_slots": np.broadcast_to((np.arange(EXP) * CAP).astype(np.float32), (P, EXP)),
        "padrow": np.concatenate([np.zeros((P, D + 1), np.float32),
                                  (T + np.arange(P, dtype=np.float32))[:, None]], axis=1),
        "blockno": np.arange(NSB, dtype=np.float32)[None],
    }
    nc = bacc.Bacc("TRN2", target_bir_lowering=False, num_devices=1)
    arrays = {k + "_dram": np.ascontiguousarray(v) for k, v in arrays.items()}
    aps = {k[:-5]: nc.dram_tensor(k, v.shape, mybir.dt.from_np(v.dtype), kind="ExternalInput").ap()
           for k, v in arrays.items()}
    out = nc.dram_tensor("out_dram", (T + P, D), F32, kind="ExternalOutput").ap()
    build(nc, aps, out)
    r = run_bass_kernel_spmd(nc, [arrays], core_ids=[0])
    return r.results[0]["out_dram"][:T].reshape(BATCH, SEQ, D)
```

```python
import concourse.bass as bass
from concourse import mybir
from contextlib import ExitStack

F32 = mybir.dt.float32
BF16 = mybir.dt.bfloat16
I32 = mybir.dt.int32
ACT = mybir.ActivationFunctionType
ALU = mybir.AluOpType
AX = mybir.AxisListType

BATCH, SEQ, D = 32, 256, 192
T = BATCH * SEQ
P = 128
NT = T // P
TPB = 4
BT = TPB * P
NB = T // BT
SETUP_DMAS = 12
SPB = BT // SEQ
KP, KT = 96, 2
HEADS, DTR = 8, 64
HD = HEADS * DTR
KV = 64
FF = 768
FT = FF // P
DI = 384
DT3 = DI // P
NS = 16
HRING = 4
SLOT = [n % HRING for n in range(NS)]
AT = {"norm": 1, "transpose": 4, "in_proj": 5, "silu": 9, "x_proj": 11, "dt": 12, "conv_kept": 13,
      "mamba": 0, "gate": 2, "out": 10, "out_norm": 12}
GCN_AT = {8: 3, 9: 3, 10: 2, 11: 1, 12: 2, 13: 2, 14: 1}
TAIL = 20
RANK = 12
TAPS, CTAPS = 7, 4
LOW = D - P
CPROD = TAPS + (TAPS + 1) // 2
EXP, TOPK = 8, 2
CAP = T + P
NSB = (TOPK * T + EXP * (P - 1)) // P
NSB += -NSB % 4
RING = 4
SENDS = 4
ROW = D + 2
EPS = 1e-5
TRACE_LR, TRACE_DECAY = 0.1, 0.99
CREDIT = 3

PE_STEPS = ["bias_outer", "x1", "update", "readout", "g", "scores", "probT", "b0", "b1", "c0", "c1"]
ACT_STEPS = ["x1", "readout", "g", "exp0", "exp1", "probT"]
DVE_STEPS = ["ones", "sum_row", "alpha", "scaled_mask", "m0w", "m0", "m1w", "m1", "decayed", "trace", "max",
             "negmax", "recip", "prob0", "prob1", "b0", "b1", "w0", "w1"]


def nth(steps, name):
    return steps.index(name) + 1


class Event:

    def __init__(self, sem, per, ahead=CREDIT):
        self.sem, self.per, self.ahead = sem, per, ahead

    def at(self, block, nth=None):
        return (block + self.ahead) * self.per + (self.per if nth is None else nth)


def build(nc, d, out):
    ctx = ExitStack()
    with ctx:
        def sb(name, shape, dt=F32):
            return ctx.enter_context(nc.sbuf_tensor(name, shape, dt))

        def sem(name):
            return ctx.enter_context(nc.semaphore(name))

        events = []

        def event(name, per=1, ahead=CREDIT):
            e = Event(sem(name), per, ahead)
            events.append(e)
            return e

        H = sb("H", [P, NT, D])
        ARENA = 32400
        arena = sb("arena", [P, ARENA])
        top = [0]

        def carve(p, *shape, dt=F32):
            n = 1
            for s in shape:
                n *= s
            words = (n + 1) // 2 if dt == BF16 else n
            at = top[0]
            top[0] += (words + 3) // 4 * 4
            assert top[0] <= ARENA, top[0]
            v = arena[0:p, at:at + words]
            if dt != F32:
                v = v.bitcast(dt)
            if len(shape) == 1:
                return v
            names = "abcd"[:len(shape)]
            kw = {names[q]: shape[q] for q in range(1, len(shape))}
            return v.rearrange(f"p ({' '.join(names)}) -> p {' '.join(names)}", **kw)

        ident = sb("ident", [P, P])
        ps = ctx.enter_context(nc.psum_tensor("ps", [P, 8, 512], F32))

        def tiles_of(bank):
            return ps[:, bank:bank + 2, 0:2 * D]

        def tile_in(bank, t):
            return ps[:, bank + t // 2, (t % 2) * D:(t % 2 + 1) * D]

        exps_half = sb("exps_half", [P, 8])

        wconv = sb("wconv", [P, CPROD, D])
        win_wdt = sb("win_wdt", [P, KT, 2 * DI])
        win = [win_wdt[0:P, 0, :], win_wdt[0:LOW, 1, :]]
        wdt = win_wdt[:, 1, 0:DI]
        wxp = sb("wxp", [P, DT3, 3 * 32 + RANK])
        wmo = sb("wmo", [P, DT3, D])
        wgg = sb("wgg", [KP, KT, D])
        wgm = sb("wgm", [KP, KT, D])
        wout = sb("wout", [KP, KT, D])
        pick32 = sb("pick32", [KP, 32])
        vc = sb("vc", [P, 80])
        n1w, n1b = vc[:, 38:40], vc[:, 40:42]
        gcb, cvb = vc[0:KP, 4:6], vc[0:KP, 6:8]
        ggb, gmb = vc[0:KP, 8:10], vc[0:KP, 10:12]
        cw = vc[:, 12:24].rearrange("p (a b) -> p a b", b=CTAPS)
        cb, dtb, dskip = vc[:, 24:27], vc[:, 27:30], vc[:, 30:33]
        xgb, gateb = vc[0:KP, 34:36], vc[0:KP, 36:38]
        nega = sb("nega", [P, DT3, NS])
        va = sb("va", [P, 40])
        lnw, lnb = va[0:KP, 0:2], va[0:KP, 2:4]
        mow, mob = va[0:KP, 4:6], va[0:KP, 6:8]
        bfc, b0 = va[:, 8:14], va[:, 14:20]
        wa2, wa = va[0:9, 20:22], va[0:9, 22:23]
        lnbrow = sb("lnbrow", [KP + 1, D])
        b1row = sb("b1row", [1, D])
        ones = sb("ones", [1, P])

        s_const = sem("constants_loaded")
        s_wc = sem("phase_c_weights_loaded")
        s_wc2 = sem("phase_c_late_weights_loaded")
        s_wa = sem("setup_weights_loaded")
        s_ids = sem("ids_loaded")
        tok_loaded = [event(f"tok{j}_gathered", 4 * 16, ahead=0) for j in range(2)]
        shifted = [event(f"tok{j}_shifted", 2 * 16) for j in range(2)]
        s_alone = sem("waits_alone")
        s_zero = sem("outer_banks_zero")
        s_setup = sem("setup_steps_vector")
        s_setup_pe = sem("setup_steps_tensor")
        s_setup_act = sem("setup_steps_scalar")
        s_setup_gp = sem("xs_zero_column")

        top[0] = 0
        XT = carve(KP, KT, T)
        w0 = carve(KP, KT, FF)
        w1 = carve(P, FT, D)
        base_b = top[0]
        ids = carve(P, NT, dt=I32)
        tok = [carve(P, TPB, D) for _ in range(2)]
        tok2 = [carve(P, TPB, D) for _ in range(2)]
        nrm = [carve(P, TPB, D + 1) for _ in range(2)]
        stA = carve(P, TPB, 6)
        mvA = carve(P, TPB, 2)
        veA = carve(P, TPB)
        rsA = [carve(P, TPB) for _ in range(2)]
        WpT = carve(KP, KT, HD)
        WvT = carve(KP, KT, HD)
        WpH = carve(DTR, HEADS, D)
        WoH = carve(DTR, HEADS, D)
        tr = carve(DTR, HEADS, DTR)
        MS = carve(KP, KT, D)
        srow = carve(KP + 1, D)
        X1 = WpT
        minp = carve(9, D)
        mins = carve(9, D)
        mout = carve(9, FF)
        rope = carve(KP, KT, SEQ)
        smax = carve(P, 2)
        ssum = carve(P, 2)
        prob = tok[0].rearrange("p a b -> p (a b)")[:, 0:2 * SEQ].rearrange("p (q k) -> p q k", q=2)

        idn = [sb(f"idn{j}", [P, TPB], I32)[:, :] for j in range(2)]
        ids_staged = [event(f"ids_staged{j}") for j in range(2)]
        stats_a = event("stats_a")
        mv_a = event("mean_var_a")
        var_a = event("variance_a")
        rstd_a = event("rstd_a")
        nrm_a = event("normed_a")
        nrmT_a = event("transposed_a")
        xt_a = event("xt_stored_a")
        outer_a = event("outer_product_a")

        g_wv = sb("g_wv", [P, KT * (D + KV)])
        G = g_wv[0:KP, 0:KT * D].rearrange("p (k f) -> p k f", k=KT)
        PT = sb("PT", [P, 2, SEQ])
        wv = g_wv[0:KP, KT * D:KT * (D + KV)].rearrange("p (k f) -> p k f", k=KT)
        wo = sb("wo", [KV, D])
        top[0] = base_b
        xs = carve(KP, KT, SPB, SEQ)
        h0c = carve(P, TPB, D)
        hA = [carve(P, TPB, D) for _ in range(2)]
        xn1 = carve(P, TPB, D)
        xn2 = carve(P, TPB, D)
        x1T = carve(KP, KT, BT)
        x2T = carve(KP, KT, BT)
        vs = carve(P, TPB, KV)
        oTs = carve(KV, BT)
        hT = carve(P, FT, BT)
        b1b = carve(P, D)
        stB = carve(P, TPB, 6)
        mvB = carve(P, TPB, 2)
        veB = carve(P, TPB)
        rsB = carve(P, TPB)

        xs_loaded = event("xs_loaded", 16 * KT)
        h0_ready = event("h0_ready")
        h0_kept = event("h0_kept")
        t1_ready = event("t1_ready")
        x1T_kept = event("x1T_kept")
        v_ready = event("v_ready")
        v_kept = event("v_kept")
        oT_ready = event("oT_ready")
        oT_kept = event("oT_kept")
        att_ready = event("att_ready")
        hA_kept = event("hA_kept")
        st_b = event("stats_b", 2)
        mv_b = event("mean_var_b", 2)
        ve_b = event("var_eps_b", 2)
        rs_b = event("rstd_b", 2)
        biased = event("output_bias_added")
        s_b1 = sem("output_bias_spread")
        s_b1b = sem("output_bias_kept")
        xn1_kept = event("xn1_kept")
        xn2_kept = event("xn2_kept")
        t2_ready = event("t2_ready")
        x2T_kept = event("x2T_kept")
        up_ready = event("up_ready", FT)
        gelu_kept = event("gelu_kept", FT)
        down_ready = event("down_ready")
        hB_kept = event("hB_kept")

        top[0] = 0
        wgcn = carve(P, 2, D)
        n2w, n2b, outb = (carve(P, D) for _ in range(3))
        pick = carve(KP, 32, dt=BF16)
        dtp = [carve(P, DT3, BT) for _ in range(2)]
        up_ = [carve(P, DT3, BT) for _ in range(2)]
        xm = [carve(P, DT3, BT) for _ in range(2)]
        zs = [carve(P, DT3, BT) for _ in range(2)]
        xg = [carve(KP, KT, BT) for _ in range(2)]
        xnC = carve(P, TPB, 2 * P)
        PADX = SEQ + TAPS - 1
        xnT = carve(P, 2, SPB, PADX)
        PADC = SEQ + CTAPS - 1
        xi = carve(P, DT3, SPB, PADC)
        bc = [carve(KP, BT, dt=BF16) for _ in range(2)]
        xr = carve(P, TPB, D)
        flat = lambda v: v.rearrange("p a b -> p (a b)")
        rest = flat(xr)[0:KP, 0:BT]
        mid = flat(xr)[0:KP, BT:BT + BT // 2].bitcast(BF16)
        sp1 = carve(P, DT3, BT)
        dA = [carve(P, DT3, SPB, SEQ) for _ in range(2)]
        hs = [carve(P, DT3, BT) for _ in range(HRING)]
        bs = [PT[:, :, :].rearrange("p a b -> p (a b)"), g_wv[:, :]]
        xmb_dtl = carve(P, KT, BT)
        xmb = xmb_dtl[0:KP]
        dtl = xmb_dtl[:, 0, :]
        gate = sp1[0:KP, 0:KT, :]
        o = xnC.rearrange("p t f -> p (t f)")[:, 0:TPB * D].rearrange("p (t f) -> p t f", t=TPB)
        stC = carve(P, TPB, 6)
        mvC = [carve(P, TPB, 2) for _ in range(2)]
        pvC = carve(P, 2, TPB)
        rsC = [carve(P, 2, TPB) for _ in range(2)]
        stO = carve(P, TPB, 6)
        mvO = carve(P, TPB, 2)
        veO = carve(P, TPB)
        rsO = carve(P, TPB)
        s_cset = sem("phase_c_ready")
        s_cact = sem("decay_rates_exp")

        st_c = event("stats_c")
        mv_c = event("mean_var_c")
        pv_c = event("var_eps_c")
        rs_c = event("rstd_c")
        xn_c = event("xn_c")
        xnT_ready = event("xnT_ready")
        xnT_kept = event("xnT_kept", 3)
        in_ready = event("in_proj_ready", 2 * DT3)
        in_kept = event("in_proj_kept", 2 * DT3)
        conv_ch = event("channel_conv", DT3 * CTAPS)
        silu_kept = event("silu_kept", 2 * DT3)
        xp_ready = event("x_proj_ready")
        dtl_kept = event("dt_low_kept")
        split = event("bc_split", 5)
        dt_ready = event("dt_ready", DT3)
        sp_abs = event("softplus_abs", DT3)
        sp_exp = event("softplus_exp", DT3)
        sp_log = event("softplus_log")
        sp_max = event("softplus_max", DT3)
        dt_kept = event("dt_kept")
        u_kept = event("u_kept")
        gcn_ready = event("gcn_ready", KT)
        gcn_kept = event("gcn_kept", KT)
        b_ready = event("b_broadcast", NS)
        c_ready = event("c_broadcast", NS)
        da_ready = event("decay_ready", NS * DT3)
        b_copied = event("b_copied", NS)
        dbx = event("dbx_tile_0", NS)
        dbx_gp = event("dbx_other_tiles", NS)
        scan = event("scan", NS)
        hc = event("h_times_c", NS)
        nsum = event("state_sum", NS)
        ysk = event("y_skip", DT3)
        yz = event("y_gated")
        mo_ready = event("mamba_out_ready", KT)
        mo_kept = event("mamba_out_kept", KT)
        gt_ready = event("gate_ready", KT)
        gt_kept = event("gate_kept", KT)
        gt_tanh = event("gate_tanh", KT)
        fuse = event("fuse", 3)
        out_ready = event("out_ready")
        o_kept = event("o_kept", 3)
        st_o = event("stats_o")
        mv_o = event("mean_var_o")
        ve_o = event("var_eps_o")
        rs_o = event("rstd_o")
        on_o = event("o_normed")
        tail_o = event("o_affine", 3)

        top[0] = 0
        w1e = carve(KP, EXP, KT, FF)
        w2e = carve(P, EXP, FT, D)
        rout = carve(KP, KT, EXP)
        tri = carve(P, EXP, EXP)
        below = carve(P, P)
        allones = carve(P, P)
        tokno = carve(P, TPB)
        run = carve(P, EXP)
        caps = carve(P, EXP)
        padrow = carve(P, ROW)
        expert_of = carve(1, NSB, dt=I32)
        slot_of = carve(1, NSB, dt=I32)
        pad_of = carve(1, EXP, dt=I32)
        blockno = carve(1, NSB)
        base_d = top[0]
        hS = [carve(P, FF) for _ in range(2)]
        hTs = [carve(P, FT, P) for _ in range(2)]
        xt = [carve(P, ROW) for _ in range(RING)]
        xT = [carve(KP, KT, P) for _ in range(2)]
        ys = [carve(P, D) for _ in range(RING)]
        gate_s = [carve(P, 1) for _ in range(RING)]
        tok_s = [carve(P, 1, dt=I32) for _ in range(RING)]
        top[0] = base_d
        growD = [carve(P, TPB) for _ in range(2)]
        shiftD = [carve(P, TPB) for _ in range(2)]
        stD = carve(P, TPB, 6)
        mvD = [carve(P, TPB, 2) for _ in range(2)]
        pvD = carve(P, 2, TPB)
        rsD = [carve(P, 2, TPB) for _ in range(2)]
        lg = carve(P, TPB, EXP)
        lmax = carve(P, TPB)
        pr = carve(P, TPB, EXP)
        psm = carve(P, TPB)
        cmp1 = carve(P, TPB, EXP, EXP)
        cmp2 = carve(P, TPB, EXP, EXP)
        rank = carve(P, TPB, EXP)
        pick_k = carve(P, TOPK, TPB, EXP)
        sel5 = carve(P, TPB + 1, EXP)
        sel = sel5[:, 0:TPB, :]
        pos = carve(P, TPB, EXP)
        gk = carve(P, TOPK, TPB)
        wk = carve(P, TOPK, TPB, EXP)
        sk = carve(P, TOPK, TPB)
        xTs = carve(KP, KT, BT)
        top[0] = max(top[0], base_d + 2 * NSB * (EXP + 1) + 8 * EXP)
        send_at = top[0]
        send = [carve(P, TPB, TOPK, ROW) for _ in range(SENDS)]
        slots_i = [carve(P, TOPK, TPB, dt=I32) for _ in range(SENDS)]
        top[0] = base_d
        cnt = carve(1, EXP)
        cnti = carve(1, EXP, dt=I32)
        nblk = carve(1, EXP)
        lastb = carve(1, EXP)
        firstb = carve(1, EXP)
        rowv = carve(1, EXP)
        ge_end = carve(1, NSB, EXP)
        ge_first = carve(1, NSB, EXP)
        eno = carve(1, NSB)
        sno = carve(1, NSB)
        assert top[0] <= send_at
        slots = nc.dram_tensor("slots_scratch", (EXP * CAP + P, ROW), F32).ap()

        s_wd = sem("router_loaded")
        s_we = sem("experts_loaded")
        st_d = event("stats_d")
        mv_d = event("mean_var_d")
        pv_d = event("var_eps_d")
        rs_d = event("rstd_d")
        xn_d = event("xn_d")
        xn2_d = event("xn_copied")
        dT_ready = event("dT_ready")
        dT_kept = event("dT_kept", KT)
        lg_ready = event("logits_ready")
        NG = 22
        SEL_STEP = 14
        gsteps = event("routing_steps", NG)
        gexp = event("routing_exp")
        pos_ready = event("positions_ready")
        res_d = event("residual_d", TPB)
        coef_d = event("residual_coefficients_d", 2)
        res_out = event("residual_stored", 16)
        sent = [event(f"slots{j}_written", TOPK * TPB * 16, ahead=0) for j in range(SENDS)]
        s_tab = sem("table_steps")
        s_tables = sem("tables_ready")
        s_pads = sem("padding_written")
        xt_loaded = [event(f"slot_rows{j}_loaded", 16) for j in range(RING)]
        xt_T = event("slot_rows_transposed", ahead=RING)
        xT_kept = event("slot_T_kept", KT)
        meta = event("slot_gate_token_kept", 2, ahead=RING)
        e_up = event("expert_up")
        e_silu = event("expert_silu")
        e_hT = event("hidden_transposed")
        e_hTk = event("hidden_T_kept")
        e_down = event("expert_down")
        e_y = event("gated_output")
        added = event("outputs_added", 16, ahead=0)

        block = ctx.enter_context(nc.Block())
        V = nc.vector


        def shift(sp, i, q, j):
            sp.wait_ge(tok_loaded[j].sem, tok_loaded[j].at(q))
            sp.sem_inc(s_alone, 1)
            sp.wait_ge(outer_a.sem, outer_a.at(i - 2))
            sp.sem_inc(s_alone, 1)
            sp.dma_start(tok2[j][0:P - 2, :, :], tok[j][2:P, :, :]).then_inc(shifted[j].sem, 16)
            sp.dma_start(tok2[j][P - 2:P, 0:TPB:2, :], tok[j][0:2, 1:TPB:2, :]).then_inc(shifted[j].sem, 16)

        def load_xs(sp, i):
            sp.wait_ge(h0_ready.sem, h0_ready.at(i - 1))
            sp.sem_inc(s_alone, 1)
            for k in range(KT):
                sp.dma_start(xs[:, k, :, 1:SEQ],
                             XT[:, k, bass.ds(i * BT, BT)].rearrange("p (s t) -> p s t", s=SPB)[:, :, 0:SEQ - 1])\
                    .then_inc(xs_loaded.sem, 16)

        @block.sync
        def _(sp):
            sp.dma_start(ids, d["ids"]).then_inc(s_ids, 16)
            sp.dma_start(ident[:, :], d["ident"]).then_inc(s_const, 16)
            sp.dma_start(exps_half[:, :], d["mhalf"]).then_inc(s_const, 16)
            sp.dma_start(va[0:KP, 0:8], d["va_fm"]).then_inc(s_const, 16)
            sp.dma_start(va[:, 8:14], d["b_fc"]).then_inc(s_const, 16)
            sp.dma_start(wa2, d["alphas"]).then_inc(s_const, 16)
            sp.dma_start(lnbrow[KP:KP + 1, :], d["ln_b_row"]).then_inc(s_const, 16)
            sp.dma_start(b1row[:, :], d["b_proj_row"]).then_inc(s_const, 16)
            for dst, name in ((WpT, "WpT"), (WvT, "WvT"), (WpH, "WpH"), (WoH, "WoH"), (tr, "traceT"),
                              (minp, "mask_in"), (mout, "mask_out"), (rope, "rope"), (w0, "W0T"), (w1, "W1T")):
                sp.dma_start(dst, d[name]).then_inc(s_wa, 16)
            sp.dma_start(wv[:, :, :], d["Wv"]).then_inc(s_wa, 16)
            sp.dma_start(wo[:, :], d["Wo"]).then_inc(s_wa, 16)
            with sp.Fori(0, NB // 2) as q:
                for j in (0, 1):
                    shift(sp, 2 * q + j, q, j)
            sp.dma_start(win[0], d["win"][0:P, :]).then_inc(s_wc, 16)
            sp.dma_start(win[1], d["win"][P:D, :]).then_inc(s_wc, 16)
            sp.dma_start(vc[:, 38:42], d["norm1"]).then_inc(s_wc, 16)
            for dst, name in ((wconv, "wconv"), (wxp, "wxp"), (wmo, "wmo"), (wgg, "wgg"),
                              (wgm, "wgm"), (wout, "wout")):
                sp.dma_start(dst[:, :] if len(dst.shape) == 2 else
                             (dst[:, :, :] if len(dst.shape) == 3 else dst[:, :, :, :]),
                             d[name]).then_inc(s_wc, 16)
            sp.dma_start(wdt[96:96 + RANK, :], d["wdt"]).then_inc(s_wc, 16)
            sp.dma_start(pick32[:, :], d["pick"]).then_inc(s_wc, 16)
            sp.dma_start(vc[0:KP, 4:12], d["vc_fm"]).then_inc(s_wc, 16)
            sp.dma_start(vc[:, 12:33], d["vc_ch"]).then_inc(s_wc, 16)
            sp.dma_start(nega[:, :, :], d["A_log"]).then_inc(s_wc, 16)
            sp.wait_ge(s_setup_gp, 1)
            load_xs(sp, 0)
            with sp.Fori(1, NB) as i:
                load_xs(sp, i)
            sp.wait_ge(hB_kept.sem, hB_kept.at(NB - 1))
            sp.sem_inc(s_alone, 1)
            sp.dma_start(wgcn, d["wgcn"]).then_inc(s_wc2, 16)
            for dst, name in ((n2w, "n2w"), (n2b, "n2b"), (outb, "outb")):
                sp.dma_start(dst, d[name].partition_broadcast(P)).then_inc(s_wc2, 16)
            sp.wait_ge(tail_o.sem, tail_o.at(NB - 1))
            sp.sem_inc(s_alone, 1)
            for dst, name in ((rout, "router"), (tri, "tri"), (below, "below"), (allones, "allones"),
                              (tokno, "tokno"), (run, "first_slots"), (caps, "first_slots"),
                              (padrow, "padrow"), (blockno, "blockno")):
                sp.dma_start(dst, d[name]).then_inc(s_wd, 16)
            sp.dma_start(w1e, d["w1"]).then_inc(s_we, 16)
            sp.dma_start(w2e, d["w2"]).then_inc(s_we, 16)
            with sp.Fori(0, NB) as i:
                sp.wait_ge(res_d.sem, res_d.at(i))
                sp.sem_inc(s_alone, 1)
                sp.dma_start(out[bass.ds(i * BT, BT), :].rearrange("(t p) f -> p t f", p=P),
                             H[:, bass.ds(i * TPB, TPB), :]).then_inc(res_out.sem, 16)
            sp.wait_ge(s_tab, 1)
            for e in range(EXP):
                row = sp.value_load(pad_of[0:1, e:e + 1], min_val=0, max_val=EXP * CAP)
                sp.dma_start(slots[bass.ds(row, P), :], padrow).then_inc(s_pads, 16)
            sp.dma_start(slots[EXP * CAP:EXP * CAP + P, :], padrow).then_inc(s_pads, 16)
            sp.wait_ge(s_pads, 16 * (EXP + 1))
            sp.wait_ge(s_tables, 1)
            for j in range(SENDS):
                sp.wait_ge(sent[j].sem, sent[j].at(NB // SENDS - 1))
                sp.sem_inc(s_alone, 1)
            with sp.Fori(0, NSB // RING) as q:
                for j in range(RING):
                    b = RING * q + j
                    sp.wait_ge(xt_T.sem, xt_T.at(b - RING))
                    sp.sem_inc(s_alone, 1)
                    sp.wait_ge(meta.sem, meta.at(b - RING))
                    sp.sem_inc(s_alone, 1)
                    row = sp.value_load(slot_of[0:1, bass.ds(b, 1)], min_val=0, max_val=EXP * CAP)
                    sp.dma_start(xt[j], slots[bass.ds(row, P), :]).then_inc(xt_loaded[j].sem, 16)
            sp.wait_ge(added.sem, added.at(NSB - 1))

        def inv_root_a(gp, i, j):
            gp.wait_ge(var_a.sem, var_a.at(i))
            gp.wait_ge(nrm_a.sem, nrm_a.at(i - 2))
            nc.gpsimd.tensor_tensor(rsA[j], veA, exps_half[:, 0:TPB], ALU.pow).then_inc(rstd_a.sem, 1)

        def root_d(gp, i, p):
            gp.wait_ge(pv_d.sem, pv_d.at(i))
            nc.gpsimd.tensor_tensor(rsD[p], pvD, exps_half[:, 0:8].rearrange("p (a b) -> p a b", a=2),
                                    ALU.pow).then_inc(rs_d.sem, 1)

        def send_slots(gp, i, j):
            gp.wait_ge(gsteps.sem, gsteps.at(i))
            gp.sem_inc(s_alone, 1)
            gp.wait_ge(xn2_d.sem, xn2_d.at(i))
            gp.sem_inc(s_alone, 1)
            for t in range(TPB):
                for k in range(TOPK):
                    gp.indirect_dma_start(
                        out=slots, out_offset=bass.IndirectOffsetOnAxis(ap=slots_i[j][:, k, t:t + 1], axis=0),
                        in_=send[j][:, t, k, :], in_offset=None).then_inc(sent[j].sem, 16)

        def add_outputs(gp, b, j, first=False):
            gp.wait_ge(e_y.sem, e_y.at(b))
            gp.sem_inc(s_alone, 1)
            if not first:
                gp.wait_ge(added.sem, added.at(b - 1))
                gp.sem_inc(s_alone, 1)
            gp.indirect_dma_start(out=out, out_offset=bass.IndirectOffsetOnAxis(ap=tok_s[j], axis=0),
                                  in_=ys[j], in_offset=None, compute_op=ALU.add).then_inc(added.sem, 16)

        def gather(gp, i, q, j):
            gp.wait_ge(nrm_a.sem, nrm_a.at(i - 2))
            gp.wait_ge(shifted[j].sem, shifted[j].at(q - 1))
            nc.gpsimd.tensor_copy(idn[j], ids[:, bass.ds(i * TPB, TPB)]).then_inc(ids_staged[j].sem, 1)
            gp.wait_ge(ids_staged[j].sem, ids_staged[j].at(q))
            gp.sem_inc(s_alone, 1)
            for t in range(TPB):
                gp.indirect_dma_start(
                    out=tok[j][:, t, :], out_offset=None, in_=d["wte"],
                    in_offset=bass.IndirectOffsetOnAxis(ap=idn[j][:, t:t + 1], axis=0))\
                    .then_inc(tok_loaded[j].sem, 16)

        def body_b_gp(gp, i, j):
            for q in (1, 2):
                gp.wait_ge(ve_b.sem, ve_b.at(i, q))
                nc.gpsimd.tensor_tensor(rsB, veB, exps_half[:, 0:TPB], ALU.pow).then_inc(rs_b.sem, 1)
            gp.wait_ge(xn2_kept.sem, xn2_kept.at(i))
            nc.gpsimd.tensor_tensor(hA[j], hA[j], b1b.unsqueeze(1).broadcast_to([P, TPB, D]), ALU.add)\
                .then_inc(biased.sem, 1)

        def rs_c_step(gp, i, j):
            gp.wait_ge(pv_c.sem, pv_c.at(i))
            nc.gpsimd.tensor_tensor(rsC[j], pvC, exps_half[:, 0:8].rearrange("p (a b) -> p a b", a=2),
                                    ALU.pow).then_inc(rs_c.sem, 1)

        def root_o(gp, i):
            gp.wait_ge(ve_o.sem, ve_o.at(i))
            nc.gpsimd.tensor_tensor(rsO, veO, exps_half[:, 0:TPB], ALU.pow).then_inc(rs_o.sem, 1)

        def back_gp(gp, i):
            gp.wait_ge(on_o.sem, on_o.at(i))
            nc.gpsimd.tensor_tensor(o, o, n2w.unsqueeze(1).broadcast_to([P, TPB, D]), ALU.mult)\
                .then_inc(tail_o.sem, 1)
            gp.wait_ge(tail_o.sem, tail_o.at(i, 1))
            nc.gpsimd.tensor_tensor(o, o, n2b.unsqueeze(1).broadcast_to([P, TPB, D]), ALU.add)\
                .then_inc(tail_o.sem, 1)
            gp.wait_ge(tail_o.sem, tail_o.at(i, 2))
            Hi = H[:, bass.ds(i * TPB, TPB), :]
            nc.gpsimd.tensor_tensor(Hi, Hi, o, ALU.add).then_inc(tail_o.sem, 1)

        def free_state(eng, i, n):
            before = [m for m in range(n) if SLOT[m] == SLOT[n]]
            if before:
                eng.wait_ge(nsum.sem, nsum.at(i, before[-1] + 1))
            else:
                eng.wait_ge(nsum.sem, nsum.at(i - 1, max(m for m in range(NS) if SLOT[m] == SLOT[n]) + 1))

        def dbx_step(gp, i, j, n):
            if n == 0:
                gp.wait_ge(u_kept.sem, u_kept.at(i))
            gp.wait_ge(b_copied.sem, b_copied.at(i, n + 1))
            free_state(gp, i, n)
            nc.gpsimd.tensor_tensor(hs[SLOT[n]][:, 1:DT3, :], up_[j][:, 1:DT3, :],
                                    bs[n % 2].unsqueeze(1).broadcast_to([P, DT3 - 1, BT]), ALU.mult)\
                .then_inc(dbx_gp.sem, 1)

        def body_gp(gp, i, j, front=True, back=True):
            for n in range(NS):
                dbx_step(gp, i, j, n)
                if front and n == AT["norm"] + 1:
                    rs_c_step(gp, i + 1, 1 - j)
                if back and n == AT["out_norm"]:
                    root_o(gp, i - 1)
            if back:
                back_gp(gp, i - 1)

        @block.gpsimd
        def _(gp):
            for e in events:
                if e.ahead:
                    gp.sem_inc(e.sem, e.ahead * e.per)
            gp.wait_ge(s_ids, 16)
            for j in (0, 1):
                gather(gp, j, 0, j)
            gp.wait_ge(s_const, 16 * 7)
            with gp.Fori(1, NB // 2) as q:
                for j in (0, 1):
                    inv_root_a(gp, 2 * q - 2 + j, j)
                    gather(gp, 2 * q + j, q, j)
            for j in (0, 1):
                inv_root_a(gp, NB - 2 + j, j)
            gp.wait_ge(s_setup, nth(DVE_STEPS, "w1"))
            nc.gpsimd.memset(xs[:, :, :, 0:1], 0.0).then_inc(s_setup_gp, 1)
            gp.wait_ge(s_b1b, 1)
            with gp.Fori(0, NB // 2) as ii:
                for j in (0, 1):
                    body_b_gp(gp, 2 * ii + j, j)
            rs_c_step(gp, 0, 0)
            body_gp(gp, 0, 0, back=False)
            with gp.Fori(0, NB // 2 - 1) as ii:
                for j in (1, 0):
                    body_gp(gp, 2 * ii + (1 if j else 2), j)
            body_gp(gp, NB - 1, 1, front=False)
            root_o(gp, NB - 1)
            back_gp(gp, NB - 1)
            for i in (0, 1):
                root_d(gp, i, i)
            with gp.Fori(0, NB // SENDS - 1) as q:
                for j in range(SENDS):
                    root_d(gp, SENDS * q + j + 2, j % 2)
                    send_slots(gp, SENDS * q + j, j)
            for j in range(SENDS):
                if j + 2 < SENDS:
                    root_d(gp, NB - SENDS + j + 2, j % 2)
                send_slots(gp, NB - SENDS + j, j)
            gp.wait_ge(res_out.sem, res_out.at(NB - 1))
            for j in range(RING):
                add_outputs(gp, j, j, first=j == 0)
            with gp.Fori(1, NSB // RING) as q:
                for j in range(RING):
                    add_outputs(gp, RING * q + j, j)

        def router_T_pe(pe, i, j):
            pe.wait_ge(xn_d.sem, xn_d.at(i))
            pe.wait_ge(dT_kept.sem, dT_kept.at(i - 1))
            for t in range(TPB):
                for k in range(KT):
                    last = nc.tensor.transpose(ps[0:KP, k, t * P:(t + 1) * P],
                                               send[j][:, t, 0, k * KP:(k + 1) * KP], ident[:, :])
            last.then_inc(dT_ready.sem, 1)

        def logits_pe(pe, i):
            pe.wait_ge(dT_kept.sem, dT_kept.at(i))
            pe.wait_ge(gsteps.sem, gsteps.at(i - 1, 1))
            for t in range(TPB):
                for k in range(KT):
                    last = nc.tensor.matmul(ps[:, 2, t * EXP:(t + 1) * EXP], xTs[:, k, t * P:(t + 1) * P],
                                            rout[:, k, :], start=(k == 0), stop=(k == KT - 1))
            last.then_inc(lg_ready.sem, 1)

        def positions_pe(pe, i):
            pe.wait_ge(gsteps.sem, gsteps.at(i, SEL_STEP))
            pe.wait_ge(gsteps.sem, gsteps.at(i - 1))
            nc.tensor.matmul(ps[:, 3, 0:(TPB + 1) * EXP], below, sel5.rearrange("p t e -> p (t e)"),
                             start=True, stop=False)
            for n in range(1, TPB + 1):
                last = nc.tensor.matmul(ps[:, 3, n * EXP:(TPB + 1) * EXP], allones,
                                        sel5[:, 0:TPB + 1 - n, :].rearrange("p t e -> p (t e)"),
                                        start=False, stop=(n == TPB))
            last.then_inc(pos_ready.sem, 1)

        def slot_transpose(pe, b, q, r):
            pe.wait_ge(xt_loaded[r].sem, xt_loaded[r].at(q))
            pe.wait_ge(xT_kept.sem, xT_kept.at(b - 1))
            for k in range(KT):
                last = nc.tensor.transpose(ps[0:KP, 7, k * P:(k + 1) * P], xt[r][:, k * KP:(k + 1) * KP], ident[:, :])
            last.then_inc(xt_T.sem, 1)

        def expert_up(pe, b, j):
            j = j % 2
            e = pe.value_load(expert_of[0:1, bass.ds(b, 1)], min_val=0, max_val=EXP - 1)
            pe.wait_ge(xT_kept.sem, xT_kept.at(b))
            pe.wait_ge(e_silu.sem, e_silu.at(b - 2))
            for n in range(2):
                for k in range(KT):
                    w = w1e[:, bass.ds(e, 1), k, n * (FF // 2):(n + 1) * (FF // 2)].rearrange("p e f -> p (e f)")
                    last = nc.tensor.matmul(ps[:, 2 * j + n, 0:FF // 2], xT[j][:, k, :], w,
                                            start=(k == 0), stop=(k == KT - 1))
            last.then_inc(e_up.sem, 1)

        def expert_block(pe, b, q, j, last=0):
            h = j % 2
            pe.wait_ge(e_silu.sem, e_silu.at(b))
            pe.wait_ge(e_hTk.sem, e_hTk.at(b - 1))
            for f in range(FT):
                ins = nc.tensor.transpose(ps[:, 4 + f // 3, (f % 3) * P:(f % 3 + 1) * P],
                                          hS[h][:, f * P:(f + 1) * P], ident[:, :])
            ins.then_inc(e_hT.sem, 1)
            if last < 2:
                expert_up(pe, b + 1, j + 1)
            if not last:
                slot_transpose(pe, b + 2, q + (j + 2) // RING, (j + 2) % RING)
            e = pe.value_load(expert_of[0:1, bass.ds(b, 1)], min_val=0, max_val=EXP - 1)
            pe.wait_ge(e_hTk.sem, e_hTk.at(b))
            pe.wait_ge(e_y.sem, e_y.at(b - 1))
            for f in range(FT):
                w = w2e[:, bass.ds(e, 1), f, :].rearrange("p e f -> p (e f)")
                ins = nc.tensor.matmul(ps[:, 6, 0:D], hTs[h][:, f, :], w, start=(f == 0), stop=(f == FT - 1))
            ins.then_inc(e_down.sem, 1)

        def setup_pe(pe):
            steps = iter(PE_STEPS)

            def done(name, ins):
                assert next(steps) == name
                ins.then_inc(s_setup_pe, 1)

            pe.wait_ge(s_setup, nth(DVE_STEPS, "sum_row"))
            for k in range(KT):
                last = nc.tensor.matmul(ps[0:KP, 6, k * D:(k + 1) * D], lnbrow[KP:KP + 1, k * KP:(k + 1) * KP],
                                        srow[KP:KP + 1, :], start=True, stop=True)
            done("bias_outer", last)
            pe.wait_ge(s_wa, 16 * SETUP_DMAS)
            pe.wait_ge(xt_a.sem, xt_a.at(NB - 1))
            pe.wait_ge(s_setup, nth(DVE_STEPS, "m1"))
            for m in range(KT):
                for k in range(KT):
                    last = nc.tensor.matmul(ps[0:KP, m, :], MS[:, k, m * KP:(m + 1) * KP], WpT[:, k, :],
                                            start=(k == 0), stop=(k == KT - 1))
            done("x1", last)
            pe.wait_ge(s_setup_act, nth(ACT_STEPS, "x1"))
            for h in range(HEADS):
                for k in range(KT):
                    last = nc.tensor.matmul(ps[0:DTR, 2, h * DTR:(h + 1) * DTR], WvT[:, k, h * DTR:(h + 1) * DTR],
                                            X1[:, k, h * DTR:(h + 1) * DTR], start=(k == 0), stop=(k == KT - 1))
            done("update", last)
            pe.wait_ge(s_setup, nth(DVE_STEPS, "trace"))
            for h in range(HEADS):
                last = nc.tensor.matmul(ps[0:DTR, 4 + h // 2, (h % 2) * D:(h % 2 + 1) * D], tr[:, h, :],
                                        WoH[:, h, :], start=True, stop=True)
            done("readout", last)
            pe.wait_ge(s_setup_act, nth(ACT_STEPS, "readout"))
            for k in range(KT):
                for h in range(HEADS):
                    last = nc.tensor.matmul(ps[0:KP, k, 0:D], WpH[:, h, k * KP:(k + 1) * KP], WoH[:, h, :],
                                            start=(h == 0), stop=(h == HEADS - 1))
            done("g", last)
            for q in range(2):
                for k in range(KT):
                    last = nc.tensor.matmul(ps[:, 2 + q, 0:SEQ], rope[:, k, q * P:(q + 1) * P], rope[:, k, :],
                                            start=(k == 0), stop=(k == KT - 1))
            done("scores", last)
            pe.wait_ge(s_setup, nth(DVE_STEPS, "prob1"))
            for q in range(2):
                for k in range(2):
                    last = nc.tensor.transpose(ps[:, 4 + k, q * P:(q + 1) * P], prob[:, q, k * P:(k + 1) * P],
                                               ident[:, :])
            done("probT", last)
            for f in range(FT):
                last = nc.tensor.matmul(ps[:, 6, f:f + 1], mout[:, f * P:(f + 1) * P], wa, start=True, stop=True)
            done("b0", last)
            last = nc.tensor.matmul(ps[0:1, 7, 0:D], wa, minp, start=True, stop=True)
            done("b1", last)
            pe.wait_ge(s_setup_act, nth(ACT_STEPS, "g"))
            for k in range(KT):
                for n in range(2):
                    last = nc.tensor.matmul(ps[0:KP, 2 * k + n, 0:FF // 2], mins[:, k * KP:(k + 1) * KP],
                                            mout[:, n * (FF // 2):(n + 1) * (FF // 2)], start=True, stop=True)
            done("c0", last)
            pe.wait_ge(s_setup, nth(DVE_STEPS, "w0"))
            for f in range(FT):
                last = nc.tensor.matmul(ps[:, f // 2, (f % 2) * D:(f % 2 + 1) * D], mout[:, f * P:(f + 1) * P],
                                        mins, start=True, stop=True)
            done("c1", last)

        def h0_pe(pe, i):
            pe.wait_ge(xs_loaded.sem, xs_loaded.at(i))
            pe.wait_ge(hA_kept.sem, hA_kept.at(i - 1))
            for t in range(TPB):
                for k in range(KT):
                    last = nc.tensor.matmul(tile_in(0, t), xs[:, k, t // 2, (t % 2) * P:(t % 2 + 1) * P],
                                            G[:, k, :], start=(k == 0), stop=(k == KT - 1))
            last.then_inc(h0_ready.sem, 1)

        def x1T_pe(pe, i):
            pe.wait_ge(xn1_kept.sem, xn1_kept.at(i))
            pe.wait_ge(x2T_kept.sem, x2T_kept.at(i - 1))
            for t in range(TPB):
                for k in range(KT):
                    last = nc.tensor.transpose(ps[0:KP, 2 + k, t * P:(t + 1) * P], xn1[:, t, k * KP:(k + 1) * KP],
                                               ident[:, :])
            last.then_inc(t1_ready.sem, 1)

        def v_pe(pe, i):
            pe.wait_ge(x1T_kept.sem, x1T_kept.at(i))
            for t in range(TPB):
                for k in range(KT):
                    last = nc.tensor.matmul(ps[:, 2, t * KV:(t + 1) * KV], x1T[:, k, t * P:(t + 1) * P], wv[:, k, :],
                                            start=(k == 0), stop=(k == KT - 1))
            last.then_inc(v_ready.sem, 1)

        def oT_pe(pe, i):
            pe.wait_ge(v_kept.sem, v_kept.at(i))
            for s in range(SPB):
                for k in range(2):
                    last = nc.tensor.matmul(ps[0:KV, 3, s * SEQ:(s + 1) * SEQ], vs[:, 2 * s + k, :], PT[:, k, :],
                                            start=(k == 0), stop=(k == 1))
            last.then_inc(oT_ready.sem, 1)

        def att_pe(pe, i):
            pe.wait_ge(oT_kept.sem, oT_kept.at(i))
            pe.wait_ge(h0_kept.sem, h0_kept.at(i))
            for t in range(TPB):
                last = nc.tensor.matmul(tile_in(0, t), oTs[:, t * P:(t + 1) * P], wo[:, :], start=True, stop=True)
            last.then_inc(att_ready.sem, 1)

        def x2T_pe(pe, i):
            pe.wait_ge(xn2_kept.sem, xn2_kept.at(i))
            pe.wait_ge(oT_kept.sem, oT_kept.at(i))
            for t in range(TPB):
                for k in range(KT):
                    last = nc.tensor.transpose(ps[0:KP, 2 + k, t * P:(t + 1) * P], xn2[:, t, k * KP:(k + 1) * KP],
                                               ident[:, :])
            last.then_inc(t2_ready.sem, 1)

        def ffn_up_pe(pe, i, tiles):
            for f in tiles:
                if f == 0:
                    pe.wait_ge(x2T_kept.sem, x2T_kept.at(i))
                if f >= 2:
                    pe.wait_ge(gelu_kept.sem, gelu_kept.at(i, f - 1))
                else:
                    pe.wait_ge(gelu_kept.sem, gelu_kept.at(i - 1, FT + f - 1))
                for k in range(KT):
                    last = nc.tensor.matmul(ps[:, 6 + f % 2, :], w0[:, k, f * P:(f + 1) * P], x2T[:, k, :],
                                            start=(k == 0), stop=(k == KT - 1))
                last.then_inc(up_ready.sem, 1)

        def ffn_down_pe(pe, i, t):
            if t == 0:
                pe.wait_ge(gelu_kept.sem, gelu_kept.at(i))
                pe.wait_ge(hB_kept.sem, hB_kept.at(i - 1))
            for f in range(FT):
                last = nc.tensor.matmul(tile_in(4, t), hT[:, f, t * P:(t + 1) * P], w1[:, f, :],
                                 start=(f == 0), stop=(f == FT - 1))
            if t == TPB - 1:
                last.then_inc(down_ready.sem, 1)

        def body_b_pe(pe, i, before=True, more=2):
            x2T_pe(pe, i)
            if before:
                ffn_down_pe(pe, i - 1, 3)
            ffn_up_pe(pe, i, (0, 1, 2))
            if more:
                x1T_pe(pe, i + 1)
            ffn_up_pe(pe, i, (3, 4, 5))
            if more:
                v_pe(pe, i + 1)
            ffn_down_pe(pe, i, 0)
            if more:
                oT_pe(pe, i + 1)
            ffn_down_pe(pe, i, 1)
            if more:
                att_pe(pe, i + 1)
            ffn_down_pe(pe, i, 2)
            if more == 2:
                h0_pe(pe, i + 2)
            if not more:
                ffn_down_pe(pe, i, 3)

        def transposes_c(pe, i):
            pe.wait_ge(xn_c.sem, xn_c.at(i))
            pe.wait_ge(mo_kept.sem, mo_kept.at(i - 2))
            pe.wait_ge(sp_abs.sem, sp_abs.at(i - 1))
            pe.wait_ge(gt_kept.sem, gt_kept.at(i - 2, 1))
            pe.wait_ge(gcn_kept.sem, gcn_kept.at(i - 1))
            for t in range(TPB):
                nc.tensor.transpose(ps[:, 6, t * P:(t + 1) * P], xnC[:, t, 0:P], ident[:, :])
                last = nc.tensor.transpose(ps[:, 7, t * P:(t + 1) * P], xnC[:, t, P:2 * P], ident[:, :])
            last.then_inc(xnT_ready.sem, 1)

        def in_proj(pe, i, f):
            if f == 0:
                pe.wait_ge(xnT_kept.sem, xnT_kept.at(i))
                pe.wait_ge(gt_kept.sem, gt_kept.at(i - 2))
            if f >= 2:
                pe.wait_ge(in_kept.sem, in_kept.at(i, f - 1))
            for k in range(KT):
                last = nc.tensor.matmul(ps[:, 5 + f % 2, :], win[k][:, f * P:(f + 1) * P],
                                        xnT[0:(P, LOW)[k], k, :, TAPS // 2:TAPS // 2 + SEQ],
                                        start=(k == 0), stop=(k == KT - 1))
            last.then_inc(in_ready.sem, 1)

        def x_proj(pe, i, j):
            pe.wait_ge(silu_kept.sem, silu_kept.at(i, DT3))
            pe.wait_ge(in_kept.sem, in_kept.at(i))
            pe.wait_ge(o_kept.sem, o_kept.at(i - 2, 3))
            for k in range(DT3):
                last = nc.tensor.matmul(ps[0:108, 5, :], wxp[:, k, :], xm[j][:, k, :],
                                        start=(k == 0), stop=(k == DT3 - 1))
            last.then_inc(xp_ready.sem, 1)

        def dt_proj(pe, i, fs):
            pe.wait_ge(dtl_kept.sem, dtl_kept.at(i))
            for f in fs:
                if f == 1:
                    pe.wait_ge(split.sem, split.at(i, 2))
                if f == 2:
                    pe.wait_ge(sp_abs.sem, sp_abs.at(i, 1))
                nc.tensor.matmul(ps[:, 6 - f % 2, :], wdt[96:96 + RANK, f * P:(f + 1) * P],
                                 dtl[96:96 + RANK, :], start=True, stop=True).then_inc(dt_ready.sem, 1)

        def gcn(pe, i, a, b):
            for n in range(a, b):
                m, r = divmod(n, CPROD)
                if n == 0:
                    pe.wait_ge(xnT_kept.sem, xnT_kept.at(i))
                elif r == 0:
                    pe.wait_ge(gcn_kept.sem, gcn_kept.at(i, 1))
                k, tap = (0, r) if r < TAPS else (1, 2 * (r - TAPS))
                rows = LOW if r == CPROD - 1 else P
                last = nc.tensor.matmul(ps[0:KP, 7, :], wconv[0:rows, r, m * KP:(m + 1) * KP],
                                        xnT[0:rows, k, :, tap:tap + SEQ], start=(r == 0), stop=(r == CPROD - 1))
                if r == CPROD - 1:
                    last.then_inc(gcn_ready.sem, 1)

        def front_pe(pe, i, j):
            transposes_c(pe, i)
            for f in range(2 * DT3):
                in_proj(pe, i, f)
            x_proj(pe, i, j)
            dt_proj(pe, i, (0, 1, 2))
            gcn(pe, i, 0, 2 * CPROD)

        def mamba_out(pe, i, j, m, last_block):
            if m == 0:
                pe.wait_ge(yz.sem, yz.at(i))
            if not last_block:
                pe.wait_ge(sp_abs.sem, sp_abs.at(i + 1))
            pe.wait_ge(o_kept.sem, o_kept.at(i - 1, 3))
            for k in range(DT3):
                last = nc.tensor.matmul(ps[0:KP, 5 + m, :], wmo[:, k, m * KP:(m + 1) * KP], zs[j][:, k, :],
                                        start=(k == 0), stop=(k == DT3 - 1))
            last.then_inc(mo_ready.sem, 1)

        def gate_pe(pe, i, j, m, last_block):
            pe.wait_ge(mo_kept.sem, mo_kept.at(i))
            pe.wait_ge(gcn_kept.sem, gcn_kept.at(i if last_block else i + 1))
            ops = [(wgg, xg[j]), (wgm, xmb)]
            n = 0
            for w, x in ops:
                for k in range(KT):
                    last = nc.tensor.matmul(ps[0:KP, 7 - 2 * m, :], w[:, k, m * KP:(m + 1) * KP], x[:, k, :],
                                            start=(n == 0), stop=(n == 3))
                    n += 1
            last.then_inc(gt_ready.sem, 1)

        def out_pe(pe, i, last_block):
            pe.wait_ge(fuse.sem, fuse.at(i))
            pe.wait_ge(gt_kept.sem, gt_kept.at(i))
            if not last_block:
                pe.wait_ge(in_kept.sem, in_kept.at(i + 2))
            for t in range(TPB):
                for k in range(KT):
                    last = nc.tensor.matmul(tile_in(5, t), gate[:, k, t * P:(t + 1) * P], wout[:, k, :],
                                            start=(k == 0), stop=(k == KT - 1))
            last.then_inc(out_ready.sem, 1)

        def back_pe(pe, i, j, last):
            for m in range(KT):
                mamba_out(pe, i, j, m, last)
            for m in range(KT):
                gate_pe(pe, i, j, m, last)
            out_pe(pe, i, last)

        def bcast(pe, i, j, n, which):
            if n == 0:
                pe.wait_ge(split.sem, split.at(i, 5))
            for ev in ((dbx, b_copied) if which == 0 else (hc,)):
                if n:
                    pe.wait_ge(ev.sem, ev.at(i, n))
                else:
                    pe.wait_ge(ev.sem, ev.at(i - 1))
            row = pick[:, which * NS + n:which * NS + n + 1].broadcast_to([KP, P])
            nc.tensor.matmul(ps[:, 3 + which, :], row, bc[j], start=True, stop=True)\
                .then_inc((b_ready, c_ready)[which].sem, 1)

        def body_pe(pe, i, j, front=True, back=True):
            if isinstance(i, int) and i == 0:
                for which in (0, 1):
                    bcast(pe, i, j, 0, which)
            bcast(pe, i, j, 1, 0)
            done = 0
            for n in range(NS):
                if n + 2 < NS:
                    bcast(pe, i, j, n + 2, 0)
                if back:
                    if n == 0:
                        gcn(pe, i, TAIL, 2 * CPROD)
                    if n in (AT["mamba"], AT["mamba"] + 1):
                        mamba_out(pe, i - 1, 1 - j, n - AT["mamba"], False)
                    if n in (AT["gate"], AT["gate"] + 1):
                        gate_pe(pe, i - 1, 1 - j, n - AT["gate"], False)
                    if n == AT["out"]:
                        out_pe(pe, i - 1, not front)
                if front:
                    if n == AT["transpose"]:
                        transposes_c(pe, i + 1)
                    if AT["in_proj"] <= n < AT["in_proj"] + DT3:
                        in_proj(pe, i + 1, 2 * (n - AT["in_proj"]))
                        in_proj(pe, i + 1, 2 * (n - AT["in_proj"]) + 1)
                    if n == AT["x_proj"]:
                        x_proj(pe, i + 1, 1 - j)
                    gcn(pe, i + 1, done, done + GCN_AT.get(n, 0))
                    done += GCN_AT.get(n, 0)
                if n + 1 < NS:
                    bcast(pe, i, j, n + 1, 1)
                for f in range(DT3):
                    if f == 0:
                        pe.wait_ge(hc.sem, hc.at(i, n + 1))
                    if n == 0:
                        pe.wait_ge(ysk.sem, ysk.at(i - 1, f + 1))
                    last = nc.tensor.matmul(ps[:, f, :], ident[:, :], hs[SLOT[n]][:, f, :],
                                            start=(n == 0), stop=(n == NS - 1))
                last.then_inc(nsum.sem, 1)
                if front and n == AT["dt"]:
                    dt_proj(pe, i + 1, (0, 1))
                if front and n == AT["dt"] + 1:
                    dt_proj(pe, i + 1, (2,))
            if front:
                for which in (0, 1):
                    bcast(pe, i + 1, 1 - j, 0, which)
                gcn(pe, i + 1, done, TAIL)

        @block.tensor
        def _(pe):
            pe.wait_ge(s_const, 16 * 7)
            pe.wait_ge(s_zero, 1)
            with pe.Fori(0, NB // 2) as ii:
                for j in (0, 1):
                    i = 2 * ii + j
                    pe.wait_ge(nrm_a.sem, nrm_a.at(i))
                    pe.wait_ge(xt_a.sem, xt_a.at(i - 2))
                    for t in range(TPB):
                        for k in range(KT):
                            last = nc.tensor.transpose(ps[0:KP, 2 * j + k, t * P:(t + 1) * P],
                                                       nrm[j][:, t, k * KP:(k + 1) * KP], ident[:, :])
                    last.then_inc(nrmT_a.sem, 1)
                    pe.wait_ge(shifted[j].sem, shifted[j].at(ii))
                    for t in range(TPB):
                        rows = P if t % 2 == 0 else P - 2
                        for k in range(KT):
                            m = KP + k
                            last = nc.tensor.matmul(ps[0:m, 4 + k, 0:D], nrm[j][0:rows, t, k * KP:k * KP + m],
                                                    tok2[j][0:rows, t, :], start=False, stop=False,
                                                    skip_group_check=True)
                    last.then_inc(outer_a.sem, 1)
            setup_pe(pe)
            pe.wait_ge(s_setup, nth(DVE_STEPS, "w1"))
            nc.tensor.matmul(ps[:, 6, 0:D], ones[:, :], b1row[:, :], start=True, stop=True).then_inc(s_b1, 1)
            for part in (h0_pe, x1T_pe, v_pe, oT_pe, att_pe):
                part(pe, 0)
            h0_pe(pe, 1)
            pe.wait_ge(s_b1b, 1)
            body_b_pe(pe, 0, before=False)
            with pe.Fori(1, NB - 2) as i:
                body_b_pe(pe, i)
            body_b_pe(pe, NB - 2, more=1)
            body_b_pe(pe, NB - 1, more=0)
            pe.wait_ge(s_cset, 1)
            front_pe(pe, 0, 0)
            body_pe(pe, 0, 0, back=False)
            with pe.Fori(0, NB // 2 - 1) as ii:
                for j in (1, 0):
                    body_pe(pe, 2 * ii + (1 if j else 2), j)
            body_pe(pe, NB - 1, 1, front=False)
            back_pe(pe, NB - 1, 1, last=True)
            pe.wait_ge(s_wd, 16 * 9)
            router_T_pe(pe, 0, 0)
            logits_pe(pe, 0)
            with pe.Fori(0, NB // SENDS - 1) as q:
                for j in range(SENDS):
                    router_T_pe(pe, SENDS * q + j + 1, (j + 1) % SENDS)
                    positions_pe(pe, SENDS * q + j)
                    logits_pe(pe, SENDS * q + j + 1)
            for j in range(SENDS):
                if j + 1 < SENDS:
                    router_T_pe(pe, NB - SENDS + j + 1, j + 1)
                positions_pe(pe, NB - SENDS + j)
                if j + 1 < SENDS:
                    logits_pe(pe, NB - SENDS + j + 1)
            pe.wait_ge(s_we, 32)
            pe.wait_ge(s_tables, 1)
            slot_transpose(pe, 0, 0, 0)
            slot_transpose(pe, 1, 0, 1)
            expert_up(pe, 0, 0)
            with pe.Fori(0, NSB // RING - 1) as q:
                for j in range(RING):
                    expert_block(pe, RING * q + j, q, j)
            for j in range(RING):
                expert_block(pe, NSB - RING + j, NSB // RING - 1, j, last=max(0, j + 3 - RING))

        def probs_act(act, i):
            act.wait_ge(gsteps.sem, gsteps.at(i, 3))
            nc.scalar.activation(pr, lg, ACT.Exp).then_inc(gexp.sem, 1)

        def rows_act(act, i, j):
            act.wait_ge(dT_ready.sem, dT_ready.at(i))
            act.wait_ge(lg_ready.sem, lg_ready.at(i - 1))
            for k in range(KT):
                nc.scalar.activation(xTs[:, k, :], ps[0:KP, k, :], ACT.Identity, bias=mob[:, k:k + 1],
                                     scale=mow[:, k:k + 1]).then_inc(dT_kept.sem, 1)
            act.wait_ge(xn_d.sem, xn_d.at(i))
            nc.scalar.activation(send[j][:, :, 1, 0:D], send[j][:, :, 0, 0:D], ACT.Copy).then_inc(xn2_d.sem, 1)
            act.wait_ge(coef_d.sem, coef_d.at(i))
            for t in range(TPB):
                Ht = H[:, bass.ds(i * TPB + t, 1), :].rearrange("p t f -> p (t f)")
                nc.scalar.activation(Ht, Ht, ACT.Identity, bias=shiftD[j % 2][:, t:t + 1],
                                     scale=growD[j % 2][:, t:t + 1]).then_inc(res_d.sem, 1)

        def slot_T_act(act, b, j):
            act.wait_ge(xt_T.sem, xt_T.at(b))
            act.wait_ge(e_up.sem, e_up.at(b - 2))
            for k in range(KT):
                nc.scalar.activation(xT[j][:, k, :], ps[0:KP, 7, k * P:(k + 1) * P], ACT.Identity,
                                     bias=mob[:, k:k + 1], scale=mow[:, k:k + 1]).then_inc(xT_kept.sem, 1)

        def silu_e(act, b, j):
            act.wait_ge(e_up.sem, e_up.at(b))
            act.wait_ge(e_hT.sem, e_hT.at(b - 2))
            nc.scalar.activation(hS[j].rearrange("p (n f) -> p n f", n=2), ps[:, 2 * j:2 * j + 2, 0:FF // 2],
                                 ACT.Silu).then_inc(e_silu.sem, 1)

        def x1T_act(act, i):
            act.wait_ge(t1_ready.sem, t1_ready.at(i))
            act.wait_ge(v_ready.sem, v_ready.at(i - 1))
            nc.scalar.activation(x1T, ps[0:KP, 2:4, :], ACT.Copy).then_inc(x1T_kept.sem, 1)

        def att_act(act, i):
            act.wait_ge(v_ready.sem, v_ready.at(i))
            act.wait_ge(oT_ready.sem, oT_ready.at(i - 1))
            nc.scalar.activation(vs, ps[:, 2, 0:TPB * KV].rearrange("p (t f) -> p t f", t=TPB), ACT.Copy)\
                .then_inc(v_kept.sem, 1)
            act.wait_ge(oT_ready.sem, oT_ready.at(i))
            act.wait_ge(att_ready.sem, att_ready.at(i - 1))
            nc.scalar.activation(oTs, ps[0:KV, 3, :], ACT.Copy).then_inc(oT_kept.sem, 1)
            act.wait_ge(t2_ready.sem, t2_ready.at(i))
            act.wait_ge(up_ready.sem, up_ready.at(i - 1))
            nc.scalar.activation(x2T, ps[0:KP, 2:4, :], ACT.Copy).then_inc(x2T_kept.sem, 1)

        def gelu_act(act, i, tiles):
            for f in tiles:
                if f == 0:
                    act.wait_ge(down_ready.sem, down_ready.at(i - 1))
                act.wait_ge(up_ready.sem, up_ready.at(i, f + 1))
                nc.scalar.activation(hT[:, f, :], ps[:, 6 + f % 2, :], ACT.Gelu_apprx_tanh,
                                     bias=b0[:, f:f + 1]).then_inc(gelu_kept.sem, 1)

        def body_b_act(act, i, more=True):
            gelu_act(act, i, (0, 1, 2))
            if more:
                x1T_act(act, i + 1)
            gelu_act(act, i, (3, 4, 5))
            if more:
                att_act(act, i + 1)

        def decay(act, i, j, n):
            if n >= 2:
                act.wait_ge(scan.sem, scan.at(i, n - 1))
            else:
                act.wait_ge(scan.sem, scan.at(i - 1, NS - 1 + n))
            for f in range(DT3):
                if n == 0:
                    act.wait_ge(dt_kept.sem, dt_kept.at(i))
                nc.scalar.activation(dA[n % 2][:, f, :, 1:SEQ],
                                     dtp[j][:, f, :].rearrange("p (s t) -> p s t", s=SPB)[:, :, 1:SEQ],
                                     ACT.Exp, scale=nega[:, f, n:n + 1]).then_inc(da_ready.sem, 1)

        def copy_b(act, i, n):
            act.wait_ge(b_ready.sem, b_ready.at(i, n + 1))
            if n >= 2:
                act.wait_ge(dbx_gp.sem, dbx_gp.at(i, n - 1))
            else:
                act.wait_ge(dbx_gp.sem, dbx_gp.at(i - 1, NS - 1 + n))
            nc.scalar.activation(bs[n % 2], ps[:, 3, :], ACT.Copy).then_inc(b_copied.sem, 1)

        def xnT_act(act, i):
            act.wait_ge(xnT_ready.sem, xnT_ready.at(i))
            act.wait_ge(in_ready.sem, in_ready.at(i - 1))
            act.wait_ge(gcn_ready.sem, gcn_ready.at(i - 1))
            for lo, hi, k, at in ((0, P, 0, TAPS // 2), (0, LOW, 1, TAPS // 2), (LOW, P, 1, TAPS // 2 - 1)):
                nc.scalar.activation(xnT[lo:hi, k, :, at:at + SEQ],
                                     ps[lo:hi, 6 + k, :].rearrange("p (s t) -> p s t", s=SPB),
                                     ACT.Identity, bias=n1b[lo:hi, k:k + 1], scale=n1w[lo:hi, k:k + 1])\
                    .then_inc(xnT_kept.sem, 1)

        def in_act(act, i, j, f):
            act.wait_ge(in_ready.sem, in_ready.at(i, f + 1))
            src = ps[:, 5 + f % 2, :]
            if f < DT3:
                if f == 0:
                    act.wait_ge(conv_ch.sem, conv_ch.at(i - 1))
                nc.scalar.activation(xi[:, f, :, CTAPS - 1:PADC], src.rearrange("p (s t) -> p s t", s=SPB),
                                     ACT.Copy).then_inc(in_kept.sem, 1)
            else:
                if f == DT3:
                    act.wait_ge(mo_ready.sem, mo_ready.at(i - 2))
                nc.scalar.activation(zs[j][:, f - DT3, :], src, ACT.Copy).then_inc(in_kept.sem, 1)

        def silus_act(act, i, j):
            act.wait_ge(conv_ch.sem, conv_ch.at(i))
            for f in range(DT3):
                nc.scalar.activation(xm[j][:, f, :], xm[j][:, f, :], ACT.Silu).then_inc(silu_kept.sem, 1)
            for f in range(DT3):
                if f == 0:
                    act.wait_ge(in_kept.sem, in_kept.at(i))
                nc.scalar.activation(zs[j][:, f, :], zs[j][:, f, :], ACT.Silu).then_inc(silu_kept.sem, 1)

        def dtl_act(act, i):
            act.wait_ge(xp_ready.sem, xp_ready.at(i))
            act.wait_ge(dt_ready.sem, dt_ready.at(i - 1))
            nc.scalar.activation(dtl[96:96 + RANK, :], ps[96:96 + RANK, 5, :], ACT.Copy).then_inc(dtl_kept.sem, 1)

        def softplus_act(act, i, f):
            act.wait_ge(dt_ready.sem, dt_ready.at(i, f + 1))
            act.wait_ge(sp_max.sem, sp_max.at(i, f + 1))
            act.wait_ge(out_ready.sem, out_ready.at(i - 2))
            s = sp1[:, f, :]
            nc.scalar.activation(s, ps[:, 6 - f % 2, :], ACT.Abs, bias=dtb[:, f:f + 1]).then_inc(sp_abs.sem, 1)
            act.wait_ge(sp_abs.sem, sp_abs.at(i, f + 1))
            nc.scalar.activation(s, s, ACT.Exp, scale=-1.0).then_inc(sp_exp.sem, 1)
            if f == DT3 - 1:
                act.wait_ge(sp_exp.sem, sp_exp.at(i))
                nc.scalar.activation(sp1, sp1, ACT.Ln, bias=1.0).then_inc(sp_log.sem, 1)

        def gcn_act(act, i, j, m):
            act.wait_ge(gcn_ready.sem, gcn_ready.at(i, m + 1))
            act.wait_ge(fuse.sem, fuse.at(i - 2))
            nc.scalar.activation(xg[j][:, m, :], ps[0:KP, 7, :], ACT.Identity, bias=xgb[:, m:m + 1])\
                .then_inc(gcn_kept.sem, 1)

        def mo_act(act, i, m):
            act.wait_ge(mo_ready.sem, mo_ready.at(i, m + 1))
            act.wait_ge(gt_ready.sem, gt_ready.at(i - 1))
            act.wait_ge(fuse.sem, fuse.at(i - 1))
            nc.scalar.activation(xmb[:, m, :], ps[0:KP, 5 + m, :], ACT.Copy).then_inc(mo_kept.sem, 1)

        def gate_act(act, i, m, last=False):
            act.wait_ge(gt_ready.sem, gt_ready.at(i, m + 1))
            act.wait_ge(dt_kept.sem, dt_kept.at(i if last else i + 1))
            nc.scalar.activation(gate[:, m, :], ps[0:KP, 7 - 2 * m, :], ACT.Identity, bias=gateb[:, m:m + 1])\
                .then_inc(gt_kept.sem, 1)

        def tanh_act(act, i):
            act.wait_ge(gt_kept.sem, gt_kept.at(i))
            for m in range(KT):
                nc.scalar.activation(gate[:, m, :], gate[:, m, :], ACT.Tanh, scale=0.5).then_inc(gt_tanh.sem, 1)

        def front_act(act, i, j):
            xnT_act(act, i)
            for f in range(2 * DT3):
                in_act(act, i, j, f)
            silus_act(act, i, j)
            dtl_act(act, i)
            for f in range(DT3):
                softplus_act(act, i, f)
            for m in range(KT):
                gcn_act(act, i, j, m)

        def body_act(act, i, j, front=True, back=True):
            for n in (0, 1):
                copy_b(act, i, n)
                decay(act, i, j, n)
            for n in range(NS):
                if back:
                    if n == 0:
                        gcn_act(act, i, j, 1)
                    if n in (AT["mamba"], AT["mamba"] + 1):
                        mo_act(act, i - 1, n - AT["mamba"])
                    if n in (AT["gate"], AT["gate"] + 1):
                        gate_act(act, i - 1, n - AT["gate"])
                if front:
                    if n == AT["transpose"]:
                        xnT_act(act, i + 1)
                    if AT["in_proj"] <= n < AT["in_proj"] + DT3:
                        in_act(act, i + 1, 1 - j, 2 * (n - AT["in_proj"]))
                        in_act(act, i + 1, 1 - j, 2 * (n - AT["in_proj"]) + 1)
                if n == AT["silu"]:
                    if back:
                        tanh_act(act, i - 1)
                    if front:
                        silus_act(act, i + 1, 1 - j)
                if front:
                    if n == AT["x_proj"]:
                        dtl_act(act, i + 1)
                    if n == AT["dt"] + 2:
                        softplus_act(act, i + 1, 0)
                        softplus_act(act, i + 1, 1)
                    if n == AT["dt"] + 3:
                        softplus_act(act, i + 1, 2)
                    if n == AT["conv_kept"]:
                        gcn_act(act, i + 1, 1 - j, 0)
                if n + 2 < NS:
                    copy_b(act, i, n + 2)
                    decay(act, i, j, n + 2)
            if not front:
                for m in range(KT):
                    mo_act(act, i, m)
                for m in range(KT):
                    gate_act(act, i, m, last=True)
                tanh_act(act, i)

        @block.scalar
        def _(act):
            act.wait_ge(s_const, 16 * 7)
            with act.Fori(0, NB // 2) as ii:
                for j in (0, 1):
                    i = 2 * ii + j
                    act.wait_ge(nrmT_a.sem, nrmT_a.at(i))
                    for k in range(KT):
                        last = nc.scalar.activation(XT[:, k, bass.ds(i * BT, BT)], ps[0:KP, 2 * j + k, :],
                                                    ACT.Identity, bias=lnb[:, k:k + 1], scale=lnw[:, k:k + 1])
                    last.then_inc(xt_a.sem, 1)
            act.wait_ge(s_setup_pe, nth(PE_STEPS, "x1"))
            nc.scalar.activation(X1, ps[0:KP, 0:2, :], ACT.Copy).then_inc(s_setup_act, 1)
            act.wait_ge(s_setup_pe, nth(PE_STEPS, "readout"))
            nc.scalar.activation(WoH[:, :, :].rearrange("p (a b) o -> p a (b o)", b=2), ps[0:DTR, 4:8, 0:2 * D],
                                 ACT.Copy).then_inc(s_setup_act, 1)
            act.wait_ge(s_setup_pe, nth(PE_STEPS, "g"))
            nc.scalar.activation(G[:, :, :], ps[0:KP, 0:2, 0:D], ACT.Copy).then_inc(s_setup_act, 1)
            act.wait_ge(s_setup, nth(DVE_STEPS, "negmax"))
            for q in range(2):
                nc.scalar.activation(prob[:, q, :], ps[:, 2 + q, 0:SEQ], ACT.Exp, bias=smax[:, q:q + 1],
                                     accum_out=ssum[:, q:q + 1]).then_inc(s_setup_act, 1)
            act.wait_ge(s_setup_pe, nth(PE_STEPS, "probT"))
            nc.scalar.activation(PT[:, :, :], ps[:, 4:6, 0:SEQ], ACT.Copy).then_inc(s_setup_act, 1)
            x1T_act(act, 0)
            att_act(act, 0)
            with act.Fori(0, NB - 1) as i:
                body_b_act(act, i)
            body_b_act(act, NB - 1, False)
            act.wait_ge(s_wc, 16 * 14)
            nc.scalar.activation(nega[:, :, :], nega[:, :, :], ACT.Exp).then_inc(s_cact, 1)
            act.wait_ge(hB_kept.sem, hB_kept.at(NB - 1))
            front_act(act, 0, 0)
            body_act(act, 0, 0, back=False)
            with act.Fori(0, NB // 2 - 1) as ii:
                for j in (1, 0):
                    body_act(act, 2 * ii + (1 if j else 2), j)
            body_act(act, NB - 1, 1, front=False)
            rows_act(act, 0, 0)
            with act.Fori(0, NB // SENDS - 1) as q:
                for j in range(SENDS):
                    probs_act(act, SENDS * q + j)
                    rows_act(act, SENDS * q + j + 1, (j + 1) % SENDS)
            for j in range(SENDS):
                probs_act(act, NB - SENDS + j)
                if j + 1 < SENDS:
                    rows_act(act, NB - SENDS + j + 1, j + 1)
            act.wait_ge(s_tables, 1)
            slot_T_act(act, 0, 0)
            slot_T_act(act, 1, 1)
            silu_e(act, 0, 0)
            with act.Fori(0, NSB // 2 - 1) as q:
                for j in (0, 1):
                    silu_e(act, 2 * q + j + 1, 1 - j)
                    slot_T_act(act, 2 * q + j + 2, j)
            silu_e(act, NSB - 1, 1)

        def setup_dve(dve):
            steps = iter(DVE_STEPS)
            assert next(steps) == "ones"

            def step(name, ins):
                assert next(steps) == name
                ins.then_inc(s_setup, 1)
                dve.wait_ge(s_setup, nth(DVE_STEPS, name))

            def pe_done(name):
                dve.wait_ge(s_setup_pe, nth(PE_STEPS, name))

            dve.wait_ge(outer_a.sem, outer_a.at(NB - 1))
            step("sum_row", V.tensor_copy(srow[KP:KP + 1, :], ps[KP:KP + 1, 5, 0:D]))
            step("alpha", V.tensor_tensor(wa, wa2[:, 0:1], wa2[:, 1:2], ALU.mult))
            dve.wait_ge(s_wa, 16 * SETUP_DMAS)
            step("scaled_mask", V.tensor_scalar(mins, minp, wa, None, ALU.mult))
            pe_done("bias_outer")
            for k in range(KT):
                step(f"m{k}w", V.tensor_scalar(MS[:, k, :], ps[0:KP, 4 + k, 0:D], lnw[:, k:k + 1], None, ALU.mult))
                step(f"m{k}", V.tensor_tensor(MS[:, k, :], MS[:, k, :], ps[0:KP, 6, k * D:(k + 1) * D], ALU.add))
            step("decayed", V.tensor_scalar(tr, tr, TRACE_DECAY, None, ALU.mult))
            pe_done("update")
            trf = tr.rearrange("p h q -> p (h q)")
            step("trace", V.scalar_tensor_tensor(out=trf, in0=ps[0:DTR, 2, :],
                                                 scalar=TRACE_LR / (BATCH * (SEQ - 2)), in1=trf,
                                                 op0=ALU.mult, op1=ALU.add))
            pe_done("scores")
            step("max", V.tensor_reduce(smax, ps[:, 2:4, 0:SEQ], AX.X, ALU.max))
            step("negmax", V.tensor_scalar(smax, smax, -1.0, None, ALU.mult))
            dve.wait_ge(s_setup_act, nth(ACT_STEPS, "exp1"))
            step("recip", V.reciprocal(ssum, ssum))
            for q in range(2):
                step(f"prob{q}", V.tensor_scalar(prob[:, q, :], prob[:, q, :], ssum[:, q:q + 1], None, ALU.mult))
            pe_done("b1")
            step("b0", V.tensor_tensor(b0, bfc, ps[:, 6, 0:FT], ALU.mult))
            step("b1", V.tensor_tensor(b1row[:, :], b1row[:, :], ps[0:1, 7, 0:D], ALU.mult))
            pe_done("c0")
            w0v = w0.rearrange("p k (n f) -> p (k n) f", n=2)
            step("w0", V.tensor_tensor(w0v, w0v, ps[0:KP, 0:4, 0:FF // 2], ALU.mult))
            pe_done("c1")
            w1v = w1.rearrange("p (a b) e -> p a (b e)", b=2)
            step("w1", V.tensor_tensor(w1v, w1v, ps[:, 0:3, 0:2 * D], ALU.mult))

        def norm_b(dve, i, q, src, dst, dst_free, done):
            for t in range(TPB):
                last = V.bn_stats(stB[:, t, :], src[:, t, :])
            last.then_inc(st_b.sem, 1)
            dve.wait_ge(st_b.sem, st_b.at(i, q))
            dve.sem_inc(s_alone, 1)
            for t in range(TPB):
                last = V.bn_aggr(mvB[:, t, :], stB[:, t, :])
            last.then_inc(mv_b.sem, 1)
            dve.wait_ge(mv_b.sem, mv_b.at(i, q))
            V.tensor_scalar(veB, mvB[:, :, 1], EPS, None, ALU.add).then_inc(ve_b.sem, 1)
            dve.wait_ge(rs_b.sem, rs_b.at(i, q))
            dve.wait_ge(dst_free.sem, dst_free.at(i - 1))
            for t in range(TPB):
                last = V.tensor_scalar(dst[:, t, :], src[:, t, :], mvB[:, t, 0:1], rsB[:, t:t + 1],
                                       ALU.subtract, ALU.mult)
            last.then_inc(done.sem, 1)

        def h0_dve(dve, i):
            dve.wait_ge(h0_ready.sem, h0_ready.at(i))
            V.tensor_copy(h0c.rearrange("p (a b) f -> p a (b f)", b=2), tiles_of(0)).then_inc(h0_kept.sem, 1)
            dve.wait_ge(h0_kept.sem, h0_kept.at(i))
            norm_b(dve, i, 1, h0c, xn1, t1_ready, xn1_kept)

        def att_dve(dve, i, j):
            dve.wait_ge(att_ready.sem, att_ready.at(i))
            V.tensor_tensor(hA[j].rearrange("p (a b) f -> p a (b f)", b=2), h0c.rearrange("p (a b) f -> p a (b f)", b=2),
                            tiles_of(0), ALU.add).then_inc(hA_kept.sem, 1)
            dve.wait_ge(hA_kept.sem, hA_kept.at(i))
            norm_b(dve, i, 2, hA[j], xn2, t2_ready, xn2_kept)

        def mlp_dve(dve, i, j):
            dve.wait_ge(down_ready.sem, down_ready.at(i))
            dve.wait_ge(biased.sem, biased.at(i))
            V.tensor_tensor(H[:, bass.ds(i * TPB, TPB), :].rearrange("p (a b) f -> p a (b f)", b=2),
                            hA[j].rearrange("p (a b) f -> p a (b f)", b=2), tiles_of(4), ALU.add)\
                .then_inc(hB_kept.sem, 1)

        def body_b_dve(dve, i, j, before=True):
            h0_dve(dve, i + 1)
            if before:
                mlp_dve(dve, i - 1, 1 - j)
            att_dve(dve, i + 1, 1 - j)

        def norm_c(dve, i, j):
            Hi = lambda t: H[:, bass.ds(i * TPB + t, 1), :].rearrange("p t f -> p (t f)")
            if isinstance(i, int) and i == 0:
                dve.wait_ge(hB_kept.sem, hB_kept.at(NB - 1))
            for t in range(TPB):
                last = V.bn_stats(stC[:, t, :], Hi(t))
            last.then_inc(st_c.sem, 1)
            dve.wait_ge(st_c.sem, st_c.at(i))
            dve.sem_inc(s_alone, 1)
            for t in range(TPB):
                last = V.bn_aggr(mvC[j][:, t, :], stC[:, t, :])
            last.then_inc(mv_c.sem, 1)
            dve.wait_ge(mv_c.sem, mv_c.at(i))
            dve.wait_ge(rs_c.sem, rs_c.at(i - 1))
            V.tensor_scalar(pvC[:, 0, :], mvC[j][:, :, 1], EPS, None, ALU.add)
            V.tensor_scalar(pvC[:, 1, :], mvC[j][:, :, 1], 1.0 + EPS, EPS * EPS, ALU.mult, ALU.add)\
                .then_inc(pv_c.sem, 1)

        def xn_dve(dve, i, j):
            dve.wait_ge(rs_c.sem, rs_c.at(i))
            dve.wait_ge(xnT_ready.sem, xnT_ready.at(i - 1))
            dve.wait_ge(tail_o.sem, tail_o.at(i - 3))
            for t in range(TPB):
                Ht = H[:, bass.ds(i * TPB + t, 1), :].rearrange("p t f -> p (t f)")
                V.tensor_scalar(xnC[:, t, 0:D], Ht, mvC[j][:, t, 0:1], rsC[j][:, 1, t:t + 1],
                                ALU.subtract, ALU.mult)
                last = V.tensor_scalar(xnC[:, t, D:2 * P], Ht[:, P:D], mvC[j][:, t, 0:1], rsC[j][:, 1, t:t + 1],
                                       ALU.subtract, ALU.mult)
            last.then_inc(xn_c.sem, 1)

        def conv_dve(dve, i, j, f):
            dve.wait_ge(in_kept.sem, in_kept.at(i, f + 1))
            x3 = xm[j][:, f, :].rearrange("p (s t) -> p s t", s=SPB)
            for tap in range(CTAPS):
                src = xi[:, f, :, tap:tap + SEQ]
                if tap == 0:
                    ins = V.tensor_scalar(x3, src, cw[:, f, 0:1], cb[:, f:f + 1], ALU.mult, ALU.add)
                else:
                    dve.wait_ge(conv_ch.sem, conv_ch.at(i, f * CTAPS + tap))
                    ins = V.scalar_tensor_tensor(out=x3, in0=src, scalar=cw[:, f, tap:tap + 1], in1=x3,
                                                 op0=ALU.mult, op1=ALU.add)
                ins.then_inc(conv_ch.sem, 1)

        def split_dve(dve, i, j):
            dve.wait_ge(xp_ready.sem, xp_ready.at(i))
            src = ps[0:96, 5, :]
            bcp = bc[j]
            V.tensor_copy(bcp, src).then_inc(split.sem, 1)
            dve.wait_ge(split.sem, split.at(i, 1))
            V.tensor_tensor(rest, src, bcp, ALU.subtract).then_inc(split.sem, 1)
            dve.wait_ge(split.sem, split.at(i, 2))
            V.tensor_copy(mid, rest).then_inc(split.sem, 1)
            dve.wait_ge(split.sem, split.at(i, 3))
            V.tensor_copy(bcp[32:64, :], mid[32:64, :]).then_inc(split.sem, 1)
            V.tensor_tensor(bcp[64:96, :], rest[64:96, :], mid[64:96, :], ALU.subtract).then_inc(split.sem, 1)

        def softplus_max_dve(dve, i, j, f):
            dve.wait_ge(dt_ready.sem, dt_ready.at(i, f + 1))
            V.tensor_scalar(dtp[j][:, f, :], ps[:, 6 - f % 2, :], dtb[:, f:f + 1], 0.0, ALU.add, ALU.max)\
                .then_inc(sp_max.sem, 1)

        def softplus_dve(dve, i, j):
            dve.wait_ge(sp_max.sem, sp_max.at(i))
            dve.wait_ge(sp_log.sem, sp_log.at(i))
            V.tensor_tensor(dtp[j], dtp[j], sp1, ALU.add).then_inc(dt_kept.sem, 1)
            dve.wait_ge(dt_kept.sem, dt_kept.at(i))
            dve.wait_ge(silu_kept.sem, silu_kept.at(i, DT3))
            V.tensor_tensor(up_[j], dtp[j], xm[j], ALU.mult).then_inc(u_kept.sem, 1)

        def front_dve(dve, i, j):
            norm_c(dve, i, j)
            xn_dve(dve, i, j)
            for f in range(DT3):
                conv_dve(dve, i, j, f)
            split_dve(dve, i, j)
            for f in range(DT3):
                softplus_max_dve(dve, i, j, f)
            softplus_dve(dve, i, j)

        def fuse_dve(dve, i, j):
            dve.wait_ge(gt_tanh.sem, gt_tanh.at(i))
            dve.wait_ge(gcn_kept.sem, gcn_kept.at(i))
            V.tensor_tensor(xg[j], xg[j], xmb, ALU.subtract).then_inc(fuse.sem, 1)
            dve.wait_ge(fuse.sem, fuse.at(i, 1))
            V.scalar_tensor_tensor(out=xg[j], in0=gate, scalar=1.0, in1=xg[j], op0=ALU.add, op1=ALU.mult)\
                .then_inc(fuse.sem, 1)
            dve.wait_ge(fuse.sem, fuse.at(i, 2))
            V.scalar_tensor_tensor(out=gate, in0=xg[j], scalar=0.5, in1=xmb, op0=ALU.mult, op1=ALU.add)\
                .then_inc(fuse.sem, 1)

        def xr_dve(dve, i, j):
            dve.wait_ge(o_kept.sem, o_kept.at(i - 1, 3))
            for t in range(TPB):
                last = V.tensor_scalar(xr[:, t, :], H[:, bass.ds(i * TPB + t, 1), :].rearrange("p t f -> p (t f)"),
                                       mvC[j][:, t, 0:1], rsC[j][:, 0, t:t + 1], ALU.subtract, ALU.mult)
            last.then_inc(o_kept.sem, 1)
            dve.wait_ge(o_kept.sem, o_kept.at(i, 1))
            V.tensor_tensor(xr, xr, outb.unsqueeze(1).broadcast_to([P, TPB, D]), ALU.add)\
                .then_inc(o_kept.sem, 1)

        def out_dve(dve, i, last=False):
            dve.wait_ge(xnT_ready.sem, xnT_ready.at(i if last else i + 2))
            dve.wait_ge(out_ready.sem, out_ready.at(i))
            dve.wait_ge(o_kept.sem, o_kept.at(i, 2))
            dve.wait_ge(tail_o.sem, tail_o.at(i - 1))
            V.tensor_tensor(o.rearrange("p (a b) f -> p a (b f)", b=2), xr.rearrange("p (a b) f -> p a (b f)", b=2),
                            tiles_of(5), ALU.add).then_inc(o_kept.sem, 1)
            dve.wait_ge(o_kept.sem, o_kept.at(i, 3))
            for t in range(TPB):
                last = V.bn_stats(stO[:, t, :], o[:, t, :])
            last.then_inc(st_o.sem, 1)
            dve.wait_ge(st_o.sem, st_o.at(i))
            dve.sem_inc(s_alone, 1)
            for t in range(TPB):
                last = V.bn_aggr(mvO[:, t, :], stO[:, t, :])
            last.then_inc(mv_o.sem, 1)
            dve.wait_ge(mv_o.sem, mv_o.at(i))
            V.tensor_scalar(veO, mvO[:, :, 1], EPS, None, ALU.add).then_inc(ve_o.sem, 1)

        def onorm_dve(dve, i):
            dve.wait_ge(rs_o.sem, rs_o.at(i))
            for t in range(TPB):
                last = V.tensor_scalar(o[:, t, :], o[:, t, :], mvO[:, t, 0:1], rsO[:, t:t + 1],
                                       ALU.subtract, ALU.mult)
            last.then_inc(on_o.sem, 1)

        def y_dve(dve, i, j):
            dve.wait_ge(nsum.sem, nsum.at(i))
            for f in range(DT3):
                V.scalar_tensor_tensor(out=xm[j][:, f, :], in0=xm[j][:, f, :], scalar=dskip[:, f:f + 1],
                                       in1=ps[:, f, :], op0=ALU.mult, op1=ALU.add).then_inc(ysk.sem, 1)
            dve.wait_ge(ysk.sem, ysk.at(i))
            V.tensor_tensor(zs[j], xm[j], zs[j], ALU.mult).then_inc(yz.sem, 1)

        def dbx_dve(dve, i, j, n):
            if n == 0:
                dve.wait_ge(u_kept.sem, u_kept.at(i))
            dve.wait_ge(b_copied.sem, b_copied.at(i, n + 1))
            free_state(dve, i, n)
            V.tensor_tensor(hs[SLOT[n]][:, 0, :], up_[j][:, 0, :], ps[:, 3, :], ALU.mult).then_inc(dbx.sem, 1)

        def body_dve(dve, i, j, front=True, back=True):
            dbx_dve(dve, i, j, 0)
            if back:
                y_dve(dve, i - 1, 1 - j)
            for n in range(NS):
                buf = hs[SLOT[n]]
                if n + 1 < NS:
                    dbx_dve(dve, i, j, n + 1)
                dve.wait_ge(dbx.sem, dbx.at(i, n + 1))
                dve.wait_ge(dbx_gp.sem, dbx_gp.at(i, n + 1))
                dve.wait_ge(da_ready.sem, da_ready.at(i, (n + 1) * DT3))
                V.tensor_tensor_scan(out=flat(buf), data0=dA[n % 2].rearrange("p f s t -> p (f s t)"),
                                     data1=flat(buf), initial=0.0, op0=ALU.mult, op1=ALU.add)\
                    .then_inc(scan.sem, 1)
                dve.wait_ge(scan.sem, scan.at(i, n + 1))
                dve.wait_ge(c_ready.sem, c_ready.at(i, n + 1))
                V.tensor_tensor(buf, buf, ps[:, 4, :].unsqueeze(1).broadcast_to([P, DT3, BT]), ALU.mult)\
                    .then_inc(hc.sem, 1)
                if back and n == 0:
                    xr_dve(dve, i - 1, 1 - j)
                if front:
                    if n == AT["norm"]:
                        norm_c(dve, i + 1, 1 - j)
                    if n == AT["norm"] + 2:
                        xn_dve(dve, i + 1, 1 - j)
                    if AT["in_proj"] < n <= AT["in_proj"] + DT3:
                        conv_dve(dve, i + 1, 1 - j, n - AT["in_proj"] - 1)
                if back:
                    if n == AT["silu"]:
                        fuse_dve(dve, i - 1, 1 - j)
                    if n == AT["out"]:
                        out_dve(dve, i - 1, last=not front)
                    if n == AT["out_norm"]:
                        onorm_dve(dve, i - 1)
                if front:
                    if n == AT["x_proj"]:
                        split_dve(dve, i + 1, 1 - j)
                    if n == AT["dt"] + 1:
                        softplus_max_dve(dve, i + 1, 1 - j, 0)
                        softplus_max_dve(dve, i + 1, 1 - j, 1)
                    if n == AT["dt"] + 2:
                        softplus_max_dve(dve, i + 1, 1 - j, 2)
                    if n == AT["dt"] + 3:
                        softplus_dve(dve, i + 1, 1 - j)

        def meta_dve(dve, b, q, r, first=False):
            dve.wait_ge(xt_loaded[r].sem, xt_loaded[r].at(q))
            if not first:
                dve.wait_ge(added.sem, added.at(b - RING))
            V.tensor_copy(gate_s[r], xt[r][:, D:D + 1]).then_inc(meta.sem, 1)
            V.tensor_copy(tok_s[r], xt[r][:, D + 1:D + 2]).then_inc(meta.sem, 1)

        def expert_dve(dve, b, q, r, first=False, last=False):
            j = r % 2
            dve.wait_ge(e_hT.sem, e_hT.at(b))
            dve.wait_ge(e_down.sem, e_down.at(b - 2))
            V.tensor_copy(hTs[j].rearrange("p (a b) t -> p a (b t)", b=3), ps[:, 4:6, 0:3 * P])\
                .then_inc(e_hTk.sem, 1)
            if not last:
                meta_dve(dve, b + 2, q + (r + 2) // RING, (r + 2) % RING, first)
            dve.wait_ge(e_down.sem, e_down.at(b))
            dve.wait_ge(meta.sem, meta.at(b))
            V.tensor_scalar(ys[r], ps[:, 6, 0:D], gate_s[r], None, ALU.mult).then_inc(e_y.sem, 1)

        def tables_dve(dve):
            n = [0]

            def step(ins):
                n[0] += 1
                ins.then_inc(s_tab, 1)
                dve.wait_ge(s_tab, n[0])

            r1 = run[0:1, :]
            first = caps[0:1, :]
            dve.wait_ge(gsteps.sem, gsteps.at(NB - 1))
            dve.wait_ge(xn_d.sem, xn_d.at(NB - 1))
            step(V.tensor_copy(pad_of, r1))
            step(V.tensor_tensor(cnt, r1, first, ALU.subtract))
            step(V.tensor_scalar(cnt, cnt, float(P - 1), None, ALU.add))
            step(V.tensor_copy(cnti, cnt))
            step(V.tensor_scalar(cnti, cnti, 7, None, ALU.arith_shift_right))
            step(V.tensor_copy(nblk, cnti))
            step(V.tensor_tensor_scan(out=lastb, data0=nblk, data1=nblk, initial=0.0, op0=ALU.add, op1=ALU.bypass))
            step(V.tensor_tensor(firstb, lastb, nblk, ALU.subtract))
            step(V.scalar_tensor_tensor(out=rowv, in0=firstb, scalar=-float(P), in1=first, op0=ALU.mult, op1=ALU.add))
            bb = blockno.unsqueeze(2).broadcast_to([1, NSB, EXP])
            over = lambda v: v.unsqueeze(1).broadcast_to([1, NSB, EXP])
            step(V.tensor_tensor(ge_end, bb, over(lastb), ALU.is_ge))
            step(V.tensor_tensor(ge_first, bb, over(firstb), ALU.is_ge))
            step(V.tensor_reduce(eno, ge_end, AX.X, ALU.add))
            step(V.tensor_scalar(eno, eno, float(EXP - 1), None, ALU.min))
            step(V.tensor_copy(expert_of, eno))
            step(V.tensor_tensor(ge_first, ge_first, ge_end, ALU.subtract))
            step(V.tensor_tensor(ge_first, ge_first, over(rowv), ALU.mult))
            step(V.tensor_reduce(sno, ge_first, AX.X, ALU.add))
            past = ge_end[:, :, EXP - 1]
            step(V.tensor_scalar(eno, past, -1.0, 1.0, ALU.mult, ALU.add))
            step(V.tensor_tensor(eno, eno, blockno, ALU.mult))
            step(V.scalar_tensor_tensor(out=sno, in0=eno, scalar=float(P), in1=sno, op0=ALU.mult, op1=ALU.add))
            step(V.scalar_tensor_tensor(out=sno, in0=past, scalar=float(EXP * CAP), in1=sno, op0=ALU.mult, op1=ALU.add))
            step(V.tensor_copy(slot_of, sno))
            dve.sem_inc(s_tables, 1)

        def stats_d(dve, i, p):
            for t in range(TPB):
                last = V.bn_stats(stD[:, t, :], H[:, bass.ds(i * TPB + t, 1), :].rearrange("p t f -> p (t f)"))
            last.then_inc(st_d.sem, 1)
            dve.wait_ge(st_d.sem, st_d.at(i))
            dve.sem_inc(s_alone, 1)
            for t in range(TPB):
                last = V.bn_aggr(mvD[p][:, t, :], stD[:, t, :])
            last.then_inc(mv_d.sem, 1)
            dve.wait_ge(mv_d.sem, mv_d.at(i))
            dve.wait_ge(rs_d.sem, rs_d.at(i - 1))
            V.tensor_scalar(pvD[:, 0, :], mvD[p][:, :, 1], EPS, None, ALU.add)
            V.tensor_scalar(pvD[:, 1, :], mvD[p][:, :, 1], 1.0 + EPS, EPS * EPS, ALU.mult, ALU.add)\
                .then_inc(pv_d.sem, 1)

        def xn_d_dve(dve, i, p, j, q=None):
            dve.wait_ge(rs_d.sem, rs_d.at(i))
            if q is not None:
                dve.wait_ge(sent[j].sem, sent[j].at(q - 1))
            for t in range(TPB):
                last = V.tensor_scalar(send[j][:, t, 0, 0:D], H[:, bass.ds(i * TPB + t, 1), :].rearrange("p t f -> p (t f)"),
                                       mvD[p][:, t, 0:1], rsD[p][:, 1, t:t + 1], ALU.subtract, ALU.mult)
            last.then_inc(xn_d.sem, 1)
            dve.wait_ge(res_d.sem, res_d.at(i - 2))
            V.tensor_scalar(growD[p], rsD[p][:, 0, :], 1.0, None, ALU.add).then_inc(coef_d.sem, 1)
            V.scalar_tensor_tensor(out=shiftD[p], in0=mvD[p][:, :, 0], scalar=-1.0, in1=rsD[p][:, 0, :],
                                   op0=ALU.mult, op1=ALU.mult).then_inc(coef_d.sem, 1)

        def gating_dve(dve, i, j, more=2, q=None):
            n = [0]

            def step(ins):
                n[0] += 1
                ins.then_inc(gsteps.sem, 1)
                dve.wait_ge(gsteps.sem, gsteps.at(i, n[0]))

            dve.wait_ge(lg_ready.sem, lg_ready.at(i))
            step(V.tensor_copy(lg, ps[:, 2, 0:TPB * EXP].rearrange("p (t e) -> p t e", t=TPB)))
            step(V.tensor_reduce(lmax, lg, AX.X, ALU.max))
            step(V.tensor_tensor(lg, lg, lmax.unsqueeze(2).broadcast_to([P, TPB, EXP]), ALU.subtract))
            if more >= 1:
                xn_d_dve(dve, i + 1, (j + 1) % 2, (j + 1) % SENDS, q)
            dve.wait_ge(gexp.sem, gexp.at(i))
            step(V.tensor_reduce(psm, pr, AX.X, ALU.add))
            step(V.reciprocal(psm, psm))
            step(V.tensor_tensor(pr, pr, psm.unsqueeze(2).broadcast_to([P, TPB, EXP]), ALU.mult))
            pe_ = pr.unsqueeze(3).broadcast_to([P, TPB, EXP, EXP])
            pj_ = pr.unsqueeze(2).broadcast_to([P, TPB, EXP, EXP])
            step(V.tensor_tensor(cmp1, pj_, pe_, ALU.is_gt))
            step(V.tensor_tensor(cmp2, pj_, pe_, ALU.is_equal))
            step(V.tensor_tensor(cmp2, cmp2, tri.unsqueeze(1).broadcast_to([P, TPB, EXP, EXP]), ALU.mult))
            step(V.tensor_tensor(cmp1, cmp1, cmp2, ALU.add))
            step(V.tensor_reduce(rank, cmp1, AX.X, ALU.add))
            for k in range(TOPK):
                step(V.tensor_scalar(pick_k[:, k, :, :], rank, float(k), None, ALU.is_equal))
            step(V.tensor_tensor(sel, pick_k[:, 0, :, :], pick_k[:, 1, :, :], ALU.add))
            assert n[0] == SEL_STEP
            if more >= 2:
                stats_d(dve, i + 2, j % 2)
            step(V.tensor_tensor(wk, pick_k, pr.unsqueeze(1).broadcast_to([P, TOPK, TPB, EXP]), ALU.mult))
            step(V.tensor_reduce(gk, wk, AX.X, ALU.add))
            step(V.tensor_tensor(psm, gk[:, 0, :], gk[:, 1, :], ALU.add))
            step(V.reciprocal(psm, psm))
            for k in range(TOPK):
                V.tensor_tensor(send[j][:, :, k, D], gk[:, k, :], psm, ALU.mult)
                V.tensor_copy(send[j][:, :, k, D + 1], tokno)
            dve.wait_ge(pos_ready.sem, pos_ready.at(i))
            step(V.tensor_tensor(pos, ps[:, 3, 0:TPB * EXP].rearrange("p (t e) -> p t e", t=TPB),
                                 run.unsqueeze(1).broadcast_to([P, TPB, EXP]), ALU.add))
            V.tensor_scalar(tokno, tokno, float(BT), None, ALU.add)
            V.tensor_tensor(run, run, ps[:, 3, TPB * EXP:(TPB + 1) * EXP], ALU.add)
            step(V.tensor_tensor(wk, pick_k, pos.unsqueeze(1).broadcast_to([P, TOPK, TPB, EXP]), ALU.mult))
            step(V.tensor_reduce(sk, wk, AX.X, ALU.add))
            step(V.tensor_copy(slots_i[j], sk))
            assert n[0] == NG

        @block.vector
        def _(dve):
            V.memset(ones[:, :], 1.0).then_inc(s_setup, 1)
            for j in (0, 1):
                V.memset(nrm[j][:, :, D:D + 1], 1.0)
            V.memset(ps[:, 4:6, 0:D], 0.0).then_inc(s_zero, 1)
            dve.wait_ge(s_const, 16 * 7)
            with dve.Fori(0, NB // 2) as ii:
                for j in (0, 1):
                    i = 2 * ii + j
                    dve.wait_ge(tok_loaded[j].sem, tok_loaded[j].at(ii))
                    for t in range(TPB):
                        last = V.bn_stats(stA[:, t, :], tok[j][:, t, :])
                    last.then_inc(stats_a.sem, 1)
                    dve.wait_ge(stats_a.sem, stats_a.at(i))
                    dve.sem_inc(s_alone, 1)
                    for t in range(TPB):
                        last = V.bn_aggr(mvA[:, t, :], stA[:, t, :])
                    last.then_inc(mv_a.sem, 1)
                    dve.wait_ge(mv_a.sem, mv_a.at(i))
                    dve.wait_ge(rstd_a.sem, rstd_a.at(i - 1))
                    V.tensor_scalar(veA, mvA[:, :, 1], EPS, None, ALU.add).then_inc(var_a.sem, 1)
                    dve.wait_ge(rstd_a.sem, rstd_a.at(i))
                    dve.wait_ge(outer_a.sem, outer_a.at(i - 2))
                    dve.wait_ge(nrmT_a.sem, nrmT_a.at(i - 2))
                    for t in range(TPB):
                        last = V.tensor_scalar(nrm[j][:, t, 0:D], tok[j][:, t, :], mvA[:, t, 0:1],
                                               rsA[j][:, t:t + 1], ALU.subtract, ALU.mult)
                    last.then_inc(nrm_a.sem, 1)
            setup_dve(dve)
            dve.wait_ge(s_b1, 1)
            V.tensor_copy(b1b, ps[:, 6, 0:D]).then_inc(s_b1b, 1)
            h0_dve(dve, 0)
            att_dve(dve, 0, 0)
            body_b_dve(dve, 0, 0, before=False)
            with dve.Fori(0, NB // 2 - 1) as ii:
                for j in (1, 0):
                    body_b_dve(dve, 2 * ii + (1 if j else 2), j)
            for i in (NB - 2, NB - 1):
                mlp_dve(dve, i, i % 2)
            dve.wait_ge(s_wc2, 16 * 4)
            dve.wait_ge(s_wc, 16 * 14)
            for buf in dA:
                V.memset(buf[:, :, :, 0:1], 0.0)
            V.memset(xnT[:, :, :, 0:TAPS // 2], 0.0)
            V.memset(xnT[:, :, :, TAPS // 2 + SEQ - 1:PADX], 0.0)
            V.memset(xi[:, :, :, 0:CTAPS - 1], 0.0)
            V.tensor_tensor(wconv[:, TAPS // 2, :], wconv[:, TAPS // 2, :], wgcn[:, 0, :], ALU.add)
            r = TAPS + TAPS // 2 // 2
            V.tensor_tensor(wconv[LOW:P, r, :], wconv[LOW:P, r, :], wgcn[LOW:P, 1, :], ALU.add)
            V.tensor_tensor(xgb, gcb, cvb, ALU.add)
            V.tensor_tensor(gateb, ggb, gmb, ALU.add)
            V.tensor_copy(pick, pick32[:, :])
            dve.wait_ge(s_cact, 1)
            V.tensor_scalar(nega[:, :, :], nega[:, :, :], -1.0, None, ALU.mult).then_inc(s_cset, 1)
            front_dve(dve, 0, 0)
            body_dve(dve, 0, 0, back=False)
            with dve.Fori(0, NB // 2 - 1) as ii:
                for j in (1, 0):
                    body_dve(dve, 2 * ii + (1 if j else 2), j)
            body_dve(dve, NB - 1, 1, front=False)
            y_dve(dve, NB - 1, 1)
            xr_dve(dve, NB - 1, 1)
            fuse_dve(dve, NB - 1, 1)
            out_dve(dve, NB - 1, last=True)
            onorm_dve(dve, NB - 1)
            dve.wait_ge(tail_o.sem, tail_o.at(NB - 1))
            V.memset(sel5[:, TPB:TPB + 1, :], 0.0)
            stats_d(dve, 0, 0)
            stats_d(dve, 1, 1)
            xn_d_dve(dve, 0, 0, 0)
            dve.wait_ge(s_wd, 16 * 9)
            for j in range(SENDS):
                gating_dve(dve, j, j, q=1 if j + 1 == SENDS else None)
            with dve.Fori(1, NB // SENDS - 1) as q:
                for j in range(SENDS):
                    gating_dve(dve, SENDS * q + j, j, q=q + (j + 1) // SENDS)
            for j in range(SENDS):
                gating_dve(dve, NB - SENDS + j, j, more=min(2, SENDS - 1 - j), q=NB // SENDS - 1)
            tables_dve(dve)
            for j in (0, 1):
                meta_dve(dve, j, 0, j, first=True)
            for j in range(RING):
                expert_dve(dve, j, 0, j, first=j + 2 < RING)
            with dve.Fori(1, NSB // RING - 1) as q:
                for j in range(RING):
                    expert_dve(dve, RING * q + j, q, j)
            for j in range(RING):
                expert_dve(dve, NSB - RING + j, NSB // RING - 1, j, last=j + 2 >= RING)


def kernel(**inputs):
    import numpy as np
    import concourse.bacc as bacc
    from concourse.bass_utils import run_bass_kernel_spmd

    a = {k: np.asarray(v) for k, v in inputs.items()}

    def halves(w, tail):
        return w.reshape(KT, KP, *tail).swapaxes(0, 1)

    def tiles(w, n, tail):
        return w.reshape(n, P, *tail).swapaxes(0, 1)

    col = lambda v: v.reshape(KT, KP).T
    ch = lambda v: v.reshape(DT3, P).T
    freqs = 10000.0 ** (-np.arange(0, D, 2, dtype=np.float32) / np.float32(D))
    ang = np.arange(SEQ, dtype=np.float32)[:, None] * freqs[None].astype(np.float32)
    rope = np.concatenate([np.sin(ang), np.cos(ang)], axis=-1).astype(np.float32)
    widths, ratios = (96, 144, 192), (2, 3, 4)
    mask_in = np.array([[float(x < w) for x in range(D)] for w in widths for _ in ratios], np.float32)
    mask_out = np.array([[float(x < w * r) for x in range(FF)] for w in widths for r in ratios], np.float32)
    heads = lambda w: w.reshape(HEADS, DTR, -1).swapaxes(0, 1)
    xp = a["L1_attn_m_xproj_w"]
    bcw = xp[:, RANK:]
    conv, gcn_w = a["L1_attn_conv_w"].transpose(1, 2, 0), a["L1_attn_gcn_w"]
    ae, ar = a["L0_ffn_alpha_e"], a["L0_ffn_alpha_r"]
    arrays = {
        "ids": a["x"].reshape(NT, P).T,
        "wte": a["L0_tok_wte"],
        "ident": np.eye(P, dtype=np.float32),
        "mhalf": np.full((P, 8), -0.5, np.float32),
        "va_fm": np.concatenate([col(a[k]) for k in ("L0_tok_ln_w", "L0_tok_ln_b", "L1_ffn_ln_gamma",
                                                     "L1_ffn_ln_beta")], axis=1),
        "b_fc": a["L0_ffn_b_fc"].reshape(FT, P).T,
        "alphas": np.stack([np.broadcast_to(ae[:, None], (3, 3)).reshape(9),
                            np.broadcast_to(ar[None], (3, 3)).reshape(9)], axis=1),
        "ln_b_row": a["L0_tok_ln_b"].reshape(1, D),
        "b_proj_row": a["L0_ffn_b_proj"].reshape(1, D),
        "WpT": halves(a["L0_tok_W_proj"].T, (HD,)),
        "WvT": halves(a["L0_tok_W_val"].T, (HD,)),
        "WpH": heads(a["L0_tok_W_proj"]),
        "WoH": heads(a["L0_tok_W_out"].T),
        "traceT": a["L0_tok_trace0"].transpose(2, 0, 1),
        "mask_in": mask_in,
        "mask_out": mask_out,
        "rope": halves(rope.T, (SEQ,)),
        "W0T": halves(a["L0_ffn_w_fc"].T, (FF,)),
        "W1T": tiles(a["L0_ffn_w_proj"].T, FT, (D,)),
        "Wv": halves(a["L0_attn_Wv"].T, (KV,)),
        "Wo": a["L0_attn_Wo"].T,
        "wconv": np.concatenate([conv[0:P], np.concatenate([conv[P:, 0::2], conv[P:, [1, 3, 5, 6]]], axis=0)], axis=1),
        "wgcn": np.stack([gcn_w[0:P], np.concatenate([gcn_w[P:], gcn_w[P:]], axis=0)], axis=1),
        "win": a["L1_attn_m_in_w"],
        "norm1": np.stack([v for k in ("w", "b") for n1 in [a["L1_attn_norm1_" + k]]
                           for v in (n1[0:P], np.concatenate([n1[P:], n1[P:]]))], axis=1),
        "wxp": tiles(np.concatenate([bcw, bcw, bcw, xp[:, :RANK]], axis=1), DT3, (3 * 32 + RANK,)),
        "wdt": a["L1_attn_m_dt_w"],
        "wmo": tiles(a["L1_attn_m_out_w"], DT3, (D,)),
        "wgg": halves(a["L1_attn_gate_gcn_w"], (D,)),
        "wgm": halves(a["L1_attn_gate_mamba_w"], (D,)),
        "wout": halves(a["L1_attn_out_w"], (D,)),
        "pick": np.tile(np.eye(32, dtype=np.float32), (3, 1)),
        "vc_fm": np.concatenate([col(a["L1_attn_" + k]) for k in (
            "gcn_b", "conv_b", "gate_gcn_b", "gate_mamba_b")], axis=1),
        "vc_ch": np.concatenate([a["L1_attn_m_conv_w"].reshape(DT3, P, CTAPS).swapaxes(0, 1).reshape(P, -1),
                                 ch(a["L1_attn_m_conv_b"]), ch(a["L1_attn_m_dt_b"]), ch(a["L1_attn_m_D"])], axis=1),
        "A_log": tiles(a["L1_attn_m_A_log"], DT3, (NS,)),
        "n2w": a["L1_attn_norm2_w"],
        "n2b": a["L1_attn_norm2_b"],
        "outb": a["L1_attn_out_b"],
        "router": halves(a["L1_ffn_router_w"], (EXP,)),
        "tri": np.broadcast_to(np.tril(np.ones((EXP, EXP), np.float32), -1), (P, EXP, EXP)),
        "w1": a["L1_ffn_w1"].reshape(EXP, KT, KP, FF).transpose(2, 0, 1, 3),
        "w2": a["L1_ffn_w2"].reshape(EXP, FT, P, D).transpose(2, 0, 1, 3),
        "below": np.triu(np.ones((P, P), np.float32), 1),
        "allones": np.ones((P, P), np.float32),
        "tokno": (np.arange(TPB) * P + np.arange(P)[:, None]).astype(np.float32),
        "first_slots": np.broadcast_to((np.arange(EXP) * CAP).astype(np.float32), (P, EXP)),
        "padrow": np.concatenate([np.zeros((P, D + 1), np.float32),
                                  (T + np.arange(P, dtype=np.float32))[:, None]], axis=1),
        "blockno": np.arange(NSB, dtype=np.float32)[None],
    }
    nc = bacc.Bacc("TRN2", target_bir_lowering=False, num_devices=1)
    arrays = {k + "_dram": np.ascontiguousarray(v) for k, v in arrays.items()}
    aps = {k[:-5]: nc.dram_tensor(k, v.shape, mybir.dt.from_np(v.dtype), kind="ExternalInput").ap()
           for k, v in arrays.items()}
    out = nc.dram_tensor("out_dram", (T + P, D), F32, kind="ExternalOutput").ap()
    build(nc, aps, out)
    r = run_bass_kernel_spmd(nc, [arrays], core_ids=[0])
    return r.results[0]["out_dram"][:T].reshape(BATCH, SEQ, D)
```
